# Optimizing a Trainium2 kernel written in Bass

```python
import numpy as np
import jax
import jax.numpy as jnp

def _softmax(x, axis=-1):
    return jax.nn.softmax(x, axis=axis)

def _gelu(x):
    return jax.nn.gelu(x, approximate=True)

def _silu(x):
    return jax.nn.silu(x)

def _sigmoid(x):
    return jax.nn.sigmoid(x)

def _layernorm(x, axis=-1, eps=1e-05):
    m = jnp.mean(x, axis=axis, keepdims=True)
    v = jnp.var(x, axis=axis, keepdims=True)
    return (x - m) / jnp.sqrt(v + eps)

def _scatter_add(tgt, idx, src, axis=0):
    return tgt.at[idx].add(src)

def _segment_sum(src, seg, n):
    return jax.ops.segment_sum(src, seg, n)
kernel_name = 'mk_recurrent_d2_jaxref_r8_dbe6ba'

def setup_inputs(seed: int=0):
    np.random.seed(seed)
    _w = jnp.asarray

    def _L0_attn_setup():
        import jax, jax.numpy as jnp
        import numpy as np
        H = 32
        KV = 8
        D = 128
        WINDOW = 128
        THETA = 10000.0

        def _rope_tables(seq_len, dtype=jnp.float32):
            inv_freq = 1.0 / THETA ** (jnp.arange(0, D, 2, dtype=jnp.float32) / D)
            t = jnp.arange(seq_len, dtype=jnp.float32)
            freqs = t[:, None] * inv_freq[None, :]
            emb = jnp.concatenate([freqs, freqs], axis=-1)
            return (jnp.cos(emb).astype(dtype), jnp.sin(emb).astype(dtype))

        def _rotate_half(x):
            x1, x2 = (x[..., :D // 2], x[..., D // 2:])
            return jnp.concatenate([-x2, x1], axis=-1)
        key = jax.random.key(seed)
        ks = jax.random.split(key, 5)
        B, S, E = (1, 256, 512)
        sc = 0.02
        return {'hidden_states': jax.random.normal(ks[0], (B, S, E), jnp.float32), 'Wq': jax.random.normal(ks[1], (H * D, E), jnp.float32) * sc, 'Wk': jax.random.normal(ks[2], (KV * D, E), jnp.float32) * sc, 'Wv': jax.random.normal(ks[3], (KV * D, E), jnp.float32) * sc, 'Wo': jax.random.normal(ks[4], (E, H * D), jnp.float32) * sc}
    _L0_attn_in = _L0_attn_setup()

    def _L0_ffn_setup():
        import jax, jax.numpy as jnp
        import numpy as np
        HID, BOT, RDIM, NSLOT, K, VB = (512, 64, 48, 128, 8, 32)
        TAU_LOW, TAU_HIGH, EARLY_EXIT = (0.5, 2.0, 0.05)

        def _uncertainty(h, Wu1, bu1, Wu2, bu2):
            var = jnp.var(h, axis=-1)
            log_var = jnp.log1p(var)
            norm_var = log_var / (jnp.mean(log_var) + 1e-06)
            learned = (jax.nn.gelu(h @ Wu1.T + bu1) @ Wu2.T + bu2)[..., 0]
            return jnp.clip(norm_var * 0.5 + jax.nn.sigmoid(learned) * 2.5, 0.0, 5.0)
        key = jax.random.key(seed)
        ks = jax.random.split(key, 12)
        B, S = (2, 256)
        return {'hidden_states': jax.random.normal(ks[0], (B, S, HID), dtype=jnp.float32), 'Wq': jax.random.normal(ks[1], (BOT, HID), dtype=jnp.float32) / np.sqrt(HID), 'Wr': jax.random.normal(ks[2], (RDIM, BOT), dtype=jnp.float32) / np.sqrt(BOT), 'aux_keys': jax.random.normal(ks[3], (NSLOT, BOT), dtype=jnp.float32) * 0.01, 'aux_values': jax.random.normal(ks[4], (NSLOT, HID), dtype=jnp.float32) * 0.02, 'Wvd': jax.random.normal(ks[5], (VB, HID), dtype=jnp.float32) * 0.1 / np.sqrt(HID), 'Wvu': jax.random.normal(ks[6], (HID, VB), dtype=jnp.float32) * 0.1 / np.sqrt(VB), 'Wu1': jax.random.normal(ks[7], (HID // 4, HID), dtype=jnp.float32) / np.sqrt(HID), 'bu1': jnp.zeros((HID // 4,), dtype=jnp.float32), 'Wu2': jax.random.normal(ks[8], (1, HID // 4), dtype=jnp.float32) * 0.01, 'bu2': jnp.zeros((1,), dtype=jnp.float32), 'gate_w1': jnp.float32(0.5), 'gate_bias': jnp.float32(-1.0), 'log_rel': jnp.zeros((NSLOT,), dtype=jnp.float32)}
    _L0_ffn_in = _L0_ffn_setup()

    def _L1_attn_setup():
        import jax, jax.numpy as jnp
        import numpy as np
        import math
        B, T, D_IN, D_OUT = (2, 256, 512, 512)
        N_HEADS, N_KV = (32, 8)
        HEAD_DIM = D_OUT // N_HEADS
        GROUP_SIZE = N_HEADS // N_KV
        ROPE_BASE = 500000.0
        CTX = 256

        def _rope_tables(head_dim, base, seq_len):
            inv_freq = 1.0 / base ** (jnp.arange(0, head_dim, 2, dtype=jnp.float32) / head_dim)
            t = jnp.arange(seq_len, dtype=jnp.float32)
            freqs = jnp.einsum('i,j->ij', t, inv_freq)
            return (jnp.cos(freqs), jnp.sin(freqs))

        def _apply_rope(x, cos, sin):
            x1, x2 = jnp.split(x, 2, axis=-1)
            c = cos[None, None]
            s = sin[None, None]
            return jnp.concatenate([x1 * c - x2 * s, x1 * s + x2 * c], axis=-1)
        key = jax.random.key(seed)
        ks = jax.random.split(key, 5)
        scale = 0.02
        return {'x': jax.random.normal(ks[0], (B, T, D_IN), dtype=jnp.float32), 'Wq': jax.random.normal(ks[1], (D_IN, D_OUT), dtype=jnp.float32) * scale, 'Wk': jax.random.normal(ks[2], (D_IN, N_KV * HEAD_DIM), dtype=jnp.float32) * scale, 'Wv': jax.random.normal(ks[3], (D_IN, N_KV * HEAD_DIM), dtype=jnp.float32) * scale, 'Wo': jax.random.normal(ks[4], (D_OUT, D_OUT), dtype=jnp.float32) * scale}
    _L1_attn_in = _L1_attn_setup()

    def _L1_ffn_setup():
        import jax, jax.numpy as jnp
        import numpy as np
        key = jax.random.key(seed)
        k = jax.random.split(key, 6)
        x = jax.random.normal(k[0], (4, 256, 512), jnp.float32)
        W = jax.random.normal(k[1], (512, 512), jnp.float32) * 0.02
        bias = jax.random.normal(k[2], (512,), jnp.float32) * 0.02
        A = jax.random.normal(k[3], (16, 16, 512), jnp.float32) * 0.02
        Bf = jax.random.normal(k[4], (16, 512, 16), jnp.float32) * 0.02
        coeffs = jax.random.uniform(k[5], (16,), jnp.float32)
        scales = jnp.full((16,), 0.5, jnp.float32)
        return {'x': x, 'W': W, 'bias': bias, 'A': A, 'Bf': Bf, 'coeffs': coeffs, 'scales': scales}
    _L1_ffn_in = _L1_ffn_setup()
    _d = {'L0_attn_hidden_states': _L0_attn_in['hidden_states'], 'L0_attn_Wq': _L0_attn_in['Wq'], 'L0_attn_Wk': _L0_attn_in['Wk'], 'L0_attn_Wv': _L0_attn_in['Wv'], 'L0_attn_Wo': _L0_attn_in['Wo'], 'L0_ffn_Wq': _L0_ffn_in['Wq'], 'L0_ffn_Wr': _L0_ffn_in['Wr'], 'L0_ffn_aux_keys': _L0_ffn_in['aux_keys'], 'L0_ffn_aux_values': _L0_ffn_in['aux_values'], 'L0_ffn_Wvd': _L0_ffn_in['Wvd'], 'L0_ffn_Wvu': _L0_ffn_in['Wvu'], 'L0_ffn_Wu1': _L0_ffn_in['Wu1'], 'L0_ffn_bu1': _L0_ffn_in['bu1'], 'L0_ffn_Wu2': _L0_ffn_in['Wu2'], 'L0_ffn_bu2': _L0_ffn_in['bu2'], 'L0_ffn_gate_w1': _L0_ffn_in['gate_w1'], 'L0_ffn_gate_bias': _L0_ffn_in['gate_bias'], 'L0_ffn_log_rel': _L0_ffn_in['log_rel'], 'L1_attn_Wq': _L1_attn_in['Wq'], 'L1_attn_Wk': _L1_attn_in['Wk'], 'L1_attn_Wv': _L1_attn_in['Wv'], 'L1_attn_Wo': _L1_attn_in['Wo'], 'L1_ffn_W': _L1_ffn_in['W'], 'L1_ffn_bias': _L1_ffn_in['bias'], 'L1_ffn_A': _L1_ffn_in['A'], 'L1_ffn_Bf': _L1_ffn_in['Bf'], 'L1_ffn_coeffs': _L1_ffn_in['coeffs'], 'L1_ffn_scales': _L1_ffn_in['scales']}
    _x0 = _d['L0_attn_hidden_states']
    _d['L0_attn_hidden_states'] = jax.random.normal(jax.random.fold_in(jax.random.key(seed), 1), (2, 1024, 512), dtype=_x0.dtype)
    del _x0
    return _d

def reference(L0_attn_hidden_states, L0_attn_Wq, L0_attn_Wk, L0_attn_Wv, L0_attn_Wo, L0_ffn_Wq, L0_ffn_Wr, L0_ffn_aux_keys, L0_ffn_aux_values, L0_ffn_Wvd, L0_ffn_Wvu, L0_ffn_Wu1, L0_ffn_bu1, L0_ffn_Wu2, L0_ffn_bu2, L0_ffn_gate_w1, L0_ffn_gate_bias, L0_ffn_log_rel, L1_attn_Wq, L1_attn_Wk, L1_attn_Wv, L1_attn_Wo, L1_ffn_W, L1_ffn_bias, L1_ffn_A, L1_ffn_Bf, L1_ffn_coeffs, L1_ffn_scales):

    def _L0_attn_ref(hidden_states, Wq, Wk, Wv, Wo):
        import jax, jax.numpy as jnp
        import numpy as np
        H = 32
        KV = 8
        D = 128
        WINDOW = 128
        THETA = 10000.0

        def _rope_tables(seq_len, dtype=jnp.float32):
            inv_freq = 1.0 / THETA ** (jnp.arange(0, D, 2, dtype=jnp.float32) / D)
            t = jnp.arange(seq_len, dtype=jnp.float32)
            freqs = t[:, None] * inv_freq[None, :]
            emb = jnp.concatenate([freqs, freqs], axis=-1)
            return (jnp.cos(emb).astype(dtype), jnp.sin(emb).astype(dtype))

        def _rotate_half(x):
            x1, x2 = (x[..., :D // 2], x[..., D // 2:])
            return jnp.concatenate([-x2, x1], axis=-1)
        B, S, E = hidden_states.shape
        q = (hidden_states @ Wq.T).reshape(B, S, H, D).transpose(0, 2, 1, 3)
        k = (hidden_states @ Wk.T).reshape(B, S, KV, D).transpose(0, 2, 1, 3)
        v = (hidden_states @ Wv.T).reshape(B, S, KV, D).transpose(0, 2, 1, 3)
        cos, sin = _rope_tables(S, hidden_states.dtype)
        cos = cos[None, None]
        sin = sin[None, None]
        q = q * cos + _rotate_half(q) * sin
        k = k * cos + _rotate_half(k) * sin
        k = jnp.repeat(k, H // KV, axis=1)
        v = jnp.repeat(v, H // KV, axis=1)
        scores = jnp.einsum('bhqd,bhkd->bhqk', q, k) / jnp.sqrt(jnp.asarray(D, q.dtype))
        i = jnp.arange(S)[:, None]
        j = jnp.arange(S)[None, :]
        band = jnp.abs(i - j) < WINDOW
        scores = jnp.where(band[None, None], -jnp.inf, scores)
        attn = jax.nn.softmax(scores, axis=-1)
        out = jnp.einsum('bhqk,bhkd->bhqd', attn, v)
        out = out.transpose(0, 2, 1, 3).reshape(B, S, H * D)
        return out @ Wo.T

    def _L0_ffn_ref(hidden_states, Wq, Wr, aux_keys, aux_values, Wvd, Wvu, Wu1, bu1, Wu2, bu2, gate_w1, gate_bias, log_rel):
        import jax, jax.numpy as jnp
        import numpy as np
        HID, BOT, RDIM, NSLOT, K, VB = (512, 64, 48, 128, 8, 32)
        TAU_LOW, TAU_HIGH, EARLY_EXIT = (0.5, 2.0, 0.05)

        def _uncertainty(h, Wu1, bu1, Wu2, bu2):
            var = jnp.var(h, axis=-1)
            log_var = jnp.log1p(var)
            norm_var = log_var / (jnp.mean(log_var) + 1e-06)
            learned = (jax.nn.gelu(h @ Wu1.T + bu1) @ Wu2.T + bu2)[..., 0]
            return jnp.clip(norm_var * 0.5 + jax.nn.sigmoid(learned) * 2.5, 0.0, 5.0)
        query = hidden_states @ Wq.T
        rq = query @ Wr.T
        rk = aux_keys @ Wr.T
        router_scores = jnp.einsum('bsr,nr->bsn', rq, rk) / np.sqrt(RDIM) + log_rel
        top_scores, top_idx = jax.lax.top_k(router_scores, K)
        sel_keys = aux_keys[top_idx]
        attn = jnp.einsum('bsd,bskd->bsk', query, sel_keys) / np.sqrt(BOT) + log_rel[top_idx]
        w = jax.nn.softmax(attn, axis=-1)
        sel_vals = aux_values[top_idx]
        aux_out = jnp.einsum('bsk,bskh->bsh', w, sel_vals)
        aux_out = aux_out @ Wvd.T @ Wvu.T
        u = _uncertainty(hidden_states, Wu1, bu1, Wu2, bu2)
        u_norm = jnp.clip((u - TAU_LOW) / (TAU_HIGH - TAU_LOW), 0.0, 1.0)
        gate = jax.nn.sigmoid(gate_w1 * u_norm + gate_bias)
        gate = jnp.where(gate < EARLY_EXIT, 0.0, gate)
        return hidden_states + gate[..., None] * aux_out

    def _L1_attn_ref(x, Wq, Wk, Wv, Wo):
        import jax, jax.numpy as jnp
        import numpy as np
        import math
        B, T, D_IN, D_OUT = (2, 256, 512, 512)
        N_HEADS, N_KV = (32, 8)
        HEAD_DIM = D_OUT // N_HEADS
        GROUP_SIZE = N_HEADS // N_KV
        ROPE_BASE = 500000.0
        CTX = 256

        def _rope_tables(head_dim, base, seq_len):
            inv_freq = 1.0 / base ** (jnp.arange(0, head_dim, 2, dtype=jnp.float32) / head_dim)
            t = jnp.arange(seq_len, dtype=jnp.float32)
            freqs = jnp.einsum('i,j->ij', t, inv_freq)
            return (jnp.cos(freqs), jnp.sin(freqs))

        def _apply_rope(x, cos, sin):
            x1, x2 = jnp.split(x, 2, axis=-1)
            c = cos[None, None]
            s = sin[None, None]
            return jnp.concatenate([x1 * c - x2 * s, x1 * s + x2 * c], axis=-1)
        b, t, _ = x.shape
        cos, sin = _rope_tables(HEAD_DIM, ROPE_BASE, t)
        q = (x @ Wq).reshape(b, t, N_HEADS, HEAD_DIM).transpose(0, 2, 1, 3)
        k = (x @ Wk).reshape(b, t, N_KV, HEAD_DIM).transpose(0, 2, 1, 3)
        v = (x @ Wv).reshape(b, t, N_KV, HEAD_DIM).transpose(0, 2, 1, 3)
        q = _apply_rope(q, cos, sin)
        k = _apply_rope(k, cos, sin)
        k_h = jnp.repeat(k, GROUP_SIZE, axis=1)
        v_h = jnp.repeat(v, GROUP_SIZE, axis=1)
        scores = jnp.einsum('bhqd,bhkd->bhqk', q, k_h) / math.sqrt(HEAD_DIM)
        causal = jnp.triu(jnp.ones((t, t), dtype=bool), k=1)
        scores = jnp.where(causal[None, None], jnp.finfo(scores.dtype).min, scores)
        attn = jax.nn.softmax(scores, axis=-1)
        ctx = jnp.einsum('bhqk,bhkd->bhqd', attn, v_h)
        ctx = ctx.transpose(0, 2, 1, 3).reshape(b, t, D_OUT)
        return ctx @ Wo

    def _L1_ffn_ref(x, W, bias, A, Bf, coeffs, scales):
        import jax, jax.numpy as jnp
        import numpy as np
        out = jnp.einsum('bsd,od->bso', x, W) + bias
        xa = jnp.einsum('bsd,erd->ebsr', x, A)
        w = coeffs * scales
        upd = jnp.einsum('ebsr,eor,e->bso', xa, Bf, w)
        return out + upd
    x = L0_attn_hidden_states
    xn = _layernorm(x, axis=-1)
    s = _L0_attn_ref(xn, L0_attn_Wq, L0_attn_Wk, L0_attn_Wv, L0_attn_Wo)
    g = _silu(_L0_ffn_ref(xn, L0_ffn_Wq, L0_ffn_Wr, L0_ffn_aux_keys, L0_ffn_aux_values, L0_ffn_Wvd, L0_ffn_Wvu, L0_ffn_Wu1, L0_ffn_bu1, L0_ffn_Wu2, L0_ffn_bu2, L0_ffn_gate_w1, L0_ffn_gate_bias, L0_ffn_log_rel))
    x = x + s * g
    xn = _layernorm(x, axis=-1)
    s = _L1_attn_ref(xn, L1_attn_Wq, L1_attn_Wk, L1_attn_Wv, L1_attn_Wo)
    g = _silu(_L1_ffn_ref(xn, L1_ffn_W, L1_ffn_bias, L1_ffn_A, L1_ffn_Bf, L1_ffn_coeffs, L1_ffn_scales))
    x = x + s * g
    return x

_drawn_inputs = setup_inputs


def setup_inputs(seed=0):
    import zlib

    import numpy as np

    out = dict(_drawn_inputs(seed))
    spreads = {'L0_ffn_bu1': (0.0, 2.0), 'L0_ffn_log_rel': (0.0, 0.8), 'L1_ffn_scales': (0.5, 0.6)}
    factors = {'L0_attn_Wq': 8.0,
     'L0_attn_Wk': 8.0,
     'L0_attn_Wv': 4.629,
     'L0_attn_Wo': 4.531,
     'L0_ffn_Wq': 8.0,
     'L0_ffn_Wr': 8.0,
     'L0_ffn_aux_keys': 8.0,
     'L0_ffn_aux_values': 8.0,
     'L0_ffn_Wvd': 8.0,
     'L0_ffn_Wvu': 8.0,
     'L0_ffn_Wu1': 36.963,
     'L0_ffn_Wu2': 35.879,
     'L1_attn_Wq': 8.0,
     'L1_attn_Wk': 8.0,
     'L1_attn_Wv': 7.1,
     'L1_attn_Wo': 7.547,
     'L1_ffn_W': 8.0,
     'L1_ffn_bias': 64.0,
     'L1_ffn_A': 8.0,
     'L1_ffn_Bf': 8.0,
     'L1_ffn_coeffs': 8.0}
    for name, (base, spread) in spreads.items():
        noise = np.random.default_rng([zlib.crc32(name.encode()), seed]).standard_normal(out[name].shape)
        drawn = base * np.exp(spread * noise) if base else spread * noise
        out[name] = jnp.asarray(drawn.astype(out[name].dtype))
    for name, factor in factors.items():
        out[name] = (out[name] * factor).astype(out[name].dtype)
    return out
```

```python
from contextlib import ExitStack

import numpy as np
import concourse.bass as bass
from concourse import mybir

F = mybir.dt.float32
R = mybir.dt.float32r
BF = mybir.dt.bfloat16
ALU = mybir.AluOpType
ACT = mybir.ActivationFunctionType
AX = mybir.AxisListType

P = 128
B, S, E = 2, 1024, 512
NT = S // P
EC = E // P
H0, KV0, D0 = 32, 8, 128
GQ = H0 // KV0
KV1, D1 = 8, 16
NSLOT, BOT, RDIM, VB, TOPK = 128, 64, 48, 32, 8
LN_EPS = 1e-5
NEG = -1e30
KEYS = S - P
TG = GQ * NT
CG = TG // 4
GELU_C, GELU_A = 0.7978845608028654, 0.044715
W1N = E + 2 * KV1 * D1
QK1 = W1N - KV1 * D1
ST1 = 4 * D1 + 2
ONE = 1
V1W = 32


def build(nc, a, out):
    ctx = ExitStack()
    with ctx:
        def sbuf(stack, name, shape, dt=F):
            return stack.enter_context(nc.sbuf_tensor(name, shape, dt))

        def sem(name):
            return ctx.enter_context(nc.semaphore(name))

        ident = sbuf(ctx, "ident", [P, P])
        ident_r = sbuf(ctx, "ident_r", [P, P], R)
        ident_b = sbuf(ctx, "ident_b", [P, P], BF)
        mask_ge = sbuf(ctx, "mask_ge", [P, P], BF)
        mask_le = sbuf(ctx, "mask_le", [P, P], BF)
        bu1_b = sbuf(ctx, "bu1_b", [P, P])
        wu2_b = sbuf(ctx, "wu2_b", [P, P])
        scal_b = sbuf(ctx, "scal_b", [P, 4])
        row64 = sbuf(ctx, "row64", [P, 1])
        minus_half = sbuf(ctx, "minus_half", [P, NT])
        router = sbuf(ctx, "router", [P, 2 * P])
        auxvu = sbuf(ctx, "auxvu", [P, E])
        mv0 = sbuf(ctx, "mv0", [P, B * NT, 2])
        rstd0 = sbuf(ctx, "rstd0", [P, B * NT])
        half_norm = sbuf(ctx, "half_norm", [P, B * NT])
        cs1 = sbuf(ctx, "cs1", [P, NT, 2 * D1])
        xT_hi = sbuf(ctx, "xT_hi", [P, EC, S], R)
        xT_lo = sbuf(ctx, "xT_lo", [P, EC, S], R)
        acc = sbuf(ctx, "acc", [P, NT, E])
        psum = ctx.enter_context(nc.psum_tensor("psum", [P, 8, 512], F))
        g0_dram = nc.dram_tensor("g0_scratch", [B * S, E], F, kind="Internal").ap()
        weff_dram = nc.dram_tensor("weff_scratch", [P, EC * E], F, kind="Internal").ap()

        pre = ExitStack()
        with pre:
            pr_keysT = sbuf(pre, "pr_keysT", [P, P])
            pr_wr = sbuf(pre, "pr_wr", [P, P])
            pr_wrT = sbuf(pre, "pr_wrT", [P, P])
            pr_rkT = sbuf(pre, "pr_rkT", [P, P])
            pr_avT = sbuf(pre, "pr_avT", [P, EC, P])
            pr_wvdT = sbuf(pre, "pr_wvdT", [P, EC, P])
            pr_wvuT = sbuf(pre, "pr_wvuT", [P, E])
            pr_avd = sbuf(pre, "pr_avd", [P, P])
            pr_a = sbuf(pre, "pr_a", [P, 2, E])
            pr_b = sbuf(pre, "pr_b", [P, 2, E])
            pr_w = sbuf(pre, "pr_w", [P, EC, E])
            pr_cs = sbuf(pre, "pr_cs", [P, 2, 2])
            pr_mix = sbuf(pre, "pr_mix", [P, 2])
            pr_x = sbuf(pre, "pr_x", [P, B * NT, E])
            pr_st = sbuf(pre, "pr_st", [P, B * NT, 6])
            pr_sm = sbuf(pre, "pr_sm", [P, 8 * B * NT])
            pr_mh = sbuf(pre, "pr_mh", [P, B * NT])
            pr_ones = sbuf(pre, "pr_ones", [P, P])

        pha = ExitStack()
        with pha:
            wa_f = sbuf(pha, "wa_f", [P, EC, 2 * P])
            wa_hi = sbuf(pha, "wa_hi", [P, EC, 2 * P], R)
            wa_lo = sbuf(pha, "wa_lo", [P, EC, 2 * P], R)
            xn = sbuf(pha, "xn", [P, NT, E])
            queryT = sbuf(pha, "queryT", [P, S])
            zb = sbuf(pha, "zb", [P, NT, P])
            zt = sbuf(pha, "zt", [P, NT, P])
            sc = sbuf(pha, "sc", [P, NT, P])
            rep = sbuf(pha, "rep", [P, NT, P])
            eT = sbuf(pha, "eT", [P, NT, P])
            ex_a = sbuf(pha, "ex_a", [P, NT, E])
            top8 = sbuf(pha, "top8", [P, NT, TOPK])
            sma = sbuf(pha, "sma", [P, 12, NT])

        phb = ExitStack()
        with phb:
            cosT = sbuf(phb, "cosT", [P, S])
            sinT = sbuf(phb, "sinT", [P, S])
            kT_hi = sbuf(phb, "kT_hi", [P, 2, S], R)
            kT_lo = sbuf(phb, "kT_lo", [P, 2, S], R)
            v_sb = sbuf(phb, "v_sb", [P, NT, D0])
            qT_hi = sbuf(phb, "qT_hi", [P, 2, S], R)
            qT_lo = sbuf(phb, "qT_lo", [P, 2, S], R)
            probs = sbuf(phb, "probs", [P, 3, KEYS])
            pT = sbuf(phb, "pT", [P, 2, NT, 512])
            oT_hi = sbuf(phb, "oT_hi", [P, 2, S], R)
            oT_lo = sbuf(phb, "oT_lo", [P, 2, S], R)
            o_f = sbuf(phb, "o_f", [P, 512])
            raw = sbuf(phb, "raw", [P, S])
            swp = sbuf(phb, "swp", [P, S])
            q_f = sbuf(phb, "q_f", [P, S])
            k_f = sbuf(phb, "k_f", [P, S])
            w_st = sbuf(phb, "w_st", [P, 2, 512])
            wq_hi = sbuf(phb, "wq_hi", [P, 2, 512], R)
            wq_lo = sbuf(phb, "wq_lo", [P, 2, 512], R)
            wk_hi = sbuf(phb, "wk_hi", [P, 512], R)
            wk_lo = sbuf(phb, "wk_lo", [P, 512], R)
            wv_hi = sbuf(phb, "wv_hi", [P, 512], R)
            wv_lo = sbuf(phb, "wv_lo", [P, 512], R)
            wo_hi = sbuf(phb, "wo_hi", [P, 2, 512], R)
            wo_lo = sbuf(phb, "wo_lo", [P, 2, 512], R)
            stat = sbuf(phb, "stat", [P, 3, 4])

        phd = ExitStack()
        with phd:
            q1 = sbuf(phd, "q1", [P, NT, E])
            k1 = sbuf(phd, "k1", [P, NT, KV1 * D1])
            v1 = sbuf(phd, "v1", [P, NT, KV1, D1 + 1])
            g1 = sbuf(phd, "g1", [P, NT, E])
            bias_b = sbuf(phd, "bias_b", [P, E])
            phc = ExitStack()
            with phc:
                gx = sbuf(phc, "gx", [P, NT, E])
                w1_f = sbuf(phc, "w1_f", [P, EC, W1N + E])
                w1_hi = sbuf(phc, "w1_hi", [P, EC, W1N + E], R)
                w1_lo = sbuf(phc, "w1_lo", [P, EC, W1N + E], R)
                st1 = sbuf(phc, "st1", [P, NT, 6])
                mv1 = sbuf(phc, "mv1", [P, NT, 2])
                rs1 = sbuf(phc, "rs1", [P, NT])
                ra = sbuf(phc, "ra", [P, QK1])
                rb = sbuf(phc, "rb", [P, QK1])
                g_lin = sbuf(phc, "g_lin", [P, 2, E])
                g_exp = sbuf(phc, "g_exp", [P, 2, E])
            q_st = sbuf(phd, "q_st", [P, 2, NT, ST1], R)
            k_st = sbuf(phd, "k_st", [P, NT, ST1], R)
            kT1 = sbuf(phd, "kT1", [P, S], R)
            qTa = sbuf(phd, "qTa", [P, S], R)
            qTb = sbuf(phd, "qTb", [P, 2, S], R)
            nm1 = sbuf(phd, "nm1", [P, 2, NT])
            rc1 = sbuf(phd, "rc1", [P, NT])
            pT1 = sbuf(phd, "pT1", [P, 2, NT * (NT + 1) // 2, P])
            ctx1 = sbuf(phd, "ctx1", [P, NT, E])
            ctxT = sbuf(phd, "ctxT", [P, EC, S])
            wo1 = sbuf(phd, "wo1", [P, EC, E])
            y_sb = sbuf(phd, "y_sb", [P, 2, E])

        s = {n: sem(n) for n in (
            "consts", "pro_loaded", "pro_x", "pro_mm", "pro_evac", "pro_act", "pro_stats", "pro_pow", "pro_weff",
            "x_loaded", "wa_loaded", "wa_hi_done", "wa_lo_done", "xn_ready", "xT_psum", "xT_hi_done", "xT_lo_done",
            "z_psum", "gelu_in", "gelu_exp", "query_psum", "query_done", "router_psum", "sc_done", "gate_in",
            "gate_exp", "att_in", "att_exp", "att_ready", "eT_psum", "eT_done", "aux_psum", "g0_lin", "g0_exp",
            "g0_ready", "g0_stored",
            "tabs_loaded", "w_loaded0", "w_loaded1", "w_hi_done", "w_ready", "prep_psum", "raw_ready", "swapped", "roped",
            "prep_hi", "prep_done", "v_psum", "v_evac", "scores_ready", "negmax_ready", "exp_done", "recip_ready",
            "ta_full", "tb_full", "ta_evac", "tb_evac", "pv_done", "o_norm", "o_hi_done", "o_lo_done",
            "oproj_psum", "oproj_evac", "acc_zero", "pt_zero", "rope_mul",
            "gx_loaded", "x1_ready", "x1_stats", "x1_rstd", "w1_loaded", "w1_hi_done", "w1_lo_done", "qkv_psum",
            "qkv_evac", "ffn_psum", "ffn_lin", "ffn_exp", "ffn_done", "xx_loaded", "x1_mul",
            "wo1_loaded", "st_hi", "st_ready", "qt_psum", "qt_evac", "kt_evac", "qm_psum", "qm_max", "nm_ready",
            "km_psum", "km_exp", "pv1_psum", "pv1_evac", "ctxT_psum", "ctxT_evac", "y_psum", "y_ready", "y_stored0", "y_stored1",
        )}

        credited = {
            "sync": ("y_stored0", "y_stored1",),
            "vector": ("y_ready", "xT_lo_done", "tb_evac", "o_norm", "oproj_evac", "qm_max", "pv1_evac", "roped", "qkv_evac", "ffn_lin", "g0_lin",),
            "scalar": ("raw_ready", "exp_done", "ta_evac", "qt_evac", "km_exp", "ctxT_evac", "o_hi_done", "v_evac",),
            "gpsimd": ("w_ready",),
            "tensor": ("pv_done", "scores_ready", "tb_full", "oproj_psum", "qt_psum", "km_psum", "qm_psum", "pv1_psum",),
        }

        def give_credit(eng, name):
            for n in credited[name]:
                eng.sem_inc(s[n], ONE)

        def hilo(pe, dst, lhs, rhs, start=True, stop=True):
            (lh, ll), (rh, rl) = lhs, rhs
            pe.matmul(dst, ll, rh, start=start, stop=False)
            pe.matmul(dst, lh, rl, start=False, stop=False)
            return pe.matmul(dst, lh, rh, start=False, stop=stop)

        W_STEP = {1: ("q", 2), 5: ("o", 0), 7: ("o", 1), 9: ("q", 3), 11: ("k", 0), 13: ("q", 0), 15: ("v", 0),
                  22: ("q", 1), 30: ("o", 2), 31: ("o", 3)}
        W_PRE = [("k", 0), ("q", 0), ("v", 0), ("q", 1)]

        def w_items(prefetch):
            return [(t, *W_STEP[t]) for t in sorted(W_STEP)
                    if prefetch or t in (1, 5, 7, 9, 30, 31)]

        def w_index(prefetch, kind, j):
            return [x[1:] for x in w_items(prefetch)].index((kind, j)) + 1

        def prep_steps(prefetch):
            own = [(j + 1, 8 * j + 2, 8 * j + 4) for j in range(GQ - 1)]
            return own + ([(4, 24, 25), (5, 27, 28)] if prefetch else [])

        w_dst = {"q": (wq_hi, wq_lo), "k": (wk_hi, wk_lo), "v": (wv_hi, wv_lo), "o": (wo_hi, wo_lo)}

        def w_slot(kind, j):
            hi, lo = w_dst[kind]
            return (hi[:, j % 2, :], lo[:, j % 2, :]) if kind in "qo" else (hi[:], lo[:])

        def pv_parts(t):
            c = (t - 6) // 4
            return (c, (t - 6) % 4) if t >= 6 else None

        def pv_keys(c):
            own = 4 * (c % 2)
            return [(own + 4) % 8 + i for i in range(4)] + [own + i for i in range(4)]

        block = ctx.enter_context(nc.Block())

        @block.sync
        def _(sp):
            give_credit(sp, "sync")
            x_view = a["x"].rearrange("(t p) e -> p t e", p=P)
            sp.dma_start(pr_x[:], x_view).then_inc(s["pro_x"], 16)
            pro = [(pr_keysT[:], a["keysT"]), (pr_wr[:], a["wr"]), (pr_wrT[:], a["wrT"]),
                   (pr_avT[:], a["avT"]), (pr_wvdT[:], a["wvdT"]), (pr_wvuT[:], a["wvuT"]),
                   (pr_a[:], a["lora_a"]), (pr_b[:], a["lora_b"]), (pr_w[:], a["w_ffn1"]), (pr_cs[:], a["mix"]),
                   (cs1[:], a["cs1"]),
                   (bu1_b[:], a["bu1"].partition_broadcast(P)[:, 0, :]),
                   (wu2_b[:], a["wu2"].partition_broadcast(P)[:, 0, :]),
                   (scal_b[:], a["scal"].partition_broadcast(P)[:, 0, :])]
            for dst, src in pro:
                sp.dma_start(dst, src).then_inc(s["pro_loaded"], 16)
            sp.wait_ge(s["consts"], 1)
            sp.dma_start(router[BOT:BOT + 1, 0:P], a["log_rel"]).then_inc(s["pro_loaded"], 16)
            sp.dma_start(router[BOT:BOT + 1, P:2 * P], a["log_rel"]).then_inc(s["pro_loaded"], 16)
            sp.wait_ge(s["pro_evac"], 4 + EC)
            sp.dma_start(weff_dram, pr_w[:].rearrange("p c e -> p (c e)")).then_inc(s["pro_weff"], 16)
            sp.wait_ge(s["pro_weff"], 16)
            with sp.Fori(0, B) as b:
                for k in range(2):
                    sp.wait_ge(s[f"y_stored{k}"], ONE + 8 * NT * b)
                sp.wait_ge(s["pro_stats"], 1)
                xb = a["x3"][b, :, :].rearrange("(t p) e -> p t e", p=P)
                sp.dma_start(acc[:], xb).then_inc(s["x_loaded"], 16)
                sp.dma_start(wa_f[:], a["wa"]).then_inc(s["wa_loaded"], 16)
                sp.wait_ge(s["g0_ready"], b + 1)
                g0b = g0_dram.rearrange("(b t p) e -> b p t e", b=B, p=P)[b, :, :, :]
                sp.dma_start(g0b, xn[:]).then_inc(s["g0_stored"], 16)
                sp.wait_ge(s["g0_stored"], 16 * (b + 1))

                sp.dma_start(cosT[:], a["cosT"]).then_inc(s["tabs_loaded"], 16)
                sp.dma_start(sinT[:], a["sinT"]).then_inc(s["tabs_loaded"], 16)
                w_src = {"q": a["wq"], "k": a["wk"], "v": a["wv"], "o": a["wo"]}

                def load_unit(kind, j, g, slot, busy_until):
                    src = w_src[kind]
                    n = GQ * g + j if kind in "qo" else g + j
                    if busy_until is not None:
                        sp.wait_ge(s["w_ready"], ONE + busy_until)
                    sp.dma_start(w_st[:, slot, :], src[n, :, :]).then_inc(s[f"w_loaded{slot}"], 16)

                def swap(p):
                    sp.wait_ge(s["raw_ready"], ONE + 2 * (p + 1))
                    sp.dma_start(swp[0:64, :], raw[64:128, :]).then_inc(s["swapped"], 16)
                    sp.dma_start(swp[64:128, :], raw[0:64, :]).then_inc(s["swapped"], 16)

                def group(G, g, prefetch):
                    items = {t: (i, k, j) for i, (t, k, j) in enumerate(w_items(prefetch))}
                    swaps = {t2: pr for pr, _, t2 in prep_steps(prefetch)}
                    for t in range(TG):
                        if t in items:
                            i, kind, j = items[t]
                            nxt = kind in "kv" or (kind == "q" and j < 2)
                            u = 10 * G + 4 + i
                            load_unit(kind, j, g + 1 if nxt else g, i % 2, u - 1)
                        if t in swaps:
                            swap(5 * G + 1 + swaps[t])
                G0 = b * KV0
                for i, (kind, j) in enumerate(W_PRE):
                    load_unit(kind, j, 0, i % 2, 10 * G0 + max(i - 1, 0))
                swap(5 * G0)
                swap(5 * G0 + 1)
                with sp.Fori(0, KV0 - 1) as g:
                    group(G0 + g, g, True)
                group(G0 + KV0 - 1, KV0 - 1, False)

                sp.wait_ge(s["oproj_evac"], ONE + 2 * NT * KV0 * (b + 1))
                sp.dma_start(gx[:], g0b).then_inc(s["gx_loaded"], 16)
                sp.dma_start(q1[:], xb).then_inc(s["xx_loaded"], 16)
                sp.dma_start(w1_f[:, :, 0:W1N], a["w_qkv1"]).then_inc(s["w1_loaded"], 16)
                sp.dma_start(w1_f[:, :, W1N:], weff_dram.rearrange("p (c e) -> p c e", c=EC)).then_inc(s["w1_loaded"], 16)
                sp.dma_start(bias_b[:], a["bias1"].partition_broadcast(P)[:, 0, :]).then_inc(s["w1_loaded"], 16)
                sp.wait_ge(s["ffn_done"], NT * (b + 1))
                sp.dma_start(wo1[:], a["wo1"]).then_inc(s["wo1_loaded"], 16)
                for t in range(NT):
                    sp.wait_ge(s["y_ready"], ONE + NT * b + t + 1)
                    sp.dma_start(a["out3"][b, :, :].rearrange("(t p) e -> t p e", p=P)[t, :, :],
                                 y_sb[:, t % 2, :]).then_inc(s[f"y_stored{t % 2}"], 16)
            for k in range(2):
                sp.wait_ge(s[f"y_stored{k}"], ONE + 8 * NT * B)
            sp.wait_ge(s["g0_stored"], 16 * B)

        @block.gpsimd
        def _(pool):
            give_credit(pool, "gpsimd")
            pool.memset(router[:], 0.0).then_inc(s["consts"], 1)
            for m in (ident, mask_ge, mask_le, row64, ident_b):
                pool.memset(m[:], 0.0)
            pool.memset(minus_half[:], -0.5)
            pool.memset(pr_ones[:], 1.0)
            pool.drain()
            for m in (ident, ident_b):
                pool.affine_select(out=m[:], in_=m[:], compare_op=ALU.not_equal, fill=1.0, base=0,
                                   pattern=[[-1, P]], channel_multiplier=1)
            pool.affine_select(out=mask_ge[:], in_=mask_ge[:], compare_op=ALU.is_ge, fill=NEG, base=0,
                               pattern=[[1, P]], channel_multiplier=-1)
            pool.affine_select(out=mask_le[:], in_=mask_le[:], compare_op=ALU.is_ge, fill=NEG, base=0,
                               pattern=[[-1, P]], channel_multiplier=1)
            pool.affine_select(out=row64[:], in_=row64[:], compare_op=ALU.not_equal, fill=1.0, base=-BOT,
                               pattern=[[0, 1]], channel_multiplier=1)
            pool.drain()
            pool.memset(pr_mh[:], -0.5).then_inc(s["consts"], 1)
            pool.wait_ge(s["consts"], 2)
            pool.wait_ge(s["pro_stats"], 1)
            pool.tensor_tensor(rstd0[:], pr_sm[:, 0:B * NT], pr_mh[:], ALU.pow).then_inc(s["pro_pow"], 1)

            with pool.Fori(0, B) as b:
                G0 = b * KV0

                def split_lo(u, kind, j):
                    hi, lo = w_slot(kind, j)
                    slot = u[1] % 2
                    pool.wait_ge(s["w_hi_done"], u[0] + 1)
                    pool.tensor_tensor(lo, w_st[:, slot, :], hi.bitcast(F), ALU.subtract).then_inc(s["w_ready"], 1)

                for i, (kind, j) in enumerate(W_PRE):
                    split_lo((10 * G0 + i, i), kind, j)

                def group(G, prefetch):
                    for i, (t, kind, j) in enumerate(w_items(prefetch)):
                        split_lo((10 * G + 4 + i, i), kind, j)
                with pool.Fori(0, KV0 - 1) as g:
                    group(G0 + g, True)
                group(G0 + KV0 - 1, False)

                pool.wait_ge(s["x1_stats"], b + 1)
                pool.tensor_tensor(rs1[:], rs1[:], minus_half[:], ALU.pow).then_inc(s["x1_rstd"], 1)

        @block.tensor
        def _(pe):
            give_credit(pe, "tensor")
            bank = lambda i: psum[:, i, :]
            pe.wait_ge(s["consts"], 2)
            pe.wait_ge(s["pro_loaded"], 16 * 16)
            pe.matmul(bank(0)[:, 0:P], pr_wrT[:], pr_keysT[:], start=True, stop=True).then_inc(s["pro_mm"], 1)
            for c in range(EC):
                last = pe.matmul(bank(1)[:, 0:P], pr_wvdT[:, c, :], pr_avT[:, c, :], start=(c == 0), stop=(c == EC - 1))
            last.then_inc(s["pro_mm"], 1)
            pe.wait_ge(s["pro_evac"], 2)
            pe.matmul(bank(2)[:, 0:P], pr_wr[:], pr_rkT[:], start=True, stop=True).then_inc(s["pro_mm"], 1)
            pe.matmul(bank(3), pr_avd[:], pr_wvuT[:], start=True, stop=True).then_inc(s["pro_mm"], 1)
            pe.wait_ge(s["pro_act"], 1)
            for c in range(EC):
                for k in range(2):
                    last = pe.matmul(bank(4 + c), pr_a[:, k, c * P:(c + 1) * P], pr_b[:, k, :],
                                     start=(k == 0), stop=(k == 1))
                last.then_inc(s["pro_mm"], 1)
            pe.wait_ge(s["pro_act"], 3)
            pe.wait_ge(s["pro_evac"], 4)
            pe.matmul(bank(2)[:, 0:2], pr_ones[:], pr_sm[:, 6 * B * NT:6 * B * NT + 2], start=True, stop=True)\
                .then_inc(s["pro_mm"], 1)

            with pe.Fori(0, B) as b:
                G0 = b * KV0
                pe.wait_ge(s["y_ready"], ONE + NT * b)

                def transposed(t, src, base):
                    pe.wait_ge(s["xn_ready"], base + t + 1)
                    pe.wait_ge(s["xT_lo_done"], ONE + base + max(t - 1, 0))
                    for c in range(EC):
                        last = pe.matmul(bank(t % 2)[:, c * P:(c + 1) * P], src[:, t, c * P:(c + 1) * P], ident[:],
                                         start=True, stop=True, is_transpose=True)
                    last.then_inc(s["xT_psum"], 1)

                def xT(c, lo, hi):
                    return (xT_hi[:, c, lo:hi], xT_lo[:, c, lo:hi])

                pe.wait_ge(s["wa_lo_done"], b + 1)
                for t in range(NT + 1):
                    if t < NT:
                        transposed(t, xn, 2 * NT * b)
                    if t >= 1:
                        u = t - 1
                        pe.wait_ge(s["xT_lo_done"], ONE + 2 * NT * b + u + 1)
                        for c in range(EC):
                            last = hilo(pe, psum[:, 2 + u // 4, (u % 4) * P:(u % 4 + 1) * P], xT(c, u * P, (u + 1) * P),
                                        (wa_hi[:, c, 0:P], wa_lo[:, c, 0:P]), c == 0, c == EC - 1)
                        last.then_inc(s["z_psum"], 1)
                for h in range(2):
                    for c in range(EC):
                        last = hilo(pe, bank(4 + h), (wa_hi[:, c, P:2 * P], wa_lo[:, c, P:2 * P]),
                                    xT(c, 512 * h, 512 * h + 512), c == 0, c == EC - 1)
                    last.then_inc(s["query_psum"], 1)
                rbank = (0, 1, 6, 7)
                pe.wait_ge(s["query_done"], 2 * (b + 1))
                for t in range(NT):
                    last = pe.matmul(psum[:, rbank[t // 2], (t % 2) * 256:(t % 2) * 256 + 256], queryT[:, t * P:(t + 1) * P],
                                     router[:], start=True, stop=True)
                last.then_inc(s["router_psum"], 1)
                pe.wait_ge(s["att_ready"], b + 1)
                for t in range(NT):
                    last = pe.matmul(psum[:, 2 + t // 4, (t % 4) * P:(t % 4 + 1) * P], sc[:, t, :], ident[:],
                                     start=True, stop=True, is_transpose=True)
                last.then_inc(s["eT_psum"], 1)
                pe.wait_ge(s["eT_done"], b + 1)
                for t in range(NT):
                    if t >= 2:
                        pe.wait_ge(s["g0_lin"], ONE + NT * b + t - 1)
                    pe.matmul(bank(4 + t % 2), eT[:, t, :], auxvu[:], start=True, stop=True).then_inc(s["aux_psum"], 1)

                pe.wait_ge(s["g0_lin"], ONE + NT * (b + 1))
                M, O, TA, TB = 7, 6, 4, 5

                def prep_lump(p, half, w):
                    for c in range(EC):
                        last = hilo(pe, bank(M), (w[0][:, c * P:(c + 1) * P], w[1][:, c * P:(c + 1) * P]),
                                    xT(c, 512 * half, 512 * half + 512), c == 0, c == EC - 1)
                    last.then_inc(s["prep_psum"], 1)

                def group(G, prefetch):
                    wbase = 10 * G + 4
                    preps = {}
                    for pr, t1, t2 in prep_steps(prefetch):
                        preps[t1] = (pr, 0)
                        preps[t2] = (pr, 1)
                    w_of = {1: ("q", 1), 2: ("q", 2), 3: ("q", 3), 4: ("k", 0), 5: ("q", 0)}
                    m_user = [None]

                    def m_free():
                        pe.wait_ge(*m_user[0])

                    def scores(t):
                        j, qi = t // NT, t % NT
                        if qi == 0:
                            pe.wait_ge(s["prep_done"], 5 * G + 2 + j)
                        pe.wait_ge(s["exp_done"], ONE + TG * G + (t - 1 if t >= 2 else 0))
                        sl = 2 * (t % 2)
                        lhs = (qT_hi[:, j % 2, qi * P:(qi + 1) * P], qT_lo[:, j % 2, qi * P:(qi + 1) * P])
                        kh, kl = kT_hi[:].rearrange("p a n -> p (a n)"), kT_lo[:].rearrange("p a n -> p (a n)")
                        k0 = (qi + 1) * P
                        for bi, (lo, n) in enumerate(((0, 512), (512, KEYS - 512))):
                            dst = psum[:, sl + bi, 0:n]
                            rhs = (kh[:, k0 + lo:k0 + lo + n], kl[:, k0 + lo:k0 + lo + n])
                            masked = (qi < NT - 1) if bi == 0 else (qi > 0)
                            last = hilo(pe, dst, lhs, rhs, True, not masked)
                            if masked:
                                m, at = (mask_ge, 0) if bi == 0 else (mask_le, n - P)
                                last = pe.matmul(psum[:, sl + bi, at:at + P], ident_b[:], m[:], start=False, stop=True)
                        last.then_inc(s["scores_ready"], 1)

                    def transposes(t):
                        qi = t % NT
                        sl = t % 3
                        pe.wait_ge(s["recip_ready"], TG * G + t + 1)
                        pe.wait_ge(s["ta_evac"], ONE + TG * G + t)
                        pe.wait_ge(s["tb_evac"], ONE + TG * G + t)
                        for kb in range(NT):
                            if kb == qi:
                                src = stat[:, 2, t % 4:t % 4 + 1].broadcast_to([P, P])
                            else:
                                c = (kb - qi - 1) % NT
                                src = probs[:, sl, c * P:(c + 1) * P]
                            last = pe.matmul(psum[:, TA + kb // 4, (kb % 4) * P:(kb % 4 + 1) * P], src, ident[:],
                                             start=True, stop=True, is_transpose=True)
                            if kb == 3:
                                last.then_inc(s["ta_full"], 1)
                        last.then_inc(s["tb_full"], 1)

                    def pv(c, part):
                        own = 4 * (c % 2)
                        if part == 0:
                            pe.wait_ge(s["ta_evac"], ONE + TG * G + 4 * c + 4)
                            pe.wait_ge(s["tb_evac"], ONE + TG * G + 4 * c + 4)
                            pe.wait_ge(s["o_norm"], ONE + CG * G + c)
                            if c == 0:
                                pe.wait_ge(s["v_evac"], ONE + 2 * (G + 1))
                                pe.wait_ge(s["oproj_evac"], ONE + 2 * NT * G)
                        for i in (2 * part, 2 * part + 1):
                            kb = pv_keys(c)[i]
                            d = kb - own
                            cols = [(0, 512)] if not 0 <= d < 4 else \
                                [x for x in ((0, d * P), ((d + 1) * P, 512)) if x[1] > x[0]]
                            for n, (lo, hi) in enumerate(cols):
                                last = pe.matmul(psum[:, O, lo:hi], v_sb[:, kb, :], pT[:, c % 2, kb, lo:hi],
                                                 start=(i == 0), stop=(i == NT - 1 and n == len(cols) - 1))
                        if part == 3:
                            last.then_inc(s["pv_done"], 1)

                    def oproj(pair, tt, dst):
                        first = 4 * pair + (3 if tt < 4 else 4)
                        if tt % 4 == 0:
                            pe.wait_ge(s["o_lo_done"], CG * G + first)
                            if tt == 0:
                                for i in (0, 1):
                                    pe.wait_ge(s["w_ready"], ONE + wbase + w_index(prefetch, "o", 2 * pair + i))
                        for i in range(2):
                            lhs = (oT_hi[:, i, tt * P:(tt + 1) * P], oT_lo[:, i, tt * P:(tt + 1) * P])
                            last = hilo(pe, bank(dst), lhs, (wo_hi[:, i, :], wo_lo[:, i, :]), i == 0, i == 1)
                        last.then_inc(s["oproj_psum"], 1)

                    for t in range(TG):
                        scores(t)
                        if t == 1:
                            for half in range(2):
                                if half == 0:
                                    pe.wait_ge(s["pv_done"], ONE + CG * G)
                                    pe.wait_ge(s["oproj_evac"], ONE + 2 * NT * G)
                                    pe.wait_ge(s["raw_ready"], ONE + 10 * G + 4)
                                    pe.wait_ge(s["w_ready"], ONE + 10 * G + 3)
                                else:
                                    pe.wait_ge(s["v_evac"], ONE + 2 * G + 1)
                                for u in range(4):
                                    tt = 4 * half + u
                                    for c in range(EC):
                                        last = hilo(pe, psum[:, M, u * P:(u + 1) * P], xT(c, tt * P, (tt + 1) * P),
                                                    (wv_hi[:, c * P:(c + 1) * P], wv_lo[:, c * P:(c + 1) * P]),
                                                    c == 0, c == EC - 1)
                                last.then_inc(s["v_psum"], 1)
                            m_user[0] = (s["v_evac"], ONE + 2 * G + 2)
                        if pv_parts(t) is not None:
                            pv(*pv_parts(t))
                        if 22 <= t < 22 + NT:
                            m_free()
                            oproj(0, t - 22, M)
                            m_user[0] = (s["oproj_evac"], ONE + 2 * NT * G + t - 22 + 1)
                        if t in preps:
                            pr, half = preps[t]
                            m_free()
                            if half == 0:
                                kind, j = w_of[pr]
                                need = 10 * G + 4 if pr == 1 else wbase + w_index(prefetch, kind, j)
                                pe.wait_ge(s["w_ready"], ONE + need)
                            kind, j = w_of[pr]
                            prep_lump(None, half, w_slot(kind, j))
                            m_user[0] = (s["raw_ready"], ONE + 10 * G + 2 * (pr + 1) + half + 1)
                        if t >= 2:
                            transposes(t - 2)
                    pv(6, 2)
                    pv(6, 3)
                    transposes(TG - 2)
                    transposes(TG - 1)
                    for part in range(4):
                        pv(7, part)
                    for tt in range(NT):
                        if tt == 0:
                            m_free()
                        elif tt == 1:
                            pe.wait_ge(s["o_norm"], ONE + CG * G + CG)
                        else:
                            pe.wait_ge(s["oproj_evac"], ONE + 2 * NT * G + NT + tt - 1)
                        oproj(1, tt, M if tt % 2 == 0 else O)

                for i, p in enumerate(("k", "q")):
                    pe.wait_ge(s["w_ready"], ONE + 10 * G0 + i + 1)
                    for half in range(2):
                        pe.wait_ge(s["raw_ready"], ONE + 10 * G0 + 2 * i + half)
                        prep_lump(None, half, w_slot(p, 0))
                with pe.Fori(0, KV0 - 1) as g:
                    group(G0 + g, True)
                group(G0 + KV0 - 1, False)

                pe.wait_ge(s["oproj_evac"], ONE + 2 * NT * KV0 * (b + 1))
                for t in range(NT + 1):
                    if t < NT:
                        transposed(t, gx, 2 * NT * b + NT)
                    if t >= 1:
                        u = t - 1
                        if u == 0:
                            pe.wait_ge(s["w1_lo_done"], b + 1)
                        pe.wait_ge(s["xT_lo_done"], ONE + 2 * NT * b + NT + u + 1)
                        if u >= 2:
                            pe.wait_ge(s["qkv_evac"], ONE + NT * b + u - 1)
                            pe.wait_ge(s["ffn_lin"], ONE + NT * b + u - 1)
                        for lo, n in ((0, 512), (512, W1N - 512)):
                            for c in range(EC):
                                last = hilo(pe, psum[:, 2 + 2 * (u % 2) + lo // 512, 0:n], xT(c, u * P, (u + 1) * P),
                                            (w1_hi[:, c, lo:lo + n], w1_lo[:, c, lo:lo + n]), c == 0, c == EC - 1)
                        last.then_inc(s["qkv_psum"], 1)
                        for c in range(EC):
                            last = hilo(pe, bank(6 + u % 2), xT(c, u * P, (u + 1) * P),
                                        (w1_hi[:, c, W1N:], w1_lo[:, c, W1N:]), c == 0, c == EC - 1)
                        last.then_inc(s["ffn_psum"], 1)

                X, QM, KM, Y = 0, 2, 4, 6

                def stack_T(src, evac_count):
                    pe.wait_ge(s["qt_evac"], ONE + evac_count)
                    for t in range(NT):
                        last = pe.matmul(psum[0:ST1, X + t // 4, (t % 4) * P:(t % 4 + 1) * P].bitcast(R), src[:, t, :],
                                         ident_r[:], start=True, stop=True, is_transpose=True)
                    last.then_inc(s["qt_psum"], 1)

                with pe.Fori(0, KV1) as g:
                    G = b * KV1 + g
                    pe.wait_ge(s["qkv_evac"], ONE + NT * (b + 1))
                    pe.wait_ge(s["ffn_lin"], ONE + NT * (b + 1))
                    pe.wait_ge(s["st_ready"], 5 * G + 1)
                    stack_T(k_st, 8 * G)
                    for step in range(GQ + 2):
                        ha, hb, hc = step, step - 1, step - 2
                        if ha < GQ:
                            pe.wait_ge(s["st_ready"], 5 * G + 2 + ha)
                            if ha == 0:
                                pe.wait_ge(s["kt_evac"], G + 1)
                            stack_T(q_st[:, ha % 2], 8 * G + 2 * ha)
                            pe.wait_ge(s["qt_evac"], ONE + 8 * G + 2 * ha + 1)
                        if 0 <= hb < GQ:
                            pe.wait_ge(s["qt_evac"], ONE + 8 * G + 2 * hb + 2)
                        for i in range(NT):
                            if ha < GQ:
                                n = (i + 1) * P
                                pe.wait_ge(s["qm_max"], ONE + NT * (GQ * G + ha) + i)
                                for bi in range((n + 511) // 512):
                                    w = min(512, n - 512 * bi)
                                    diag = 512 * bi + w == n
                                    last = pe.matmul(psum[:, QM + bi, 0:w], qTa[0:ST1, i * P:(i + 1) * P],
                                                     kT1[0:ST1, 512 * bi:512 * bi + w], start=True, stop=not diag)
                                    if diag:
                                        last = pe.matmul(psum[:, QM + bi, w - P:w], ident_b[:], mask_le[:],
                                                         start=False, stop=True)
                                last.then_inc(s["qm_psum"], 1)
                            if 0 <= hb < GQ:
                                n = S - i * P
                                pe.wait_ge(s["km_exp"], ONE + NT * (GQ * G + hb) + i)
                                for bi in range((n + 511) // 512):
                                    w = min(512, n - 512 * bi)
                                    q0 = i * P + 512 * bi
                                    last = pe.matmul(psum[:, KM + bi, 0:w], kT1[0:ST1, i * P:(i + 1) * P],
                                                     qTb[0:ST1, hb % 2, q0:q0 + w], start=True, stop=bi > 0)
                                    if bi == 0:
                                        last = pe.matmul(psum[:, KM, 0:P], ident_b[:], mask_ge[:], start=False, stop=True)
                                last.then_inc(s["km_psum"], 1)
                            if 0 <= hc < GQ:
                                if i == 0:
                                    pe.wait_ge(s["km_exp"], ONE + NT * (GQ * G + hc + 1))
                                    pe.wait_ge(s["pv1_evac"], ONE + GQ * G + hc)
                                for kb in range(i + 1):
                                    off = kb * NT - kb * (kb - 1) // 2 + (i - kb)
                                    last = pe.matmul(psum[:, Y, i * V1W:i * V1W + D1 + 1], pT1[:, hc % 2, off, :],
                                                     v1[:, kb, g, :], start=(kb == 0), stop=(kb == i))
                        if 0 <= hc < GQ:
                            last.then_inc(s["pv1_psum"], 1)
                        if ha < GQ:
                            pe.wait_ge(s["nm_ready"], GQ * G + ha + 1)
                            stack_T(q_st[:, ha % 2], 8 * G + 2 * ha + 1)

                pe.wait_ge(s["wo1_loaded"], 16 * (b + 1))
                pe.wait_ge(s["pv1_evac"], ONE + GQ * KV1 * (b + 1))
                for t in range(NT + 1):
                    if t < NT:
                        pe.wait_ge(s["ctxT_evac"], ONE + NT * b + max(t - 1, 0))
                        for c in range(EC):
                            last = pe.matmul(psum[:, t % 2, c * P:(c + 1) * P], ctx1[:, t, c * P:(c + 1) * P], ident[:],
                                             start=True, stop=True, is_transpose=True)
                        last.then_inc(s["ctxT_psum"], 1)
                    if t >= 1:
                        u = t - 1
                        pe.wait_ge(s["ctxT_evac"], ONE + NT * b + u + 1)
                        pe.wait_ge(s["y_ready"], ONE + NT * b + max(u - 1, 0))
                        for c in range(EC):
                            last = pe.matmul(bank(2 + u % 2), ctxT[:, c, u * P:(u + 1) * P], wo1[:, c, :],
                                             start=(c == 0), stop=(c == EC - 1))
                        last.then_inc(s["y_psum"], 1)

        @block.scalar
        def _(act):
            give_credit(act, "scalar")
            act.wait_ge(s["consts"], 2)
            act.activation(ident_r[:], ident[:], ACT.Copy)
            act.wait_ge(s["pro_stats"], 3)
            act.activation(pr_sm[:, 7 * B * NT:7 * B * NT + 1], pr_sm[:, 0:1], ACT.Copy).then_inc(s["pro_act"], 1)
            act.activation(pr_sm[:, 7 * B * NT + 1:7 * B * NT + 2], pr_sm[:, 0:1], ACT.Copy).then_inc(s["pro_act"], 1)
            act.wait_ge(s["pro_stats"], 4)
            act.activation(half_norm[:], pr_sm[:, B * NT:2 * B * NT], ACT.Ln, bias=1.0,
                           accum_out=pr_sm[:, 6 * B * NT:6 * B * NT + 1]).then_inc(s["pro_act"], 1)

            with act.Fori(0, B) as b:
                G0 = b * KV0

                def hi_of(t, base):
                    act.wait_ge(s["xT_psum"], base + t + 1)
                    act.activation(xT_hi[:, :, t * P:(t + 1) * P], psum[:, t % 2, :].rearrange("p (c n) -> p c n", c=EC),
                                   ACT.Copy).then_inc(s["xT_hi_done"], 1)

                act.wait_ge(s["wa_loaded"], 16 * (b + 1))
                act.activation(wa_hi[:], wa_f[:], ACT.Copy).then_inc(s["wa_hi_done"], 1)
                for t in range(NT):
                    hi_of(t, 2 * NT * b)
                act.wait_ge(s["gelu_in"], b + 1)
                act.activation(zt[:], zt[:], ACT.Tanh, scale=GELU_C).then_inc(s["gelu_exp"], 1)
                act.wait_ge(s["router_psum"], b + 1)
                for i, bk in enumerate((0, 1, 6, 7)):
                    last = act.activation(sc[:, 2 * i:2 * i + 2, :],
                                          psum[:, bk, :].rearrange("p (t k n) -> p t k n", t=2, k=2)[:, :, 0, :], ACT.Copy)
                last.then_inc(s["sc_done"], 1)
                for k in range(2):
                    act.wait_ge(s["gate_in"], 2 * b + k + 1)
                    act.activation(sma[:, 1 + k, :], sma[:, 1 + k, :], ACT.Tanh, scale=0.5).then_inc(s["gate_exp"], 1)
                act.wait_ge(s["att_in"], b + 1)
                act.activation(sc[:], rep[:], ACT.Exp).then_inc(s["att_exp"], 1)
                act.wait_ge(s["eT_psum"], b + 1)
                act.activation(eT[:].rearrange("p t n -> p (t n)"),
                               psum[:, 2:4, :].rearrange("p a n -> p (a n)"), ACT.Copy).then_inc(s["eT_done"], 1)
                for t in range(NT):
                    act.wait_ge(s["g0_lin"], ONE + NT * b + t + 1)
                    act.activation(ex_a[:, t, :], xn[:, t, :], ACT.Tanh, scale=0.5).then_inc(s["g0_exp"], 1)

                M, O, TA, TB = 7, 6, 4, 5
                act.wait_ge(s["g0_stored"], 16 * (b + 1))

                def w_hi(idx, i, kind, j):
                    act.wait_ge(s[f"w_loaded{i % 2}"], 16 * (idx + 1))
                    act.activation(w_slot(kind, j)[0], w_st[:, i % 2, :], ACT.Copy).then_inc(s["w_hi_done"], 1)

                def raw_copy(p, half):
                    act.wait_ge(s["prep_psum"], 2 * p + half + 1)
                    if half == 0:
                        act.wait_ge(s["roped"], ONE + p)
                    act.activation(raw[:, 512 * half:512 * half + 512], psum[:, M, :], ACT.Copy)\
                        .then_inc(s["raw_ready"], 1)

                def q_hi(p, j, free):
                    act.wait_ge(s["roped"], ONE + p + 1)
                    act.wait_ge(s["scores_ready"], ONE + free)
                    act.activation(qT_hi[:, j % 2, :], q_f[:], ACT.Copy).then_inc(s["prep_hi"], 1)

                def k_hi(G):
                    act.wait_ge(s["roped"], ONE + 5 * G + 1)
                    act.wait_ge(s["scores_ready"], ONE + TG * G)
                    for half in range(2):
                        last = act.activation(kT_hi[:, half, :], k_f[:], ACT.Copy)
                    last.then_inc(s["prep_hi"], 1)

                def group(G, prefetch):
                    w_at = {t: (i, k, j) for i, (t, k, j) in enumerate(w_items(prefetch))}
                    raws, his = {}, {}
                    for pr, t1, t2 in prep_steps(prefetch):
                        raws[t1] = (pr, 0)
                        raws[t2] = (pr, 1)
                        his[t2 + 2] = pr

                    def exp(t):
                        act.wait_ge(s["negmax_ready"], TG * G + t + 1)
                        act.wait_ge(s["tb_full"], ONE + TG * G + (t - 2 if t >= 3 else 0))
                        act.activation(probs[:, t % 3, :], psum[:, 2 * (t % 2):2 * (t % 2) + 2, :]
                                       .rearrange("p a n -> p (a n)")[:, 0:KEYS], ACT.Exp, bias=stat[:, 0, t % 4:t % 4 + 1],
                                       accum_out=stat[:, 1, t % 4:t % 4 + 1]).then_inc(s["exp_done"], 1)

                    def ta(t):
                        c = t // 4
                        act.wait_ge(s["ta_full"], TG * G + t + 1)
                        act.wait_ge(s["o_norm"], ONE + CG * G + (c - 1 if c >= 2 else 0))
                        act.activation(pT[:, c % 2, 0:4, (t % 4) * P:(t % 4 + 1) * P],
                                       psum[:, TA, :].rearrange("p (k n) -> p k n", k=4), ACT.Copy)\
                            .then_inc(s["ta_evac"], 1)

                    def o_hi(c):
                        j, half = c // 2, c % 2
                        act.wait_ge(s["o_norm"], ONE + CG * G + c + 1)
                        act.wait_ge(s["oproj_psum"], ONE + 2 * NT * G + (0 if j < 2 else 4 + 4 * half))
                        act.activation(oT_hi[:, j % 2, 512 * half:512 * half + 512], o_f[:], ACT.Copy)\
                            .then_inc(s["o_hi_done"], 1)

                    for t in range(TG):
                        exp(t)
                        if t == 1:
                            for half in range(2):
                                act.wait_ge(s["v_psum"], 2 * G + half + 1)
                                act.activation(v_sb[:, 4 * half:4 * half + 4, :],
                                               psum[:, M, :].rearrange("p (k n) -> p k n", k=4), ACT.Copy)\
                                    .then_inc(s["v_evac"], 1)
                        if pv_parts(t) is not None and pv_parts(t)[1] == 3:
                            o_hi(pv_parts(t)[0])
                        if t in raws:
                            pr, half = raws[t]
                            raw_copy(5 * G + 1 + pr, half)
                        if t in his and his[t] != 4:
                            pr = his[t]
                            if pr < 4:
                                q_hi(5 * G + 1 + pr, pr, TG * G + NT * (pr - 1))
                            else:
                                q_hi(5 * G + 6, 0, TG * G + 3 * NT)
                        if t in w_at:
                            i, kind, j = w_at[t]
                            if kind == "o" and j == 0:
                                act.wait_ge(s["oproj_psum"], ONE + 2 * NT * G)
                            if kind == "o" and j == 2:
                                act.wait_ge(s["oproj_psum"], ONE + 2 * NT * G + NT)
                            if kind == "q":
                                act.wait_ge(s["prep_psum"], 10 * G + {2: 4, 3: 6, 0: 8, 1: 10}[j])
                            if kind == "v":
                                act.wait_ge(s["v_psum"], 2 * G + 2)
                            w_hi(5 * G + 2 + i // 2, i, kind, j)
                        if t >= 2:
                            ta(t - 2)
                    o_hi(6)
                    ta(TG - 2)
                    ta(TG - 1)
                    if prefetch:
                        k_hi(G + 1)
                    o_hi(7)

                for i, (kind, j) in enumerate(W_PRE):
                    w_hi(5 * G0 + i // 2, i, kind, j)
                act.wait_ge(s["tabs_loaded"], 32 * (b + 1))
                for p in range(2):
                    for half in range(2):
                        raw_copy(5 * G0 + p, half)
                k_hi(G0)
                q_hi(5 * G0 + 1, 0, TG * G0)
                with act.Fori(0, KV0 - 1) as g:
                    group(G0 + g, True)
                group(G0 + KV0 - 1, False)

                act.wait_ge(s["w1_loaded"], 48 * (b + 1))
                act.activation(w1_hi[:], w1_f[:], ACT.Copy).then_inc(s["w1_hi_done"], 1)
                for t in range(NT + 1):
                    if t < NT:
                        hi_of(t, 2 * NT * b + NT)
                    if t >= 1:
                        u = t - 1
                        act.wait_ge(s["ffn_lin"], ONE + NT * b + u + 1)
                        act.activation(g_exp[:, u % 2, :], g_lin[:, u % 2, :], ACT.Tanh, scale=0.5).then_inc(s["ffn_exp"], 1)

                X, QM, KM, Y = 0, 2, 4, 6
                act.wait_ge(s["qkv_evac"], ONE + NT * (b + 1))
                act.wait_ge(s["ffn_done"], NT * (b + 1))
                with act.Fori(0, KV1) as g:
                    G = b * KV1 + g

                    def stack_evac(dst, n, sm):
                        act.wait_ge(s["qt_psum"], ONE + n)
                        act.activation(dst, psum[0:ST1, X:X + 2, :].rearrange("p a n -> p (a n)"), ACT.Copy).then_inc(sm, 1)

                    def stack_hi(dst, src, order):
                        for o in order:
                            last = act.activation(dst[:, :, o * D1:(o + 1) * D1], src, ACT.Copy)
                        last.then_inc(s["st_hi"], 1)

                    k_src = k1[:].rearrange("p t (g d) -> p t g d", d=D1)
                    q_src = q1[:].rearrange("p t (h d) -> p t h d", d=D1)

                    def q_hi1(j):
                        act.wait_ge(s["qt_psum"], ONE + 9 * G + (1 + 2 * (j - 1) if j >= 2 else 0))
                        stack_hi(q_st[:, j % 2], q_src[:, :, GQ * g + j, :], (0, 2))

                    act.wait_ge(s["qt_psum"], ONE + 9 * G)
                    stack_hi(k_st, k_src[:, :, g, :], (0, 1))
                    q_hi1(0)
                    act.wait_ge(s["km_psum"], ONE + NT * GQ * G)
                    stack_evac(kT1[0:ST1, :], 9 * G + 1, s["kt_evac"])
                    for step in range(GQ + 1):
                        ha, hb = step, step - 1
                        if ha < GQ:
                            act.wait_ge(s["qm_psum"], ONE + NT * (GQ * G + ha))
                            stack_evac(qTa[0:ST1, :], 9 * G + 2 + 2 * ha, s["qt_evac"])
                            if ha + 1 < GQ:
                                q_hi1(ha + 1)
                        if 0 <= hb < GQ:
                            act.wait_ge(s["pv1_psum"], ONE + GQ * G + max(hb - 1, 0))
                            for i in range(NT):
                                n = NT - i
                                off = i * NT - i * (i - 1) // 2
                                act.wait_ge(s["km_psum"], ONE + NT * (GQ * G + hb) + i + 1)
                                act.activation(pT1[:, hb % 2, off:off + n, :].rearrange("p k n -> p (k n)"),
                                               psum[:, KM:KM + 2, :].rearrange("p a n -> p (a n)")[:, 0:n * P],
                                               ACT.Exp).then_inc(s["km_exp"], 1)
                        if ha < GQ:
                            if ha >= 2:
                                act.wait_ge(s["km_psum"], ONE + NT * (GQ * G + ha - 1))
                            stack_evac(qTb[0:ST1, ha % 2, :], 9 * G + 3 + 2 * ha, s["qt_evac"])
                for t in range(NT):
                    act.wait_ge(s["ctxT_psum"], NT * b + t + 1)
                    act.activation(ctxT[:, :, t * P:(t + 1) * P], psum[:, t % 2, :].rearrange("p (c n) -> p c n", c=EC),
                                   ACT.Copy).then_inc(s["ctxT_evac"], 1)

        @block.vector
        def _(dve):
            give_credit(dve, "vector")
            N2 = B * NT

            def sm(i, n=N2):
                return pr_sm[:, i * N2:i * N2 + n]

            dve.wait_ge(s["pro_x"], 16)
            for t in range(N2):
                dve.bn_stats(pr_st[:, t, :], pr_x[:, t, :])
            dve.drain()
            for t in range(N2):
                dve.bn_aggr(mv0[:, t, :], pr_st[:, t, :])
            dve.drain()
            dve.tensor_scalar(sm(0), mv0[:, :, 1], LN_EPS, None, ALU.add).then_inc(s["pro_stats"], 1)
            dve.memset(sm(6, 2), 0.0)
            dve.wait_ge(s["pro_loaded"], 16 * 16)
            dve.tensor_tensor(pr_mix[:], pr_cs[:, :, 0], pr_cs[:, :, 1], ALU.mult)
            dve.drain()
            for k in range(2):
                last = dve.tensor_scalar(pr_b[:, k, :], pr_b[:, k, :], pr_mix[:, k:k + 1], None, ALU.mult)
                last.then_inc(s["pro_stats"], 1)
            dve.wait_ge(s["pro_pow"], 1)
            dve.tensor_tensor(sm(2), rstd0[:], rstd0[:], ALU.mult)
            dve.drain()
            dve.tensor_tensor(sm(1), sm(2), mv0[:, :, 1], ALU.mult).then_inc(s["pro_stats"], 1)
            dve.wait_ge(s["pro_mm"], 1)
            dve.tensor_copy(pr_rkT[:], psum[:, 0, 0:P]).then_inc(s["pro_evac"], 1)
            dve.wait_ge(s["pro_mm"], 2)
            dve.tensor_copy(pr_avd[:], psum[:, 1, 0:P]).then_inc(s["pro_evac"], 1)
            dve.wait_ge(s["pro_mm"], 3)
            dve.tensor_scalar(router[0:BOT, 0:P], psum[0:BOT, 2, 0:P], float(RDIM) ** -0.5, None, ALU.mult)
            dve.tensor_scalar(router[0:BOT, P:2 * P], pr_keysT[0:BOT, :], float(BOT) ** -0.5, None, ALU.mult)\
                .then_inc(s["pro_evac"], 1)
            dve.wait_ge(s["pro_mm"], 4)
            dve.tensor_copy(auxvu[:], psum[:, 3, :]).then_inc(s["pro_evac"], 1)
            for c in range(EC):
                dve.wait_ge(s["pro_mm"], 5 + c)
                dve.tensor_tensor(pr_w[:, c, :], psum[:, 4 + c, :], pr_w[:, c, :], ALU.add).then_inc(s["pro_evac"], 1)
            dve.wait_ge(s["pro_mm"], 5 + EC)
            dve.tensor_scalar(sm(3, 1), psum[:, 2, 0:1], 1.0 / (B * S), 1e-6, ALU.mult, ALU.add)
            dve.drain()
            dve.reciprocal(sm(4, 1), sm(3, 1))
            dve.drain()
            dve.tensor_scalar(half_norm[:], half_norm[:], sm(4, 1), 0.5, ALU.mult, ALU.mult)
            dve.drain()

            with dve.Fori(0, B) as b:
                G0 = b * KV0

                def lo_of(t, base):
                    dve.wait_ge(s["xT_hi_done"], base + t + 1)
                    dve.tensor_tensor(xT_lo[:, :, t * P:(t + 1) * P], psum[:, t % 2, :].rearrange("p (c n) -> p c n", c=EC),
                                      xT_hi[:, :, t * P:(t + 1) * P].bitcast(F), ALU.subtract).then_inc(s["xT_lo_done"], 1)

                dve.wait_ge(s["x_loaded"], 16 * (b + 1))
                dve.wait_ge(s["wa_hi_done"], b + 1)
                dve.tensor_tensor(wa_lo[:], wa_f[:], wa_hi[:].bitcast(F), ALU.subtract).then_inc(s["wa_lo_done"], 1)
                mean, rstd, hn = sma[:, 8, :], sma[:, 9, :], sma[:, 10, :]
                dve.tensor_copy(mean, mv0[:, :, 0].rearrange("p (b t) -> p b t", b=B)[:, b, :])
                dve.tensor_copy(rstd, rstd0[:].rearrange("p (b t) -> p b t", b=B)[:, b, :])
                dve.tensor_copy(hn, half_norm[:].rearrange("p (b t) -> p b t", b=B)[:, b, :])
                dve.drain()
                for t in range(NT):
                    dve.tensor_scalar(xn[:, t, :], acc[:, t, :], mean[:, t:t + 1], rstd[:, t:t + 1],
                                      ALU.subtract, ALU.mult).then_inc(s["xn_ready"], 1)
                    if t >= 1:
                        lo_of(t - 1, 2 * NT * b)
                lo_of(NT - 1, 2 * NT * b)
                dve.wait_ge(s["z_psum"], NT * (b + 1))
                zps = psum[:, 2:4, :].rearrange("p a (t n) -> p (a t) n", t=4)
                bc = lambda v: v[:, :].unsqueeze(1).broadcast_to([P, NT, P])
                dve.tensor_tensor(zb[:], zps, bc(bu1_b), ALU.add)
                dve.drain()
                dve.tensor_tensor(zt[:], zb[:], zb[:], ALU.mult)
                dve.drain()
                dve.tensor_scalar(zt[:], zt[:], GELU_A, 1.0, ALU.mult, ALU.add)
                dve.drain()
                dve.tensor_tensor(zt[:], zt[:], zb[:], ALU.mult).then_inc(s["gelu_in"], 1)
                for h in range(2):
                    dve.wait_ge(s["query_psum"], 2 * b + h + 1)
                    dve.tensor_scalar(queryT[:, 512 * h:512 * h + 512], psum[:, 4 + h, :], row64[:], None, ALU.add)\
                        .then_inc(s["query_done"], 1)
                dve.wait_ge(s["gelu_exp"], b + 1)
                dve.scalar_tensor_tensor(zt[:].rearrange("p t n -> p (t n)"), zt[:].rearrange("p t n -> p (t n)"), 1.0,
                                         zb[:].rearrange("p t n -> p (t n)"), ALU.add, ALU.mult)
                dve.drain()
                dve.tensor_tensor(zt[:], zt[:], bc(wu2_b), ALU.mult)
                dve.drain()
                sig, u, gate, ssum, coef, mx = sma[:, 1, :], sma[:, 2, :], sma[:, 3, :], sma[:, 4, :], sma[:, 5, :], sma[:, 6, :]
                tmp = sma[:, 7, :]
                dve.tensor_reduce(sig, zt[:], AX.X, ALU.add)
                dve.drain()
                dve.tensor_scalar(sig, sig, 0.5, scal_b[:, 0:1], ALU.mult, ALU.add).then_inc(s["gate_in"], 1)
                dve.wait_ge(s["gate_exp"], 2 * b + 1)
                dve.tensor_scalar(u, sig, 1.25, 1.25, ALU.mult, ALU.add)
                dve.drain()
                dve.tensor_tensor(u, u, hn, ALU.add)
                dve.drain()
                dve.tensor_scalar(u, u, 0.0, 5.0, ALU.max, ALU.min)
                dve.drain()
                dve.tensor_scalar(u, u, 0.5, 1.0 / 1.5, ALU.subtract, ALU.mult)
                dve.drain()
                dve.tensor_scalar(u, u, 0.0, 1.0, ALU.max, ALU.min)
                dve.drain()
                dve.tensor_scalar(u, u, scal_b[:, 1:2], scal_b[:, 2:3], ALU.mult, ALU.add).then_inc(s["gate_in"], 1)
                dve.wait_ge(s["gate_exp"], 2 * b + 2)
                dve.tensor_scalar(gate, u, 0.5, 0.5, ALU.mult, ALU.add)
                dve.drain()
                dve.tensor_scalar(tmp, gate, 0.05, None, ALU.is_ge)
                dve.drain()
                dve.wait_ge(s["sc_done"], b + 1)
                dve.tensor_tensor(gate, gate, tmp, ALU.mult)
                for t in range(NT):
                    dve.max(top8[:, t, :], sc[:, t, :])
                dve.drain()
                for t in range(NT):
                    dve.match_replace(rep[:, t, :], top8[:, t, :], sc[:, t, :], -3.0e38)
                dve.drain()
                dve.tensor_tensor(rep[:], rep[:], sc[:], ALU.not_equal)
                dve.drain()
                dve.tensor_scalar(rep[:], rep[:], -NEG, NEG, ALU.mult, ALU.add)
                dve.drain()
                for i, bk in enumerate((0, 1, 6, 7)):
                    dve.tensor_tensor(rep[:, 2 * i:2 * i + 2, :],
                                      psum[:, bk, :].rearrange("p (t k n) -> p t k n", t=2, k=2)[:, :, 1, :],
                                      rep[:, 2 * i:2 * i + 2, :], ALU.add)
                dve.drain()
                dve.tensor_reduce(mx, rep[:], AX.X, ALU.max)
                dve.drain()
                dve.tensor_tensor(rep[:], rep[:], mx.unsqueeze(2).broadcast_to([P, NT, P]), ALU.subtract)\
                    .then_inc(s["att_in"], 1)
                dve.wait_ge(s["att_exp"], b + 1)
                dve.tensor_reduce(ssum, sc[:], AX.X, ALU.add).then_inc(s["att_ready"], 1)
                dve.drain()
                dve.reciprocal(coef, ssum)
                dve.drain()
                dve.tensor_tensor(coef, coef, gate, ALU.mult)
                dve.drain()
                for t in range(NT):
                    dve.wait_ge(s["aux_psum"], NT * b + t + 1)
                    dve.scalar_tensor_tensor(xn[:, t, :], psum[:, 4 + t % 2, :], coef[:, t:t + 1], xn[:, t, :],
                                             ALU.mult, ALU.add).then_inc(s["g0_lin"], 1)
                dve.wait_ge(s["g0_exp"], NT * (b + 1))
                flat = lambda v: v[:].rearrange("p t n -> p (t n)")
                dve.scalar_tensor_tensor(flat(xn), flat(ex_a), 1.0, flat(xn), ALU.add, ALU.mult)\
                    .then_inc(s["g0_ready"], 1)

                M, O, TA, TB = 7, 6, 4, 5
                dve.wait_ge(s["g0_stored"], 16 * (b + 1))
                dve.wait_ge(s["tabs_loaded"], 32 * (b + 1))
                dve.memset(acc[:], 0.0).then_inc(s["acc_zero"], 1)

                def rope(p, dst):
                    dve.wait_ge(s["raw_ready"], ONE + 2 * (p + 1))
                    dve.tensor_tensor(dst[:], raw[:], cosT[:], ALU.mult)
                    dve.wait_ge(s["swapped"], 32 * (p + 1))
                    dve.tensor_tensor(swp[:], swp[:], sinT[:], ALU.mult).then_inc(s["rope_mul"], 1)
                    dve.wait_ge(s["rope_mul"], p + 1)
                    dve.tensor_tensor(dst[:], dst[:], swp[:], ALU.add).then_inc(s["roped"], 1)

                def q_lo(p, j):
                    dve.wait_ge(s["prep_hi"], p + 1)
                    dve.tensor_tensor(qT_lo[:, j % 2, :], q_f[:], qT_hi[:, j % 2, :].bitcast(F), ALU.subtract)\
                        .then_inc(s["prep_done"], 1)

                def k_lo(n):
                    dve.wait_ge(s["prep_hi"], n + 1)
                    for half in range(2):
                        last = dve.tensor_tensor(kT_lo[:, half, :], k_f[:], kT_hi[:, half, :].bitcast(F), ALU.subtract)
                    last.then_inc(s["prep_done"], 1)

                def group(G, prefetch):
                    ropes, los = {}, {}
                    for pr, t1, t2 in prep_steps(prefetch):
                        ropes[t2 + 1] = pr
                        los[t2 + 2] = pr

                    def negmax(t):
                        dve.wait_ge(s["scores_ready"], ONE + TG * G + t + 1)
                        dve.tensor_reduce(stat[:, 0, t % 4:t % 4 + 1], psum[:, 2 * (t % 2):2 * (t % 2) + 2, :]
                                          .rearrange("p a n -> p (a n)")[:, 0:KEYS], AX.X, ALU.max, negate=True)\
                            .then_inc(s["negmax_ready"], 1)

                    def recip(t):
                        dve.wait_ge(s["exp_done"], ONE + TG * G + t + 1)
                        dve.reciprocal(stat[:, 2, t % 4:t % 4 + 1], stat[:, 1, t % 4:t % 4 + 1]).then_inc(s["recip_ready"], 1)

                    def tb(t):
                        c = t // 4
                        dve.wait_ge(s["tb_full"], ONE + TG * G + t + 1)
                        dve.wait_ge(s["pv_done"], ONE + CG * G + (c - 1 if c >= 2 else 0))
                        dve.tensor_copy(pT[:, c % 2, 4:8, (t % 4) * P:(t % 4 + 1) * P],
                                        psum[:, TB, :].rearrange("p (k n) -> p k n", k=4)).then_inc(s["tb_evac"], 1)

                    def norm(c):
                        own = 4 * (c % 2)
                        dve.wait_ge(s["pv_done"], ONE + CG * G + c + 1)
                        dve.wait_ge(s["o_hi_done"], ONE + CG * G + c)
                        recs = pT[:, c % 2, own:own + 4, :].rearrange("p k (i n) -> p (k i) n", i=4)[:, 0:16:5, :]
                        dve.tensor_tensor(o_f[:].rearrange("p (i n) -> p i n", i=4),
                                          psum[:, O, :].rearrange("p (i n) -> p i n", i=4), recs, ALU.mult)\
                            .then_inc(s["o_norm"], 1)

                    def o_lo(c):
                        j, half = c // 2, c % 2
                        dve.wait_ge(s["o_hi_done"], ONE + CG * G + c + 1)
                        sl = (slice(None), j % 2, slice(512 * half, 512 * half + 512))
                        dve.tensor_tensor(oT_lo[sl], o_f[:], oT_hi[sl].bitcast(F), ALU.subtract).then_inc(s["o_lo_done"], 1)

                    def add_out(pair, tt):
                        dve.wait_ge(s["acc_zero"], b + 1)
                        dve.wait_ge(s["oproj_psum"], ONE + 2 * NT * G + NT * pair + tt + 1)
                        bk = M if pair == 0 or tt % 2 == 0 else O
                        dve.tensor_tensor(acc[:, tt, :], psum[:, bk, :], acc[:, tt, :], ALU.add)\
                            .then_inc(s["oproj_evac"], 1)

                    for t in range(TG):
                        negmax(t)
                        if t >= 1:
                            recip(t - 1)
                        pp = pv_parts(t)
                        if pp is not None and pp[1] == 3:
                            norm(pp[0])
                            o_lo(pp[0])
                        if 22 <= t < 22 + NT:
                            add_out(0, t - 22)
                        if t >= 2:
                            tb(t - 2)
                        if t in ropes:
                            pr = ropes[t]
                            rope(5 * G + 1 + pr, k_f if pr == 4 else q_f)
                        if t in los and los[t] != 4:
                            pr = los[t]
                            dve.wait_ge(s["prep_hi"], 5 * G + 2 + pr - (1 if pr == 5 else 0))
                            j = pr if pr < 4 else 0
                            last = dve.tensor_tensor(qT_lo[:, j % 2, :], q_f[:], qT_hi[:, j % 2, :].bitcast(F), ALU.subtract)
                            last.then_inc(s["prep_done"], 1)
                    recip(TG - 1)
                    norm(6)
                    o_lo(6)
                    tb(TG - 2)
                    tb(TG - 1)
                    if prefetch:
                        k_lo(5 * G + 6)
                    norm(7)
                    o_lo(7)
                    for tt in range(NT):
                        add_out(1, tt)

                rope(5 * G0, k_f)
                k_lo(5 * G0)
                rope(5 * G0 + 1, q_f)
                q_lo(5 * G0 + 1, 0)
                with dve.Fori(0, KV0 - 1) as g:
                    group(G0 + g, True)
                group(G0 + KV0 - 1, False)

                dve.drain()
                dve.wait_ge(s["gx_loaded"], 16 * (b + 1))
                dve.scalar_tensor_tensor(flat(acc), flat(acc), 0.5, flat(gx), ALU.mult, ALU.mult)
                dve.drain()
                dve.wait_ge(s["xx_loaded"], 16 * (b + 1))
                dve.tensor_tensor(acc[:], acc[:], q1[:], ALU.add)
                dve.drain()
                for t in range(NT):
                    dve.bn_stats(st1[:, t, :], acc[:, t, :])
                dve.drain()
                for t in range(NT):
                    dve.bn_aggr(mv1[:, t, :], st1[:, t, :])
                dve.drain()
                dve.tensor_scalar(rs1[:], mv1[:, :, 1], LN_EPS, None, ALU.add).then_inc(s["x1_stats"], 1)
                dve.wait_ge(s["w1_hi_done"], b + 1)
                dve.tensor_tensor(w1_lo[:], w1_f[:], w1_hi[:].bitcast(F), ALU.subtract).then_inc(s["w1_lo_done"], 1)
                dve.memset(v1[:, :, :, D1:D1 + 1], 1.0)
                dve.wait_ge(s["x1_rstd"], b + 1)

                def qkv_out(u):
                    dve.wait_ge(s["qkv_psum"], NT * b + u + 1)
                    dve.wait_ge(s["qkv_evac"], ONE + NT * b + u)
                    both = psum[:, 2 + 2 * (u % 2):4 + 2 * (u % 2), :].rearrange("p a n -> p (a n)")
                    nh = QK1 // D1
                    qk = both[:, 0:QK1].rearrange("p (h k d) -> p h k d", k=2, d=D1 // 2)
                    tab = lambda lo, n: cs1[:, u, lo:lo + n].unsqueeze(1).broadcast_to([P, nh, n])
                    rbv = rb[:].rearrange("p (h k d) -> p h k d", k=2, d=D1 // 2)
                    dve.tensor_tensor(ra[:].rearrange("p (h d) -> p h d", d=D1),
                                      both[:, 0:QK1].rearrange("p (h d) -> p h d", d=D1), tab(0, D1), ALU.mult)
                    dve.tensor_tensor(rbv[:, :, 0, :], qk[:, :, 1, :], tab(D1, D1 // 2), ALU.mult)
                    dve.tensor_tensor(rbv[:, :, 1, :], qk[:, :, 0, :], tab(D1 + D1 // 2, D1 // 2), ALU.mult)
                    dve.tensor_copy(v1[:, u, :, 0:D1], both[:, QK1:W1N].rearrange("p (g d) -> p g d", d=D1))
                    dve.drain()
                    dve.tensor_tensor(q1[:, u, :], ra[:, 0:E], rb[:, 0:E], ALU.add)
                    dve.tensor_tensor(k1[:, u, :], ra[:, E:QK1], rb[:, E:QK1], ALU.add).then_inc(s["qkv_evac"], 1)
                    dve.wait_ge(s["ffn_psum"], NT * b + u + 1)
                    dve.tensor_tensor(g_lin[:, u % 2, :], psum[:, 6 + u % 2, :], bias_b[:], ALU.add).then_inc(s["ffn_lin"], 1)

                def silu(u):
                    dve.wait_ge(s["ffn_exp"], NT * b + u + 1)
                    dve.scalar_tensor_tensor(g1[:, u, :], g_exp[:, u % 2, :], 1.0, g_lin[:, u % 2, :],
                                             ALU.add, ALU.mult).then_inc(s["ffn_done"], 1)

                for t in range(NT + 2):
                    if t < NT:
                        dve.tensor_scalar(gx[:, t, :], acc[:, t, :], mv1[:, t, 0:1], rs1[:, t:t + 1],
                                          ALU.subtract, ALU.mult).then_inc(s["xn_ready"], 1)
                        lo_of(t, 2 * NT * b + NT)
                    if 1 <= t <= NT:
                        qkv_out(t - 1)
                    if t >= 2:
                        silu(t - 2)
                dve.drain()

                X, QM, KM, Y = 0, 2, 4, 6
                dve.memset(k_st[:, :, 4 * D1:ST1].bitcast(F), 1.0)
                with dve.Fori(0, KV1) as g:
                    G = b * KV1 + g
                    k_src = k1[:].rearrange("p t (g d) -> p t g d", d=D1)
                    q_src = q1[:].rearrange("p t (h d) -> p t h d", d=D1)

                    def stack_lo(dst, src, order, hi_at, n):
                        dve.wait_ge(s["st_hi"], n)
                        for o in order:
                            last = dve.tensor_tensor(dst[:, :, o * D1:(o + 1) * D1], src,
                                                     dst[:, :, hi_at * D1:(hi_at + 1) * D1].bitcast(F), ALU.subtract)
                        return last

                    def q_lo1(j):
                        stack_lo(q_st[:, j % 2], q_src[:, :, GQ * g + j, :], (1, 3), 0, 5 * G + 2 + j)
                        dve.memset(q_st[:, j % 2, :, 4 * D1:ST1].bitcast(F), 0.0).then_inc(s["st_ready"], 1)

                    stack_lo(k_st, k_src[:, :, g, :], (2, 3), 0, 5 * G + 1).then_inc(s["st_ready"], 1)
                    q_lo1(0)
                    for step in range(GQ + 2):
                        ha, hc = step, step - 2
                        if ha < GQ:
                            if ha + 1 < GQ:
                                q_lo1(ha + 1)
                            for i in range(NT):
                                n = (i + 1) * P
                                dve.wait_ge(s["qm_psum"], ONE + NT * (GQ * G + ha) + i + 1)
                                dve.tensor_reduce(nm1[:, ha % 2, i:i + 1],
                                                  psum[:, QM:QM + 2, :].rearrange("p a n -> p (a n)")[:, 0:n],
                                                  AX.X, ALU.max, negate=True).then_inc(s["qm_max"], 1)
                            dve.wait_ge(s["qm_max"], ONE + NT * (GQ * G + ha + 1))
                            dve.wait_ge(s["qt_evac"], ONE + 8 * G + 2 * ha + 1)
                            dve.tensor_copy(q_st[:, ha % 2, :, 4 * D1], nm1[:, ha % 2, :])
                            dve.drain()
                            dve.tensor_tensor(q_st[:, ha % 2, :, 4 * D1 + 1], nm1[:, ha % 2, :],
                                              q_st[:, ha % 2, :, 4 * D1].bitcast(F), ALU.subtract).then_inc(s["nm_ready"], 1)
                        if 0 <= hc < GQ:
                            dve.wait_ge(s["pv1_psum"], ONE + GQ * G + hc + 1)
                            ov = psum[:, Y, 0:NT * V1W].rearrange("p (t w) -> p t w", w=V1W)
                            dve.reciprocal(rc1[:], ov[:, :, D1])
                            dve.drain()
                            dve.tensor_tensor(ctx1[:].rearrange("p t (h d) -> p t h d", d=D1)[:, :, GQ * g + hc, :],
                                              ov[:, :, 0:D1], rc1[:].unsqueeze(2).broadcast_to([P, NT, D1]), ALU.mult)\
                                .then_inc(s["pv1_evac"], 1)
                for t in range(NT):
                    dve.wait_ge(s["y_psum"], NT * b + t + 1)
                    if t >= 2:
                        dve.wait_ge(s[f"y_stored{t % 2}"], ONE + 8 * NT * b + 16 * (t // 2))
                    dve.scalar_tensor_tensor(y_sb[:, t % 2, :], psum[:, 2 + t % 2, :], 0.5, g1[:, t, :],
                                             ALU.mult, ALU.mult)
                    dve.drain()
                    dve.tensor_tensor(y_sb[:, t % 2, :], y_sb[:, t % 2, :], acc[:, t, :], ALU.add).then_inc(s["y_ready"], 1)


def tables():
    t = np.arange(S, dtype=np.float32)
    inv0 = (np.float32(1.0) / np.float32(10000.0) ** (np.arange(0, D0, 2, dtype=np.float32) / np.float32(D0))).astype(np.float32)
    f0 = (t[:, None] * inv0[None, :]).astype(np.float32).astype(np.float64)
    r0 = float(D0) ** -0.25
    cosT = np.concatenate([np.cos(f0), np.cos(f0)], 1).T * r0
    sinT = np.concatenate([-np.sin(f0), np.sin(f0)], 1).T * r0
    inv1 = (np.float32(1.0) / np.float32(500000.0) ** (np.arange(0, D1, 2, dtype=np.float32) / np.float32(D1))).astype(np.float32)
    f1 = (t[:, None] * inv1[None, :]).astype(np.float32).astype(np.float64)
    r1 = float(D1) ** -0.25
    cs1 = np.concatenate([np.cos(f1), np.cos(f1), -np.sin(f1), np.sin(f1)], 1) * r1
    cs1 = cs1.reshape(NT, P, 2 * D1).transpose(1, 0, 2)
    return {k: np.ascontiguousarray(v, dtype=np.float32) for k, v in (("cosT", cosT), ("sinT", sinT), ("cs1", cs1))}


def padded(w, rows, cols):
    o = np.zeros((rows, cols), np.float32)
    o[:w.shape[0], :w.shape[1]] = w
    return o


def chunked(wT):
    return wT.reshape(EC, P, -1).transpose(1, 0, 2)


def layouts(i):
    heads = lambda w, n: w.reshape(n, D0, EC, P).transpose(0, 3, 2, 1).reshape(n, P, EC * D0)
    row = lambda v: np.asarray(v, np.float32).reshape(1, -1)
    er = lambda v: np.repeat(v, 16).reshape(2, P).T
    scal = np.zeros((1, 4), np.float32)
    scal[0, 0], scal[0, 1], scal[0, 2] = i["L0_ffn_bu2"][0], i["L0_ffn_gate_w1"], i["L0_ffn_gate_bias"]
    wa = np.zeros((E, 2 * P), np.float32)
    wa[:, 0:P] = i["L0_ffn_Wu1"].T
    wa[:, P:P + BOT] = i["L0_ffn_Wq"].T
    x = i["L0_attn_hidden_states"]
    d = {
        "x": x.reshape(B * S, E), "x3": x,
        "wq": heads(i["L0_attn_Wq"], H0), "wk": heads(i["L0_attn_Wk"], KV0), "wv": heads(i["L0_attn_Wv"], KV0),
        "wo": i["L0_attn_Wo"].T.reshape(H0, D0, E),
        "wa": chunked(wa),
        "keysT": padded(i["L0_ffn_aux_keys"].T, P, P), "wr": padded(i["L0_ffn_Wr"], P, P),
        "wrT": padded(i["L0_ffn_Wr"].T, P, P),
        "avT": chunked(i["L0_ffn_aux_values"].T), "wvdT": chunked(padded(i["L0_ffn_Wvd"].T, E, P)),
        "wvuT": padded(i["L0_ffn_Wvu"].T, P, E),
        "bu1": row(i["L0_ffn_bu1"]), "wu2": row(i["L0_ffn_Wu2"]), "scal": scal, "log_rel": row(i["L0_ffn_log_rel"]),
        "w_qkv1": chunked(np.concatenate([i["L1_attn_Wq"], i["L1_attn_Wk"], i["L1_attn_Wv"]], 1)),
        "wo1": chunked(i["L1_attn_Wo"]),
        "w_ffn1": chunked(i["L1_ffn_W"].T), "bias1": row(i["L1_ffn_bias"]),
        "lora_a": i["L1_ffn_A"].reshape(2, P, E).transpose(1, 0, 2),
        "lora_b": i["L1_ffn_Bf"].transpose(0, 2, 1).reshape(2, P, E).transpose(1, 0, 2),
        "mix": np.stack([er(i["L1_ffn_coeffs"]), er(i["L1_ffn_scales"])], 2),
    }
    return {k: np.ascontiguousarray(v) for k, v in {**d, **tables()}.items()}


def kernel(**inputs):
    import concourse.bacc as bacc
    from concourse.bass_utils import run_bass_kernel_spmd

    nc = bacc.Bacc("TRN2", target_bir_lowering=False, num_devices=1)
    arrays, aps = {}, {}
    for name, v in layouts({k: np.asarray(v) for k, v in inputs.items()}).items():
        arrays[f"in_{name}"] = v
        aps[name] = nc.dram_tensor(f"in_{name}", v.shape, mybir.dt.from_np(v.dtype), kind="ExternalInput").ap()
    out = nc.dram_tensor("out_0", [B, S, E], F, kind="ExternalOutput").ap()
    aps["out3"] = out
    build(nc, aps, out)
    r = run_bass_kernel_spmd(nc, [arrays], core_ids=[0])
    return r.results[0]["out_0"]
```

```python
from contextlib import ExitStack

import numpy as np
import concourse.bass as bass
from concourse import mybir

F = mybir.dt.float32
R = mybir.dt.float32r
BF = mybir.dt.bfloat16
ALU = mybir.AluOpType
ACT = mybir.ActivationFunctionType
AX = mybir.AxisListType

P = 128
B, S, E = 2, 1024, 512
NT = S // P
EC = E // P
H0, KV0, D0 = 32, 8, 128
GQ = H0 // KV0
KV1, D1 = 8, 16
NSLOT, BOT, RDIM, VB, TOPK = 128, 64, 48, 32, 8
LN_EPS = 1e-5
NEG = -1e30
KEYS = S - P
TG = GQ * NT
CG = TG // 4
GELU_C, GELU_A = 0.7978845608028654, 0.044715
W1N = E + 2 * KV1 * D1
QK1 = W1N - KV1 * D1
ST1 = 4 * D1 + 2
ONE = 1
VS = 48
SUM_AT = 32


def build(nc, a, out):
    ctx = ExitStack()
    with ctx:
        def sbuf(stack, name, shape, dt=F):
            return stack.enter_context(nc.sbuf_tensor(name, shape, dt))

        def sem(name):
            return ctx.enter_context(nc.semaphore(name))

        ident = sbuf(ctx, "ident", [P, P])
        ident_r = sbuf(ctx, "ident_r", [P, P], R)
        ident_b = sbuf(ctx, "ident_b", [P, P], BF)
        mask_ge = sbuf(ctx, "mask_ge", [P, P], BF)
        mask_le = sbuf(ctx, "mask_le", [P, P], BF)
        bu1_b = sbuf(ctx, "bu1_b", [P, P])
        wu2_b = sbuf(ctx, "wu2_b", [P, P])
        scal_b = sbuf(ctx, "scal_b", [P, 4])
        row64 = sbuf(ctx, "row64", [P, 1])
        minus_half = sbuf(ctx, "minus_half", [P, NT])
        ones = sbuf(ctx, "ones", [P, NT])
        router = sbuf(ctx, "router", [P, 2 * P])
        auxvu = sbuf(ctx, "auxvu", [P, E])
        mv0 = sbuf(ctx, "mv0", [P, B * NT, 2])
        rstd0 = sbuf(ctx, "rstd0", [P, B * NT])
        half_norm = sbuf(ctx, "half_norm", [P, B * NT])
        cs1 = sbuf(ctx, "cs1", [P, NT, 2 * D1])
        xT_hi = sbuf(ctx, "xT_hi", [P, EC, S], R)
        xT_lo = sbuf(ctx, "xT_lo", [P, EC, S], R)
        acc = sbuf(ctx, "acc", [P, NT, E])
        psum = ctx.enter_context(nc.psum_tensor("psum", [P, 8, 512], F))
        g0_dram = nc.dram_tensor("g0_scratch", [B * S, E], F, kind="Internal").ap()
        weff_dram = nc.dram_tensor("weff_scratch", [P, EC * E], F, kind="Internal").ap()

        pre = ExitStack()
        with pre:
            pr_keysT = sbuf(pre, "pr_keysT", [P, P])
            pr_wr = sbuf(pre, "pr_wr", [P, P])
            pr_wrT = sbuf(pre, "pr_wrT", [P, P])
            pr_rkT = sbuf(pre, "pr_rkT", [P, P])
            pr_avT = sbuf(pre, "pr_avT", [P, EC, P])
            pr_wvdT = sbuf(pre, "pr_wvdT", [P, EC, P])
            pr_wvuT = sbuf(pre, "pr_wvuT", [P, E])
            pr_avd = sbuf(pre, "pr_avd", [P, P])
            pr_a = sbuf(pre, "pr_a", [P, 2, E])
            pr_b = sbuf(pre, "pr_b", [P, 2, E])
            pr_w = sbuf(pre, "pr_w", [P, EC, E])
            pr_cs = sbuf(pre, "pr_cs", [P, 2, 2])
            pr_mix = sbuf(pre, "pr_mix", [P, 2])
            pr_x = sbuf(pre, "pr_x", [P, B * NT, E])
            pr_st = sbuf(pre, "pr_st", [P, B * NT, 6])
            pr_sm = sbuf(pre, "pr_sm", [P, 8 * B * NT])
            pr_mh = sbuf(pre, "pr_mh", [P, B * NT])
            pr_ones = sbuf(pre, "pr_ones", [P, P])

        pha = ExitStack()
        with pha:
            wa_f = sbuf(pha, "wa_f", [P, EC, 2 * P])
            wa_hi = sbuf(pha, "wa_hi", [P, EC, 2 * P], R)
            wa_lo = sbuf(pha, "wa_lo", [P, EC, 2 * P], R)
            xn = sbuf(pha, "xn", [P, NT, E])
            queryT = sbuf(pha, "queryT", [P, S])
            zb = sbuf(pha, "zb", [P, NT, P])
            zt = sbuf(pha, "zt", [P, NT, P])
            sc = sbuf(pha, "sc", [P, NT, P])
            rep = sbuf(pha, "rep", [P, NT, P])
            eT = sbuf(pha, "eT", [P, NT, P])
            ex_a = sbuf(pha, "ex_a", [P, NT, E])
            top8 = sbuf(pha, "top8", [P, NT, TOPK])
            sma = sbuf(pha, "sma", [P, 12, NT])

        phb = ExitStack()
        with phb:
            cosT = sbuf(phb, "cosT", [P, S])
            sinT = sbuf(phb, "sinT", [P, S])
            kT_hi = sbuf(phb, "kT_hi", [P, 2, S], R)
            kT_lo = sbuf(phb, "kT_lo", [P, 2, S], R)
            v_sb = sbuf(phb, "v_sb", [P, NT, D0])
            qT_hi = sbuf(phb, "qT_hi", [P, 2, S], R)
            qT_lo = sbuf(phb, "qT_lo", [P, 2, S], R)
            probs = sbuf(phb, "probs", [P, 3, KEYS])
            pT = sbuf(phb, "pT", [P, 2, NT, 512])
            oT_hi = sbuf(phb, "oT_hi", [P, 2, S], R)
            oT_lo = sbuf(phb, "oT_lo", [P, 2, S], R)
            o_f = sbuf(phb, "o_f", [P, 512])
            raw = sbuf(phb, "raw", [P, S])
            swp = sbuf(phb, "swp", [P, S])
            q_f = sbuf(phb, "q_f", [P, S])
            k_f = sbuf(phb, "k_f", [P, S])
            w_st = sbuf(phb, "w_st", [P, 2, 512])
            wq_hi = sbuf(phb, "wq_hi", [P, 2, 512], R)
            wq_lo = sbuf(phb, "wq_lo", [P, 2, 512], R)
            wk_hi = sbuf(phb, "wk_hi", [P, 512], R)
            wk_lo = sbuf(phb, "wk_lo", [P, 512], R)
            wv_hi = sbuf(phb, "wv_hi", [P, 512], R)
            wv_lo = sbuf(phb, "wv_lo", [P, 512], R)
            wo_hi = sbuf(phb, "wo_hi", [P, 2, 512], R)
            wo_lo = sbuf(phb, "wo_lo", [P, 2, 512], R)
            stat = sbuf(phb, "stat", [P, 3, 4])

        phd = ExitStack()
        with phd:
            q1 = sbuf(phd, "q1", [P, NT, E])
            k1 = sbuf(phd, "k1", [P, NT, KV1 * D1])
            v1 = sbuf(phd, "v1", [P, NT, KV1 * D1])
            g1 = sbuf(phd, "g1", [P, NT, E])
            bias_b = sbuf(phd, "bias_b", [P, E])
            phc = ExitStack()
            with phc:
                gx = sbuf(phc, "gx", [P, NT, E])
                w1_f = sbuf(phc, "w1_f", [P, EC, W1N + E])
                w1_hi = sbuf(phc, "w1_hi", [P, EC, W1N + E], R)
                w1_lo = sbuf(phc, "w1_lo", [P, EC, W1N + E], R)
                st1 = sbuf(phc, "st1", [P, NT, 6])
                mv1 = sbuf(phc, "mv1", [P, NT, 2])
                rs1 = sbuf(phc, "rs1", [P, NT])
                ra = sbuf(phc, "ra", [P, QK1])
                rb = sbuf(phc, "rb", [P, QK1])
                g_lin = sbuf(phc, "g_lin", [P, 2, E])
                g_exp = sbuf(phc, "g_exp", [P, 2, E])
            q_st = sbuf(phd, "q_st", [P, 2, NT, GQ, ST1], R)
            k_st = sbuf(phd, "k_st", [P, NT, ST1], R)
            kT1 = sbuf(phd, "kT1", [P, 2, S], R)
            qTa = sbuf(phd, "qTa", [P, 2, S], R)
            qTb = sbuf(phd, "qTb", [P, 2, S], R)
            nm1 = sbuf(phd, "nm1", [P, 2, NT])
            v_st = sbuf(phd, "v_st", [P, 2, NT, VS])
            pT1 = sbuf(phd, "pT1", [P, NT * (NT + 1) // 2 * P])
            o_st = sbuf(phd, "o_st", [VS, 2, S])
            ctxT = sbuf(phd, "ctxT", [P, EC, S])
            sumT = sbuf(phd, "sumT", [P, S])
            wo1 = sbuf(phd, "wo1", [P, EC, E])
            y_sb = sbuf(phd, "y_sb", [P, 2, E])

        s = {n: sem(n) for n in (
            "consts", "pro_loaded", "pro_x", "pro_mm", "pro_evac", "pro_act", "pro_stats", "pro_pow", "pro_weff",
            "x_loaded", "wa_loaded", "wa_hi_done", "wa_lo_done", "xn_ready", "xT_psum", "xT_hi_done", "xT_lo_done",
            "z_psum", "gelu_in", "gelu_exp", "query_psum", "query_done", "router_psum", "sc_done", "gate_in",
            "gate_exp", "att_in", "att_exp", "att_ready", "eT_psum", "eT_done", "aux_psum", "g0_lin", "g0_exp",
            "g0_ready", "g0_stored",
            "tabs_loaded", "w_loaded0", "w_loaded1", "w_hi_done", "w_ready", "prep_psum", "raw_ready", "swapped", "roped",
            "q_hi_done", "q_ready", "k_hi_done", "k_ready", "v_psum", "v_evac", "scores_ready", "negmax_ready", "exp_done", "recip_ready",
            "ta_full", "tb_full", "ta_evac", "tb_evac", "pv_done", "o_norm", "o_hi_done", "o_lo_done",
            "oproj_psum", "oproj_evac", "acc_zero", "pt_zero", "rope_mul",
            "gx_loaded", "x1_ready", "x1_stats", "x1_rstd", "w1_loaded", "w1_hi_done", "w1_lo_done", "qkv_psum",
            "qkv_evac", "ffn_psum", "ffn_lin", "ffn_exp", "ffn_done", "xx_loaded", "x1_mul",
            "wo1_loaded", "st_ready", "qt_psum", "qt_evac", "qm_psum", "qm_max", "nm_ready",
            "km_psum", "km_exp", "v1_ready", "pv1_psum", "pv1_evac", "o_moved0", "o_moved1", "ctx_ready", "y_psum", "y_ready", "y_stored0", "y_stored1",
        )}

        credited = {
            "sync": ("y_stored0", "y_stored1", "o_moved0", "o_moved1",),
            "vector": ("y_ready", "xT_lo_done", "tb_evac", "o_norm", "oproj_evac", "qm_max", "ctx_ready", "roped", "qkv_evac", "ffn_lin", "g0_lin",),
            "scalar": ("raw_ready", "exp_done", "ta_evac", "qt_evac", "km_exp", "pv1_evac", "o_hi_done", "v_evac",),
            "gpsimd": ("w_ready",),
            "tensor": ("pv_done", "scores_ready", "tb_full", "oproj_psum", "qt_psum", "km_psum", "qm_psum", "pv1_psum",),
        }

        def give_credit(eng, name):
            for n in credited[name]:
                eng.sem_inc(s[n], ONE)

        def hilo(pe, dst, lhs, rhs, start=True, stop=True):
            (lh, ll), (rh, rl) = lhs, rhs
            pe.matmul(dst, ll, rh, start=start, stop=False)
            pe.matmul(dst, lh, rl, start=False, stop=False)
            return pe.matmul(dst, lh, rh, start=False, stop=stop)

        W_STEP = {1: ("q", 2), 5: ("o", 0), 7: ("k", 0), 9: ("o", 1), 11: ("q", 3), 13: ("q", 0), 15: ("v", 0),
                  22: ("q", 1), 30: ("o", 2), 31: ("o", 3)}
        V_STEPS = (4, 5)
        W_PRE = [("k", 0), ("q", 0), ("v", 0), ("q", 1)]

        def w_items(prefetch):
            return [(t, *W_STEP[t]) for t in sorted(W_STEP)
                    if prefetch or W_STEP[t][0] == "o" or W_STEP[t][1] > 1]

        def w_index(prefetch, kind, j):
            return [x[1:] for x in w_items(prefetch)].index((kind, j)) + 1

        def preps(prefetch):
            steps = [("q", 1, 1, 3), ("q", 2, 9, 11), ("k", 0, 13, 14), ("q", 3, 17, 19), ("q", 0, TG - 1, TG)]
            return [(n + 1, *x) for n, x in enumerate(x for x in steps if prefetch or x[1] > 0)]

        w_dst = {"q": (wq_hi, wq_lo), "k": (wk_hi, wk_lo), "v": (wv_hi, wv_lo), "o": (wo_hi, wo_lo)}

        def w_slot(kind, j):
            hi, lo = w_dst[kind]
            return (hi[:, j % 2, :], lo[:, j % 2, :]) if kind in "qo" else (hi[:], lo[:])

        def pv_parts(t):
            c = (t - 6) // 4
            return (c, (t - 6) % 4) if t >= 6 else None

        def pv_keys(c):
            own = 4 * (c % 2)
            return [(own + 4) % 8 + i for i in range(4)] + [own + i for i in range(4)]

        PH, XL, XP = 2 * GQ, 8, 4 * 2 * GQ + 4
        NPAIR = KV1 // 2
        CH = NT + NT // 2

        def x_turns(j, prefetch):
            return [w for w, there in (("T1", prefetch or j + 2 < PH), ("K", j % GQ == 1 and (prefetch or j < GQ)),
                                       ("T2", prefetch or j + 1 < PH)) if there]

        def x_at(j, what, prefetch):
            return XL + 2 * (sum(len(x_turns(i, prefetch)) for i in range(j)) + x_turns(j, prefetch).index(what))

        def q_chunks():
            return [(i, k0, min(512, (i + 1) * P - k0)) for i in reversed(range(NT)) for k0 in range(0, (i + 1) * P, 512)]

        def k_chunks():
            return [(i, q0, min(512, S - q0)) for i in range(NT) for q0 in range(i * P, S, 512)]

        def pT1_cols(i, q0, w):
            at = (i * NT - i * (i - 1) // 2) * P + q0 - i * P
            return pT1[:, at:at + w]

        block = ctx.enter_context(nc.Block())

        @block.sync
        def _(sp):
            give_credit(sp, "sync")
            x_view = a["x"].rearrange("(t p) e -> p t e", p=P)
            sp.dma_start(pr_x[:], x_view).then_inc(s["pro_x"], 16)
            pro = [(pr_keysT[:], a["keysT"]), (pr_wr[:], a["wr"]), (pr_wrT[:], a["wrT"]),
                   (pr_avT[:], a["avT"]), (pr_wvdT[:], a["wvdT"]), (pr_wvuT[:], a["wvuT"]),
                   (pr_a[:], a["lora_a"]), (pr_b[:], a["lora_b"]), (pr_w[:], a["w_ffn1"]), (pr_cs[:], a["mix"]),
                   (cs1[:], a["cs1"]),
                   (bu1_b[:], a["bu1"].partition_broadcast(P)[:, 0, :]),
                   (wu2_b[:], a["wu2"].partition_broadcast(P)[:, 0, :]),
                   (scal_b[:], a["scal"].partition_broadcast(P)[:, 0, :])]
            for dst, src in pro:
                sp.dma_start(dst, src).then_inc(s["pro_loaded"], 16)
            sp.wait_ge(s["consts"], 1)
            sp.dma_start(router[BOT:BOT + 1, 0:P], a["log_rel"]).then_inc(s["pro_loaded"], 16)
            sp.dma_start(router[BOT:BOT + 1, P:2 * P], a["log_rel"]).then_inc(s["pro_loaded"], 16)
            sp.wait_ge(s["pro_evac"], 4 + EC)
            sp.dma_start(weff_dram, pr_w[:].rearrange("p c e -> p (c e)")).then_inc(s["pro_weff"], 16)
            sp.wait_ge(s["pro_weff"], 16)
            with sp.Fori(0, B) as b:
                for k in range(2):
                    sp.wait_ge(s[f"y_stored{k}"], ONE + 8 * NT * b)
                sp.wait_ge(s["pro_stats"], 1)
                xb = a["x3"][b, :, :].rearrange("(t p) e -> p t e", p=P)
                sp.dma_start(acc[:], xb).then_inc(s["x_loaded"], 16)
                sp.dma_start(wa_f[:], a["wa"]).then_inc(s["wa_loaded"], 16)
                sp.wait_ge(s["g0_ready"], b + 1)
                g0b = g0_dram.rearrange("(b t p) e -> b p t e", b=B, p=P)[b, :, :, :]
                sp.dma_start(g0b, xn[:]).then_inc(s["g0_stored"], 16)
                sp.wait_ge(s["g0_stored"], 16 * (b + 1))

                sp.dma_start(cosT[:], a["cosT"]).then_inc(s["tabs_loaded"], 16)
                sp.dma_start(sinT[:], a["sinT"]).then_inc(s["tabs_loaded"], 16)
                w_src = {"q": a["wq"], "k": a["wk"], "v": a["wv"], "o": a["wo"]}

                def load_unit(kind, j, g, slot, busy_until):
                    src = w_src[kind]
                    n = GQ * g + j if kind in "qo" else g + j
                    if busy_until is not None:
                        sp.wait_ge(s["w_ready"], ONE + busy_until)
                    sp.dma_start(w_st[:, slot, :], src[n, :, :]).then_inc(s[f"w_loaded{slot}"], 16)

                def swap(p):
                    sp.wait_ge(s["raw_ready"], ONE + 2 * (p + 1))
                    sp.dma_start(swp[0:64, :], raw[64:128, :]).then_inc(s["swapped"], 16)
                    sp.dma_start(swp[64:128, :], raw[0:64, :]).then_inc(s["swapped"], 16)

                def group(G, g, prefetch):
                    at = [0] + [t for t, _, _ in w_items(prefetch)]
                    items = {at[i]: (i, k, j) for i, (_, k, j) in enumerate(w_items(prefetch))}
                    swaps = {t2: n for n, _, _, _, t2 in preps(prefetch)}
                    for t in range(TG):
                        if t in items:
                            i, kind, j = items[t]
                            nxt = kind in "kv" or (kind == "q" and j < 2)
                            u = 10 * G + 4 + i
                            load_unit(kind, j, g + 1 if nxt else g, i % 2, u - 1)
                        if t in swaps:
                            swap(5 * G + 1 + swaps[t])
                    if TG in swaps:
                        swap(5 * G + 1 + swaps[TG])
                G0 = b * KV0
                for i, (kind, j) in enumerate(W_PRE):
                    load_unit(kind, j, 0, i % 2, 10 * G0 + max(i - 1, 0))
                swap(5 * G0)
                swap(5 * G0 + 1)
                with sp.Fori(0, KV0 - 1) as g:
                    group(G0 + g, g, True)
                group(G0 + KV0 - 1, KV0 - 1, False)

                sp.wait_ge(s["oproj_evac"], ONE + 2 * NT * KV0 * (b + 1))
                sp.dma_start(gx[:], g0b).then_inc(s["gx_loaded"], 16)
                sp.dma_start(q1[:], xb).then_inc(s["xx_loaded"], 16)
                sp.dma_start(w1_f[:, :, 0:W1N], a["w_qkv1"]).then_inc(s["w1_loaded"], 16)
                sp.dma_start(w1_f[:, :, W1N:], weff_dram.rearrange("p (c e) -> p c e", c=EC)).then_inc(s["w1_loaded"], 16)
                sp.dma_start(bias_b[:], a["bias1"].partition_broadcast(P)[:, 0, :]).then_inc(s["w1_loaded"], 16)
                sp.wait_ge(s["ffn_done"], NT * (b + 1))
                sp.dma_start(wo1[:], a["wo1"]).then_inc(s["wo1_loaded"], 16)
                with sp.Fori(0, NPAIR) as n:
                    N = NPAIR * b + n
                    for j in range(PH):
                        sp.wait_ge(s["pv1_evac"], ONE + 2 * (PH * N + j + 1))
                        rows = slice(j * D1, (j + 1) * D1)
                        sp.dma_start(ctxT[rows, n, :], o_st[0:D1, j % 2, :]).then_inc(s[f"o_moved{j % 2}"], 16)
                        if j == 0:
                            sp.wait_ge(s["ctx_ready"], ONE + 2 * N)
                        sp.dma_start(sumT[rows, :], o_st[SUM_AT:SUM_AT + D1, j % 2, :]).then_inc(s[f"o_moved{j % 2}"], 16)
                for t in range(NT):
                    sp.wait_ge(s["y_ready"], ONE + NT * b + t + 1)
                    sp.dma_start(a["out3"][b, :, :].rearrange("(t p) e -> t p e", p=P)[t, :, :],
                                 y_sb[:, t % 2, :]).then_inc(s[f"y_stored{t % 2}"], 16)
            for k in range(2):
                sp.wait_ge(s[f"y_stored{k}"], ONE + 8 * NT * B)
            sp.wait_ge(s["g0_stored"], 16 * B)

        @block.gpsimd
        def _(pool):
            give_credit(pool, "gpsimd")
            pool.memset(router[:], 0.0).then_inc(s["consts"], 1)
            for m in (ident, mask_ge, mask_le, row64, ident_b):
                pool.memset(m[:], 0.0)
            pool.memset(minus_half[:], -0.5)
            pool.memset(pr_ones[:], 1.0)
            pool.memset(ones[:], 1.0)
            pool.drain()
            for m in (ident, ident_b):
                pool.affine_select(out=m[:], in_=m[:], compare_op=ALU.not_equal, fill=1.0, base=0,
                                   pattern=[[-1, P]], channel_multiplier=1)
            pool.affine_select(out=mask_ge[:], in_=mask_ge[:], compare_op=ALU.is_ge, fill=NEG, base=0,
                               pattern=[[1, P]], channel_multiplier=-1)
            pool.affine_select(out=mask_le[:], in_=mask_le[:], compare_op=ALU.is_ge, fill=NEG, base=0,
                               pattern=[[-1, P]], channel_multiplier=1)
            pool.affine_select(out=row64[:], in_=row64[:], compare_op=ALU.not_equal, fill=1.0, base=-BOT,
                               pattern=[[0, 1]], channel_multiplier=1)
            pool.drain()
            pool.memset(pr_mh[:], -0.5).then_inc(s["consts"], 1)
            pool.wait_ge(s["consts"], 2)
            pool.wait_ge(s["pro_stats"], 1)
            pool.tensor_tensor(rstd0[:], pr_sm[:, 0:B * NT], pr_mh[:], ALU.pow).then_inc(s["pro_pow"], 1)

            with pool.Fori(0, B) as b:
                G0 = b * KV0

                def split_lo(u, kind, j):
                    hi, lo = w_slot(kind, j)
                    slot = u[1] % 2
                    pool.wait_ge(s["w_hi_done"], u[0] + 1)
                    pool.tensor_tensor(lo, w_st[:, slot, :], hi.bitcast(F), ALU.subtract).then_inc(s["w_ready"], 1)

                def rope_mul(p, dst, dst_free):
                    pool.wait_ge(s["raw_ready"], ONE + 2 * (p + 1))
                    if dst_free is not None:
                        pool.wait_ge(*dst_free)
                    pool.tensor_tensor(dst[:], raw[:], cosT[:], ALU.mult)
                    pool.wait_ge(s["swapped"], 32 * (p + 1))
                    pool.tensor_tensor(swp[:], swp[:], sinT[:], ALU.mult).then_inc(s["rope_mul"], 1)

                for i, (kind, j) in enumerate(W_PRE):
                    split_lo((10 * G0 + i, i), kind, j)
                pool.wait_ge(s["tabs_loaded"], 32 * (b + 1))
                rope_mul(5 * G0, k_f, None)
                rope_mul(5 * G0 + 1, q_f, None)

                def group(G, prefetch):
                    items = {t: (i, k, j) for i, (t, k, j) in enumerate(w_items(prefetch))}
                    ropes = {t2: (n, kind, j) for n, kind, j, _, t2 in preps(prefetch)}
                    for t in range(TG + 1):
                        if t in items:
                            i, kind, j = items[t]
                            split_lo((10 * G + 4 + i, i), kind, j)
                        if t in ropes:
                            n, kind, j = ropes[t]
                            if kind == "k":
                                rope_mul(5 * G + 1 + n, k_f, (s["k_ready"], G + 1))
                            else:
                                rope_mul(5 * G + 1 + n, q_f, (s["q_ready"], GQ * G + (j if j > 0 else GQ)))
                with pool.Fori(0, KV0 - 1) as g:
                    group(G0 + g, True)
                group(G0 + KV0 - 1, False)

                pool.wait_ge(s["x1_stats"], b + 1)
                pool.tensor_tensor(rs1[:], rs1[:], minus_half[:], ALU.pow).then_inc(s["x1_rstd"], 1)

                pool.wait_ge(s["qkv_evac"], ONE + NT * (b + 1))
                pool.wait_ge(s["ffn_done"], NT * (b + 1))

                one_b = ones[:].unsqueeze(2).broadcast_to([P, NT, D1])

                def stacks(g, par):
                    k_src = k1[:].rearrange("p t (g d) -> p t g d", d=D1)[:, :, g, :]
                    q_src = q1[:].rearrange("p t (g j d) -> p t g j d", j=GQ, d=D1)[:, :, g, :, :]
                    for o in (0, 1):
                        pool.tensor_tensor(k_st[:, :, o * D1:(o + 1) * D1], k_src, one_b, ALU.mult)
                    for o in (0, 2):
                        pool.tensor_copy(q_st[:, par, :, :, o * D1:(o + 1) * D1], q_src)
                    pool.memset(k_st[:, :, 4 * D1:ST1].bitcast(F), 1.0)
                    pool.memset(q_st[:, par, :, :, 4 * D1:ST1].bitcast(F), 0.0)
                    pool.drain()
                    for o in (2, 3):
                        last = pool.tensor_tensor(k_st[:, :, o * D1:(o + 1) * D1], k_src, k_st[:, :, 0:D1].bitcast(F),
                                                  ALU.subtract)
                    last.then_inc(s["st_ready"], 1)
                    for o in (1, 3):
                        last = pool.tensor_tensor(q_st[:, par, :, :, o * D1:(o + 1) * D1], q_src,
                                                  q_st[:, par, :, :, 0:D1].bitcast(F), ALU.subtract)
                    last.then_inc(s["st_ready"], 1)

                def values(g, par):
                    pool.tensor_tensor(v_st[:, par, :, 0:D1], v1[:].rearrange("p t (g d) -> p t g d", d=D1)[:, :, g, :],
                                       one_b, ALU.mult).then_inc(s["v1_ready"], 1)

                stacks(0, 0)
                pool.memset(v_st[:, :, :, D1:SUM_AT], 0.0)
                pool.memset(v_st[:, :, :, SUM_AT:SUM_AT + D1], 1.0)
                pool.drain()
                values(0, 0)
                values(1, 1)
                pool.wait_ge(s["qt_psum"], ONE + XP * NPAIR * b + 2)
                stacks(1, 1)

                with pool.Fori(0, NPAIR - 1) as n:
                    for par in range(2):
                        pool.wait_ge(s["qt_psum"], ONE + XP * (NPAIR * b + n) + x_at(GQ * par + 2, "T2", True) + 2)
                        stacks(2 * n + 2 + par, par)
                    values(2 * n + 2, 0)
                    pool.wait_ge(s["pv1_psum"], ONE + 2 * PH * (NPAIR * b + n + 1))
                    values(2 * n + 3, 1)

        @block.tensor
        def _(pe):
            give_credit(pe, "tensor")
            bank = lambda i: psum[:, i, :]
            pe.wait_ge(s["consts"], 2)
            pe.wait_ge(s["pro_loaded"], 16 * 16)
            pe.matmul(bank(0)[:, 0:P], pr_wrT[:], pr_keysT[:], start=True, stop=True).then_inc(s["pro_mm"], 1)
            for c in range(EC):
                last = pe.matmul(bank(1)[:, 0:P], pr_wvdT[:, c, :], pr_avT[:, c, :], start=(c == 0), stop=(c == EC - 1))
            last.then_inc(s["pro_mm"], 1)
            pe.wait_ge(s["pro_evac"], 2)
            pe.matmul(bank(2)[:, 0:P], pr_wr[:], pr_rkT[:], start=True, stop=True).then_inc(s["pro_mm"], 1)
            pe.matmul(bank(3), pr_avd[:], pr_wvuT[:], start=True, stop=True).then_inc(s["pro_mm"], 1)
            pe.wait_ge(s["pro_act"], 1)
            for c in range(EC):
                for k in range(2):
                    last = pe.matmul(bank(4 + c), pr_a[:, k, c * P:(c + 1) * P], pr_b[:, k, :],
                                     start=(k == 0), stop=(k == 1))
                last.then_inc(s["pro_mm"], 1)
            pe.wait_ge(s["pro_act"], 3)
            pe.wait_ge(s["pro_evac"], 4)
            pe.matmul(bank(2)[:, 0:2], pr_ones[:], pr_sm[:, 6 * B * NT:6 * B * NT + 2], start=True, stop=True)\
                .then_inc(s["pro_mm"], 1)

            with pe.Fori(0, B) as b:
                G0 = b * KV0
                pe.wait_ge(s["y_ready"], ONE + NT * b)

                def transposed(t, src, base):
                    pe.wait_ge(s["xn_ready"], base + t + 1)
                    pe.wait_ge(s["xT_lo_done"], ONE + base + max(t - 1, 0))
                    for c in range(EC):
                        last = pe.matmul(bank(t % 2)[:, c * P:(c + 1) * P], src[:, t, c * P:(c + 1) * P], ident[:],
                                         start=True, stop=True, is_transpose=True)
                    last.then_inc(s["xT_psum"], 1)

                def xT(c, lo, hi):
                    return (xT_hi[:, c, lo:hi], xT_lo[:, c, lo:hi])

                pe.wait_ge(s["wa_lo_done"], b + 1)
                for t in range(NT + 1):
                    if t < NT:
                        transposed(t, xn, 2 * NT * b)
                    if t >= 1:
                        u = t - 1
                        pe.wait_ge(s["xT_lo_done"], ONE + 2 * NT * b + u + 1)
                        for c in range(EC):
                            last = hilo(pe, psum[:, 2 + u // 4, (u % 4) * P:(u % 4 + 1) * P], xT(c, u * P, (u + 1) * P),
                                        (wa_hi[:, c, 0:P], wa_lo[:, c, 0:P]), c == 0, c == EC - 1)
                        last.then_inc(s["z_psum"], 1)
                for h in range(2):
                    for c in range(EC):
                        last = hilo(pe, bank(4 + h), (wa_hi[:, c, P:2 * P], wa_lo[:, c, P:2 * P]),
                                    xT(c, 512 * h, 512 * h + 512), c == 0, c == EC - 1)
                    last.then_inc(s["query_psum"], 1)
                rbank = (0, 1, 6, 7)
                pe.wait_ge(s["query_done"], 2 * (b + 1))
                for t in range(NT):
                    last = pe.matmul(psum[:, rbank[t // 2], (t % 2) * 256:(t % 2) * 256 + 256], queryT[:, t * P:(t + 1) * P],
                                     router[:], start=True, stop=True)
                last.then_inc(s["router_psum"], 1)
                pe.wait_ge(s["att_ready"], b + 1)
                for t in range(NT):
                    last = pe.matmul(psum[:, 2 + t // 4, (t % 4) * P:(t % 4 + 1) * P], sc[:, t, :], ident[:],
                                     start=True, stop=True, is_transpose=True)
                last.then_inc(s["eT_psum"], 1)
                pe.wait_ge(s["eT_done"], b + 1)
                for t in range(NT):
                    if t >= 2:
                        pe.wait_ge(s["g0_lin"], ONE + NT * b + t - 1)
                    pe.matmul(bank(4 + t % 2), eT[:, t, :], auxvu[:], start=True, stop=True).then_inc(s["aux_psum"], 1)

                pe.wait_ge(s["g0_lin"], ONE + NT * (b + 1))
                M, O, TA, TB = 7, 6, 4, 5

                def prep_lump(p, half, w):
                    for c in range(EC):
                        last = hilo(pe, bank(M), (w[0][:, c * P:(c + 1) * P], w[1][:, c * P:(c + 1) * P]),
                                    xT(c, 512 * half, 512 * half + 512), c == 0, c == EC - 1)
                    last.then_inc(s["prep_psum"], 1)

                def group(G, prefetch):
                    wbase = 10 * G + 4
                    lumps = {}
                    for n, kind, j, t1, t2 in preps(prefetch):
                        lumps[t1] = (n, kind, j, 0)
                        lumps[t2] = (n, kind, j, 1)
                    m_user = [(s["oproj_evac"], ONE + 2 * NT * G)]

                    def m_free():
                        pe.wait_ge(*m_user[0])

                    def scores(t):
                        j, qi = t // NT, t % NT
                        if qi == 0:
                            if j == 0:
                                pe.wait_ge(s["k_ready"], G + 1)
                            pe.wait_ge(s["q_ready"], GQ * G + j + 1)
                        pe.wait_ge(s["exp_done"], ONE + TG * G + (t - 1 if t >= 2 else 0))
                        sl = 2 * (t % 2)
                        lhs = (qT_hi[:, j % 2, qi * P:(qi + 1) * P], qT_lo[:, j % 2, qi * P:(qi + 1) * P])
                        kh, kl = kT_hi[:].rearrange("p a n -> p (a n)"), kT_lo[:].rearrange("p a n -> p (a n)")
                        k0 = (qi + 1) * P
                        for bi, (lo, n) in enumerate(((0, 512), (512, KEYS - 512))):
                            dst = psum[:, sl + bi, 0:n]
                            rhs = (kh[:, k0 + lo:k0 + lo + n], kl[:, k0 + lo:k0 + lo + n])
                            masked = (qi < NT - 1) if bi == 0 else (qi > 0)
                            last = hilo(pe, dst, lhs, rhs, True, not masked)
                            if masked:
                                m, at = (mask_ge, 0) if bi == 0 else (mask_le, n - P)
                                last = pe.matmul(psum[:, sl + bi, at:at + P], ident_b[:], m[:], start=False, stop=True)
                        last.then_inc(s["scores_ready"], 1)

                    def transposes(t):
                        qi = t % NT
                        sl = t % 3
                        pe.wait_ge(s["recip_ready"], TG * G + t + 1)
                        pe.wait_ge(s["ta_evac"], ONE + TG * G + t)
                        pe.wait_ge(s["tb_evac"], ONE + TG * G + t)
                        for kb in range(NT):
                            if kb == qi:
                                src = stat[:, 2, t % 4:t % 4 + 1].broadcast_to([P, P])
                            else:
                                c = (kb - qi - 1) % NT
                                src = probs[:, sl, c * P:(c + 1) * P]
                            last = pe.matmul(psum[:, TA + kb // 4, (kb % 4) * P:(kb % 4 + 1) * P], src, ident[:],
                                             start=True, stop=True, is_transpose=True)
                            if kb == 3:
                                last.then_inc(s["ta_full"], 1)
                        last.then_inc(s["tb_full"], 1)

                    def pv(c, part):
                        own = 4 * (c % 2)
                        if part == 0:
                            pe.wait_ge(s["ta_evac"], ONE + TG * G + 4 * c + 4)
                            pe.wait_ge(s["tb_evac"], ONE + TG * G + 4 * c + 4)
                            pe.wait_ge(s["o_norm"], ONE + CG * G + c)
                            if c == 0:
                                pe.wait_ge(s["v_evac"], ONE + 2 * (G + 1))
                                pe.wait_ge(s["oproj_evac"], ONE + 2 * NT * G)
                        for i in (2 * part, 2 * part + 1):
                            kb = pv_keys(c)[i]
                            d = kb - own
                            cols = [(0, 512)] if not 0 <= d < 4 else \
                                [x for x in ((0, d * P), ((d + 1) * P, 512)) if x[1] > x[0]]
                            for n, (lo, hi) in enumerate(cols):
                                last = pe.matmul(psum[:, O, lo:hi], v_sb[:, kb, :], pT[:, c % 2, kb, lo:hi],
                                                 start=(i == 0), stop=(i == NT - 1 and n == len(cols) - 1))
                        if part == 3:
                            last.then_inc(s["pv_done"], 1)

                    def oproj(pair, tt, dst):
                        first = 4 * pair + (3 if tt < 4 else 4)
                        if tt % 4 == 0:
                            pe.wait_ge(s["o_lo_done"], CG * G + first)
                            if tt == 0:
                                for i in (0, 1):
                                    pe.wait_ge(s["w_ready"], ONE + wbase + w_index(prefetch, "o", 2 * pair + i))
                        for i in range(2):
                            lhs = (oT_hi[:, i, tt * P:(tt + 1) * P], oT_lo[:, i, tt * P:(tt + 1) * P])
                            last = hilo(pe, bank(dst), lhs, (wo_hi[:, i, :], wo_lo[:, i, :]), i == 0, i == 1)
                        last.then_inc(s["oproj_psum"], 1)

                    def lump(t):
                        if t in lumps:
                            n, kind, j, half = lumps[t]
                            m_free()
                            if half == 0:
                                need = 10 * G + 4 if (kind, j) == ("q", 1) else wbase + w_index(prefetch, kind, j)
                                pe.wait_ge(s["w_ready"], ONE + need)
                            prep_lump(None, half, w_slot(kind, j))
                            m_user[0] = (s["raw_ready"], ONE + 10 * G + 2 * (n + 1) + half + 1)

                    for t in range(TG):
                        scores(t)
                        if t in V_STEPS:
                            half = V_STEPS.index(t)
                            if half == 0:
                                pe.wait_ge(s["w_ready"], ONE + 10 * G + 3)
                            else:
                                pe.wait_ge(s["v_evac"], ONE + 2 * G + 1)
                            for u in range(4):
                                tt = 4 * half + u
                                for c in range(EC):
                                    last = hilo(pe, psum[:, O, u * P:(u + 1) * P], xT(c, tt * P, (tt + 1) * P),
                                                (wv_hi[:, c * P:(c + 1) * P], wv_lo[:, c * P:(c + 1) * P]),
                                                c == 0, c == EC - 1)
                            last.then_inc(s["v_psum"], 1)
                        if pv_parts(t) is not None:
                            pv(*pv_parts(t))
                        if 22 <= t < 22 + NT:
                            m_free()
                            oproj(0, t - 22, M)
                            m_user[0] = (s["oproj_evac"], ONE + 2 * NT * G + t - 22 + 1)
                        lump(t)
                        if t >= 2:
                            transposes(t - 2)
                    pv(6, 2)
                    transposes(TG - 2)
                    pv(6, 3)
                    transposes(TG - 1)
                    lump(TG)
                    for part in range(4):
                        pv(7, part)
                    for tt in range(NT):
                        if tt == 0:
                            m_free()
                        elif tt == 1:
                            pe.wait_ge(s["o_norm"], ONE + CG * G + CG)
                        else:
                            pe.wait_ge(s["oproj_evac"], ONE + 2 * NT * G + NT + tt - 1)
                        oproj(1, tt, M if tt % 2 == 0 else O)

                for i, p in enumerate(("k", "q")):
                    pe.wait_ge(s["w_ready"], ONE + 10 * G0 + i + 1)
                    for half in range(2):
                        pe.wait_ge(s["raw_ready"], ONE + 10 * G0 + 2 * i + half)
                        prep_lump(None, half, w_slot(p, 0))
                with pe.Fori(0, KV0 - 1) as g:
                    group(G0 + g, True)
                group(G0 + KV0 - 1, False)

                pe.wait_ge(s["oproj_evac"], ONE + 2 * NT * KV0 * (b + 1))
                for t in range(NT + 1):
                    if t < NT:
                        transposed(t, gx, 2 * NT * b + NT)
                    if t >= 1:
                        u = t - 1
                        if u == 0:
                            pe.wait_ge(s["w1_lo_done"], b + 1)
                        pe.wait_ge(s["xT_lo_done"], ONE + 2 * NT * b + NT + u + 1)
                        if u >= 2:
                            pe.wait_ge(s["qkv_evac"], ONE + NT * b + u - 1)
                            pe.wait_ge(s["ffn_lin"], ONE + NT * b + u - 1)
                        for lo, n in ((0, 512), (512, W1N - 512)):
                            for c in range(EC):
                                last = hilo(pe, psum[:, 2 + 2 * (u % 2) + lo // 512, 0:n], xT(c, u * P, (u + 1) * P),
                                            (w1_hi[:, c, lo:lo + n], w1_lo[:, c, lo:lo + n]), c == 0, c == EC - 1)
                        last.then_inc(s["qkv_psum"], 1)
                        for c in range(EC):
                            last = hilo(pe, bank(6 + u % 2), xT(c, u * P, (u + 1) * P),
                                        (w1_hi[:, c, W1N:], w1_lo[:, c, W1N:]), c == 0, c == EC - 1)
                        last.then_inc(s["ffn_psum"], 1)

                QM, KM, X, Y = 0, 2, 5, 6

                def stack_T(src, half, x):
                    pe.wait_ge(s["qt_evac"], ONE + x)
                    for i in range(4):
                        last = pe.matmul(psum[0:ST1, X, i * P:(i + 1) * P].bitcast(R), src[:, 4 * half + i, :],
                                         ident_r[:], start=True, stop=True, is_transpose=True)
                    last.then_inc(s["qt_psum"], 1)

                def q_scores(j, h, c):
                    i, k0, w = q_chunks()[c]
                    pe.wait_ge(s["qm_max"], ONE + CH * h + (c - 1 if c >= 2 else 0))
                    diag = k0 + w == (i + 1) * P
                    last = pe.matmul(psum[:, QM + c % 2, 0:w], qTa[0:ST1, j % 2, i * P:(i + 1) * P],
                                     kT1[0:ST1, (j // GQ) % 2, k0:k0 + w], start=True, stop=not diag)
                    if diag:
                        last = pe.matmul(psum[:, QM + c % 2, w - P:w], ident_b[:], mask_le[:], start=False, stop=True)
                    last.then_inc(s["qm_psum"], 1)

                def k_scores(j, h, c):
                    i, q0, w = k_chunks()[c]
                    pe.wait_ge(s["km_exp"], ONE + CH * h + (c - 2 if c >= 3 else 0))
                    diag = q0 == i * P
                    last = pe.matmul(psum[:, KM + c % 3, 0:w], kT1[0:ST1, (j // GQ) % 2, i * P:(i + 1) * P],
                                     qTb[0:ST1, j % 2, q0:q0 + w], start=True, stop=not diag)
                    if diag:
                        last = pe.matmul(psum[:, KM + c % 3, 0:P], ident_b[:], mask_ge[:], start=False, stop=True)
                    last.then_inc(s["km_psum"], 1)

                def pv1(j, h, c):
                    i, q0, w = k_chunks()[c]
                    pe.wait_ge(s["km_exp"], ONE + CH * h + c + 1)
                    if c == 0:
                        pe.wait_ge(s["pv1_evac"], ONE + 2 * h)
                    for lo, hi in ((q0, min(q0 + w, 512)), (max(q0, 512), q0 + w)):
                        if lo < hi:
                            half = lo // 512
                            last = pe.matmul(psum[0:VS, Y + half, lo % 512:lo % 512 + hi - lo],
                                             v_st[:, (j // GQ) % 2, i, :], pT1_cols(i, lo, hi - lo),
                                             start=(i == 0), stop=(i == 4 * half + 3))
                    if c in (7, CH - 1):
                        last.then_inc(s["pv1_psum"], 1)

                def pair(N, prefetch):
                    for j in range(PH):
                        h = PH * N + j
                        turns = x_turns(j, prefetch)
                        for c in range(CH):
                            if c + 2 < CH:
                                k_scores(j, h, c + 2)
                            elif "T2" in turns:
                                if c + 2 == CH:
                                    pe.wait_ge(s["qt_evac"], ONE + XP * N + x_at(j, "T2", prefetch) + 2)
                                k_scores(j + 1, h + 1, c + 2 - CH)
                            if "T2" in turns and c < CH // 2:
                                q_scores(j + 1, h + 1, 2 * c)
                                q_scores(j + 1, h + 1, 2 * c + 1)
                            if "T1" in turns and c in (1, 3):
                                if c == 1:
                                    pe.wait_ge(s["st_ready"], 2 * (2 * N + (j + 2) // GQ + 1))
                                stack_T(q_st[:, ((j + 2) // GQ) % 2, :, (j + 2) % GQ, :], c // 2,
                                        XP * N + x_at(j, "T1", prefetch) + c // 2)
                            if "K" in turns and c in (5, 6):
                                if c == 5:
                                    pe.wait_ge(s["st_ready"], 2 * (2 * N + j // GQ + 1) + 1)
                                stack_T(k_st, c - 5, XP * N + x_at(j, "K", prefetch) + c - 5)
                            if "T2" in turns and c in (7, 8):
                                if c == 7:
                                    pe.wait_ge(s["nm_ready"], h + 2)
                                stack_T(q_st[:, ((j + 1) // GQ) % 2, :, (j + 1) % GQ, :], c - 7,
                                        XP * N + x_at(j, "T2", prefetch) + c - 7)
                            if c == 0 and j % GQ == 0:
                                pe.wait_ge(s["v1_ready"], 2 * N + j // GQ + 1)
                            pv1(j, h, c)

                N0 = NPAIR * b
                pe.wait_ge(s["qkv_evac"], ONE + NT * (b + 1))
                pe.wait_ge(s["ffn_lin"], ONE + NT * (b + 1))
                pe.wait_ge(s["st_ready"], 4 * N0 + 1)
                for half in range(2):
                    stack_T(k_st, half, XP * N0 + half)
                pe.wait_ge(s["st_ready"], 4 * N0 + 2)
                for j in range(2):
                    for half in range(2):
                        stack_T(q_st[:, 0, :, j, :], half, XP * N0 + 2 + 2 * j + half)
                for c in range(CH):
                    q_scores(0, PH * N0, c)
                pe.wait_ge(s["nm_ready"], PH * N0 + 1)
                for half in range(2):
                    stack_T(q_st[:, 0, :, 0, :], half, XP * N0 + 6 + half)
                pe.wait_ge(s["qt_evac"], ONE + XP * N0 + XL)
                for c in range(2):
                    k_scores(0, PH * N0, c)
                with pe.Fori(0, NPAIR - 1) as n:
                    pair(N0 + n, True)
                pair(N0 + NPAIR - 1, False)

                pe.wait_ge(s["wo1_loaded"], 16 * (b + 1))
                for t in range(NT):
                    if t in (0, NT // 2):
                        pe.wait_ge(s["ctx_ready"], ONE + 2 * NPAIR * (b + 1) - 1 + (t > 0))
                    pe.wait_ge(s["y_ready"], ONE + NT * b + max(t - 3, 0))
                    for c in range(EC):
                        last = pe.matmul(bank(t % 4), ctxT[:, c, t * P:(t + 1) * P], wo1[:, c, :],
                                         start=(c == 0), stop=(c == EC - 1))
                    last.then_inc(s["y_psum"], 1)

        @block.scalar
        def _(act):
            give_credit(act, "scalar")
            act.wait_ge(s["consts"], 2)
            act.activation(ident_r[:], ident[:], ACT.Copy)
            act.wait_ge(s["pro_stats"], 3)
            act.activation(pr_sm[:, 7 * B * NT:7 * B * NT + 1], pr_sm[:, 0:1], ACT.Copy).then_inc(s["pro_act"], 1)
            act.activation(pr_sm[:, 7 * B * NT + 1:7 * B * NT + 2], pr_sm[:, 0:1], ACT.Copy).then_inc(s["pro_act"], 1)
            act.wait_ge(s["pro_stats"], 4)
            act.activation(half_norm[:], pr_sm[:, B * NT:2 * B * NT], ACT.Ln, bias=1.0,
                           accum_out=pr_sm[:, 6 * B * NT:6 * B * NT + 1]).then_inc(s["pro_act"], 1)

            with act.Fori(0, B) as b:
                G0 = b * KV0

                def hi_of(t, base):
                    act.wait_ge(s["xT_psum"], base + t + 1)
                    act.activation(xT_hi[:, :, t * P:(t + 1) * P], psum[:, t % 2, :].rearrange("p (c n) -> p c n", c=EC),
                                   ACT.Copy).then_inc(s["xT_hi_done"], 1)

                act.wait_ge(s["wa_loaded"], 16 * (b + 1))
                act.activation(wa_hi[:], wa_f[:], ACT.Copy).then_inc(s["wa_hi_done"], 1)
                for t in range(NT):
                    hi_of(t, 2 * NT * b)
                act.wait_ge(s["gelu_in"], b + 1)
                act.activation(zt[:], zt[:], ACT.Tanh, scale=GELU_C).then_inc(s["gelu_exp"], 1)
                act.wait_ge(s["router_psum"], b + 1)
                for i, bk in enumerate((0, 1, 6, 7)):
                    last = act.activation(sc[:, 2 * i:2 * i + 2, :],
                                          psum[:, bk, :].rearrange("p (t k n) -> p t k n", t=2, k=2)[:, :, 0, :], ACT.Copy)
                last.then_inc(s["sc_done"], 1)
                for k in range(2):
                    act.wait_ge(s["gate_in"], 2 * b + k + 1)
                    act.activation(sma[:, 1 + k, :], sma[:, 1 + k, :], ACT.Tanh, scale=0.5).then_inc(s["gate_exp"], 1)
                act.wait_ge(s["att_in"], b + 1)
                act.activation(sc[:], rep[:], ACT.Exp).then_inc(s["att_exp"], 1)
                act.wait_ge(s["eT_psum"], b + 1)
                act.activation(eT[:].rearrange("p t n -> p (t n)"),
                               psum[:, 2:4, :].rearrange("p a n -> p (a n)"), ACT.Copy).then_inc(s["eT_done"], 1)
                for t in range(NT):
                    act.wait_ge(s["g0_lin"], ONE + NT * b + t + 1)
                    act.activation(ex_a[:, t, :], xn[:, t, :], ACT.Tanh, scale=0.5).then_inc(s["g0_exp"], 1)

                M, O, TA, TB = 7, 6, 4, 5
                act.wait_ge(s["g0_stored"], 16 * (b + 1))

                def w_hi(idx, i, kind, j):
                    act.wait_ge(s[f"w_loaded{i % 2}"], 16 * (idx + 1))
                    act.activation(w_slot(kind, j)[0], w_st[:, i % 2, :], ACT.Copy).then_inc(s["w_hi_done"], 1)

                def raw_copy(p, half):
                    act.wait_ge(s["prep_psum"], 2 * p + half + 1)
                    if half == 0:
                        act.wait_ge(s["roped"], ONE + p)
                    act.activation(raw[:, 512 * half:512 * half + 512], psum[:, M, :], ACT.Copy)\
                        .then_inc(s["raw_ready"], 1)

                def q_hi(p, j, free):
                    act.wait_ge(s["roped"], ONE + p + 1)
                    act.wait_ge(s["scores_ready"], ONE + free)
                    act.activation(qT_hi[:, j % 2, :], q_f[:], ACT.Copy).then_inc(s["q_hi_done"], 1)

                def k_hi(G, p):
                    act.wait_ge(s["roped"], ONE + p + 1)
                    act.wait_ge(s["scores_ready"], ONE + TG * G)
                    for half in range(2):
                        last = act.activation(kT_hi[:, half, :], k_f[:], ACT.Copy)
                    last.then_inc(s["k_hi_done"], 1)

                def group(G, prefetch):
                    w_at = {t: (i, k, j) for i, (t, k, j) in enumerate(w_items(prefetch))}
                    raws, his = {}, {}
                    for n, kind, j, t1, t2 in preps(prefetch):
                        raws[t1] = (n, 0)
                        raws[t2] = (n, 1)
                        if kind == "q" and j > 0:
                            his[t2 + 3] = (n, j)

                    def exp(t):
                        act.wait_ge(s["negmax_ready"], TG * G + t + 1)
                        act.wait_ge(s["tb_full"], ONE + TG * G + (t - 2 if t >= 3 else 0))
                        act.activation(probs[:, t % 3, :], psum[:, 2 * (t % 2):2 * (t % 2) + 2, :]
                                       .rearrange("p a n -> p (a n)")[:, 0:KEYS], ACT.Exp, bias=stat[:, 0, t % 4:t % 4 + 1],
                                       accum_out=stat[:, 1, t % 4:t % 4 + 1]).then_inc(s["exp_done"], 1)

                    def ta(t):
                        c = t // 4
                        act.wait_ge(s["ta_full"], TG * G + t + 1)
                        act.wait_ge(s["o_norm"], ONE + CG * G + (c - 1 if c >= 2 else 0))
                        act.activation(pT[:, c % 2, 0:4, (t % 4) * P:(t % 4 + 1) * P],
                                       psum[:, TA, :].rearrange("p (k n) -> p k n", k=4), ACT.Copy)\
                            .then_inc(s["ta_evac"], 1)

                    def o_hi(c):
                        j, half = c // 2, c % 2
                        act.wait_ge(s["o_norm"], ONE + CG * G + c + 1)
                        act.wait_ge(s["oproj_psum"], ONE + 2 * NT * G + (0 if j < 2 else 4 + 4 * half))
                        act.activation(oT_hi[:, j % 2, 512 * half:512 * half + 512], o_f[:], ACT.Copy)\
                            .then_inc(s["o_hi_done"], 1)

                    for t in range(TG):
                        exp(t)
                        if t in V_STEPS:
                            half = V_STEPS.index(t)
                            act.wait_ge(s["v_psum"], 2 * G + half + 1)
                            act.activation(v_sb[:, 4 * half:4 * half + 4, :],
                                           psum[:, O, :].rearrange("p (k n) -> p k n", k=4), ACT.Copy)\
                                .then_inc(s["v_evac"], 1)
                        if pv_parts(t) is not None and pv_parts(t)[1] == 3:
                            o_hi(pv_parts(t)[0])
                        if t in his:
                            n, j = his[t]
                            q_hi(5 * G + 1 + n, j, TG * G + NT * (j - 1))
                        if t in raws:
                            pr, half = raws[t]
                            raw_copy(5 * G + 1 + pr, half)
                        if t >= 2:
                            ta(t - 2)
                        if t in w_at:
                            i, kind, j = w_at[t]
                            if kind == "o" and j == 0:
                                act.wait_ge(s["oproj_psum"], ONE + 2 * NT * G)
                            if kind == "o" and j == 2:
                                act.wait_ge(s["oproj_psum"], ONE + 2 * NT * G + NT)
                            if kind == "q":
                                act.wait_ge(s["prep_psum"], 10 * G + {2: 4, 3: 6, 0: 8, 1: 12}[j])
                            if kind == "v":
                                act.wait_ge(s["v_psum"], 2 * G + 2)
                            w_hi(5 * G + 2 + i // 2, i, kind, j)
                    ta(TG - 2)
                    o_hi(6)
                    ta(TG - 1)
                    if prefetch:
                        raw_copy(5 * G + 1 + 5, 1)
                        k_hi(G + 1, 5 * G + 1 + 3)
                    o_hi(7)
                    if prefetch:
                        q_hi(5 * G + 1 + 5, 0, TG * G + 3 * NT)

                for i, (kind, j) in enumerate(W_PRE):
                    w_hi(5 * G0 + i // 2, i, kind, j)
                act.wait_ge(s["tabs_loaded"], 32 * (b + 1))
                for p in range(2):
                    for half in range(2):
                        raw_copy(5 * G0 + p, half)
                k_hi(G0, 5 * G0)
                q_hi(5 * G0 + 1, 0, TG * G0)
                with act.Fori(0, KV0 - 1) as g:
                    group(G0 + g, True)
                group(G0 + KV0 - 1, False)

                act.wait_ge(s["w1_loaded"], 48 * (b + 1))
                act.activation(w1_hi[:], w1_f[:], ACT.Copy).then_inc(s["w1_hi_done"], 1)
                for t in range(NT + 1):
                    if t < NT:
                        hi_of(t, 2 * NT * b + NT)
                    if t >= 1:
                        u = t - 1
                        act.wait_ge(s["ffn_lin"], ONE + NT * b + u + 1)
                        act.activation(g_exp[:, u % 2, :], g_lin[:, u % 2, :], ACT.Tanh, scale=0.5).then_inc(s["ffn_exp"], 1)

                QM, KM, X, Y = 0, 2, 5, 6
                act.wait_ge(s["qkv_evac"], ONE + NT * (b + 1))
                act.wait_ge(s["ffn_done"], NT * (b + 1))

                def stack_evac(dst, half, x):
                    act.wait_ge(s["qt_psum"], ONE + x + 1)
                    act.activation(dst[0:ST1, 512 * half:512 * half + 512], psum[0:ST1, X, :], ACT.Copy)\
                        .then_inc(s["qt_evac"], 1)

                def out_evac(j, h, half):
                    act.wait_ge(s["pv1_psum"], ONE + 2 * h + half + 1)
                    if half == 0:
                        act.wait_ge(s[f"o_moved{j % 2}"], ONE + 16 * (h - j) + 32 * (j // 2))
                    act.activation(o_st[:, j % 2, 512 * half:512 * half + 512], psum[0:VS, Y + half, :], ACT.Copy)\
                        .then_inc(s["pv1_evac"], 1)

                def pair(N, prefetch):
                    for j in range(PH):
                        h = PH * N + j
                        turns = x_turns(j, prefetch)
                        for c in range(CH):
                            i, q0, w = k_chunks()[c]
                            act.wait_ge(s["km_psum"], ONE + CH * h + c + 1)
                            act.activation(pT1_cols(i, q0, w), psum[:, KM + c % 3, 0:w], ACT.Exp).then_inc(s["km_exp"], 1)
                            if c == 5 and "K" in turns:
                                stack_evac(kT1[:, (j // GQ + 1) % 2], 0, XP * N + x_at(j, "K", prefetch))
                            if c in (7, 8) and "T2" in turns:
                                stack_evac(qTb[:, (j + 1) % 2], c - 7, XP * N + x_at(j, "T2", prefetch) + c - 7)
                            if c == 9:
                                out_evac(j, h, 0)
                        out_evac(j, h, 1)

                N0 = NPAIR * b
                stack_evac(kT1[:, 0], 0, XP * N0)
                for half in range(2):
                    stack_evac(qTb[:, 0], half, XP * N0 + 6 + half)
                with act.Fori(0, NPAIR - 1) as n:
                    pair(N0 + n, True)
                pair(N0 + NPAIR - 1, False)

        @block.vector
        def _(dve):
            give_credit(dve, "vector")
            N2 = B * NT

            def sm(i, n=N2):
                return pr_sm[:, i * N2:i * N2 + n]

            dve.wait_ge(s["pro_x"], 16)
            for t in range(N2):
                dve.bn_stats(pr_st[:, t, :], pr_x[:, t, :])
            dve.drain()
            for t in range(N2):
                dve.bn_aggr(mv0[:, t, :], pr_st[:, t, :])
            dve.drain()
            dve.tensor_scalar(sm(0), mv0[:, :, 1], LN_EPS, None, ALU.add).then_inc(s["pro_stats"], 1)
            dve.memset(sm(6, 2), 0.0)
            dve.wait_ge(s["pro_loaded"], 16 * 16)
            dve.tensor_tensor(pr_mix[:], pr_cs[:, :, 0], pr_cs[:, :, 1], ALU.mult)
            dve.drain()
            for k in range(2):
                last = dve.tensor_scalar(pr_b[:, k, :], pr_b[:, k, :], pr_mix[:, k:k + 1], None, ALU.mult)
                last.then_inc(s["pro_stats"], 1)
            dve.wait_ge(s["pro_pow"], 1)
            dve.tensor_tensor(sm(2), rstd0[:], rstd0[:], ALU.mult)
            dve.drain()
            dve.tensor_tensor(sm(1), sm(2), mv0[:, :, 1], ALU.mult).then_inc(s["pro_stats"], 1)
            dve.wait_ge(s["pro_mm"], 1)
            dve.tensor_copy(pr_rkT[:], psum[:, 0, 0:P]).then_inc(s["pro_evac"], 1)
            dve.wait_ge(s["pro_mm"], 2)
            dve.tensor_copy(pr_avd[:], psum[:, 1, 0:P]).then_inc(s["pro_evac"], 1)
            dve.wait_ge(s["pro_mm"], 3)
            dve.tensor_scalar(router[0:BOT, 0:P], psum[0:BOT, 2, 0:P], float(RDIM) ** -0.5, None, ALU.mult)
            dve.tensor_scalar(router[0:BOT, P:2 * P], pr_keysT[0:BOT, :], float(BOT) ** -0.5, None, ALU.mult)\
                .then_inc(s["pro_evac"], 1)
            dve.wait_ge(s["pro_mm"], 4)
            dve.tensor_copy(auxvu[:], psum[:, 3, :]).then_inc(s["pro_evac"], 1)
            for c in range(EC):
                dve.wait_ge(s["pro_mm"], 5 + c)
                dve.tensor_tensor(pr_w[:, c, :], psum[:, 4 + c, :], pr_w[:, c, :], ALU.add).then_inc(s["pro_evac"], 1)
            dve.wait_ge(s["pro_mm"], 5 + EC)
            dve.tensor_scalar(sm(3, 1), psum[:, 2, 0:1], 1.0 / (B * S), 1e-6, ALU.mult, ALU.add)
            dve.drain()
            dve.reciprocal(sm(4, 1), sm(3, 1))
            dve.drain()
            dve.tensor_scalar(half_norm[:], half_norm[:], sm(4, 1), 0.5, ALU.mult, ALU.mult)
            dve.drain()

            with dve.Fori(0, B) as b:
                G0 = b * KV0

                def lo_of(t, base):
                    dve.wait_ge(s["xT_hi_done"], base + t + 1)
                    dve.tensor_tensor(xT_lo[:, :, t * P:(t + 1) * P], psum[:, t % 2, :].rearrange("p (c n) -> p c n", c=EC),
                                      xT_hi[:, :, t * P:(t + 1) * P].bitcast(F), ALU.subtract).then_inc(s["xT_lo_done"], 1)

                dve.wait_ge(s["x_loaded"], 16 * (b + 1))
                dve.wait_ge(s["wa_hi_done"], b + 1)
                dve.tensor_tensor(wa_lo[:], wa_f[:], wa_hi[:].bitcast(F), ALU.subtract).then_inc(s["wa_lo_done"], 1)
                mean, rstd, hn = sma[:, 8, :], sma[:, 9, :], sma[:, 10, :]
                dve.tensor_copy(mean, mv0[:, :, 0].rearrange("p (b t) -> p b t", b=B)[:, b, :])
                dve.tensor_copy(rstd, rstd0[:].rearrange("p (b t) -> p b t", b=B)[:, b, :])
                dve.tensor_copy(hn, half_norm[:].rearrange("p (b t) -> p b t", b=B)[:, b, :])
                dve.drain()
                for t in range(NT):
                    dve.tensor_scalar(xn[:, t, :], acc[:, t, :], mean[:, t:t + 1], rstd[:, t:t + 1],
                                      ALU.subtract, ALU.mult).then_inc(s["xn_ready"], 1)
                    if t >= 1:
                        lo_of(t - 1, 2 * NT * b)
                lo_of(NT - 1, 2 * NT * b)
                dve.wait_ge(s["z_psum"], NT * (b + 1))
                zps = psum[:, 2:4, :].rearrange("p a (t n) -> p (a t) n", t=4)
                bc = lambda v: v[:, :].unsqueeze(1).broadcast_to([P, NT, P])
                dve.tensor_tensor(zb[:], zps, bc(bu1_b), ALU.add)
                dve.drain()
                dve.tensor_tensor(zt[:], zb[:], zb[:], ALU.mult)
                dve.drain()
                dve.tensor_scalar(zt[:], zt[:], GELU_A, 1.0, ALU.mult, ALU.add)
                dve.drain()
                dve.tensor_tensor(zt[:], zt[:], zb[:], ALU.mult).then_inc(s["gelu_in"], 1)
                for h in range(2):
                    dve.wait_ge(s["query_psum"], 2 * b + h + 1)
                    dve.tensor_scalar(queryT[:, 512 * h:512 * h + 512], psum[:, 4 + h, :], row64[:], None, ALU.add)\
                        .then_inc(s["query_done"], 1)
                dve.wait_ge(s["gelu_exp"], b + 1)
                dve.scalar_tensor_tensor(zt[:].rearrange("p t n -> p (t n)"), zt[:].rearrange("p t n -> p (t n)"), 1.0,
                                         zb[:].rearrange("p t n -> p (t n)"), ALU.add, ALU.mult)
                dve.drain()
                dve.tensor_tensor(zt[:], zt[:], bc(wu2_b), ALU.mult)
                dve.drain()
                sig, u, gate, ssum, coef, mx = sma[:, 1, :], sma[:, 2, :], sma[:, 3, :], sma[:, 4, :], sma[:, 5, :], sma[:, 6, :]
                tmp = sma[:, 7, :]
                dve.tensor_reduce(sig, zt[:], AX.X, ALU.add)
                dve.drain()
                dve.tensor_scalar(sig, sig, 0.5, scal_b[:, 0:1], ALU.mult, ALU.add).then_inc(s["gate_in"], 1)
                dve.wait_ge(s["gate_exp"], 2 * b + 1)
                dve.tensor_scalar(u, sig, 1.25, 1.25, ALU.mult, ALU.add)
                dve.drain()
                dve.tensor_tensor(u, u, hn, ALU.add)
                dve.drain()
                dve.tensor_scalar(u, u, 0.0, 5.0, ALU.max, ALU.min)
                dve.drain()
                dve.tensor_scalar(u, u, 0.5, 1.0 / 1.5, ALU.subtract, ALU.mult)
                dve.drain()
                dve.tensor_scalar(u, u, 0.0, 1.0, ALU.max, ALU.min)
                dve.drain()
                dve.tensor_scalar(u, u, scal_b[:, 1:2], scal_b[:, 2:3], ALU.mult, ALU.add).then_inc(s["gate_in"], 1)
                dve.wait_ge(s["gate_exp"], 2 * b + 2)
                dve.tensor_scalar(gate, u, 0.5, 0.5, ALU.mult, ALU.add)
                dve.drain()
                dve.tensor_scalar(tmp, gate, 0.05, None, ALU.is_ge)
                dve.drain()
                dve.wait_ge(s["sc_done"], b + 1)
                dve.tensor_tensor(gate, gate, tmp, ALU.mult)
                for t in range(NT):
                    dve.max(top8[:, t, :], sc[:, t, :])
                dve.drain()
                for t in range(NT):
                    dve.match_replace(rep[:, t, :], top8[:, t, :], sc[:, t, :], -3.0e38)
                dve.drain()
                dve.tensor_tensor(rep[:], rep[:], sc[:], ALU.not_equal)
                dve.drain()
                dve.tensor_scalar(rep[:], rep[:], -NEG, NEG, ALU.mult, ALU.add)
                dve.drain()
                for i, bk in enumerate((0, 1, 6, 7)):
                    dve.tensor_tensor(rep[:, 2 * i:2 * i + 2, :],
                                      psum[:, bk, :].rearrange("p (t k n) -> p t k n", t=2, k=2)[:, :, 1, :],
                                      rep[:, 2 * i:2 * i + 2, :], ALU.add)
                dve.drain()
                dve.tensor_reduce(mx, rep[:], AX.X, ALU.max)
                dve.drain()
                dve.tensor_tensor(rep[:], rep[:], mx.unsqueeze(2).broadcast_to([P, NT, P]), ALU.subtract)\
                    .then_inc(s["att_in"], 1)
                dve.wait_ge(s["att_exp"], b + 1)
                dve.tensor_reduce(ssum, sc[:], AX.X, ALU.add).then_inc(s["att_ready"], 1)
                dve.drain()
                dve.reciprocal(coef, ssum)
                dve.drain()
                dve.tensor_tensor(coef, coef, gate, ALU.mult)
                dve.drain()
                for t in range(NT):
                    dve.wait_ge(s["aux_psum"], NT * b + t + 1)
                    dve.scalar_tensor_tensor(xn[:, t, :], psum[:, 4 + t % 2, :], coef[:, t:t + 1], xn[:, t, :],
                                             ALU.mult, ALU.add).then_inc(s["g0_lin"], 1)
                dve.wait_ge(s["g0_exp"], NT * (b + 1))
                flat = lambda v: v[:].rearrange("p t n -> p (t n)")
                dve.scalar_tensor_tensor(flat(xn), flat(ex_a), 1.0, flat(xn), ALU.add, ALU.mult)\
                    .then_inc(s["g0_ready"], 1)

                M, O, TA, TB = 7, 6, 4, 5
                dve.wait_ge(s["g0_stored"], 16 * (b + 1))
                dve.memset(acc[:], 0.0).then_inc(s["acc_zero"], 1)

                def rope(p, dst):
                    dve.wait_ge(s["rope_mul"], p + 1)
                    dve.tensor_tensor(dst[:], dst[:], swp[:], ALU.add).then_inc(s["roped"], 1)

                def q_lo(n, j):
                    dve.wait_ge(s["q_hi_done"], n + 1)
                    dve.tensor_tensor(qT_lo[:, j % 2, :], q_f[:], qT_hi[:, j % 2, :].bitcast(F), ALU.subtract)\
                        .then_inc(s["q_ready"], 1)

                def k_lo(G):
                    dve.wait_ge(s["k_hi_done"], G + 1)
                    for half in range(2):
                        last = dve.tensor_tensor(kT_lo[:, half, :], k_f[:], kT_hi[:, half, :].bitcast(F), ALU.subtract)
                    last.then_inc(s["k_ready"], 1)

                def group(G, prefetch):
                    ropes, los = {}, {}
                    for n, kind, j, t1, t2 in preps(prefetch):
                        if t2 + 3 < TG:
                            ropes[t2 + 2] = (n, kind)
                            if kind == "q":
                                los[t2 + 3] = j

                    def negmax(t):
                        dve.wait_ge(s["scores_ready"], ONE + TG * G + t + 1)
                        dve.tensor_reduce(stat[:, 0, t % 4:t % 4 + 1], psum[:, 2 * (t % 2):2 * (t % 2) + 2, :]
                                          .rearrange("p a n -> p (a n)")[:, 0:KEYS], AX.X, ALU.max, negate=True)\
                            .then_inc(s["negmax_ready"], 1)

                    def recip(t):
                        dve.wait_ge(s["exp_done"], ONE + TG * G + t + 1)
                        dve.reciprocal(stat[:, 2, t % 4:t % 4 + 1], stat[:, 1, t % 4:t % 4 + 1]).then_inc(s["recip_ready"], 1)

                    def tb(t):
                        c = t // 4
                        dve.wait_ge(s["tb_full"], ONE + TG * G + t + 1)
                        dve.wait_ge(s["pv_done"], ONE + CG * G + (c - 1 if c >= 2 else 0))
                        dve.tensor_copy(pT[:, c % 2, 4:8, (t % 4) * P:(t % 4 + 1) * P],
                                        psum[:, TB, :].rearrange("p (k n) -> p k n", k=4)).then_inc(s["tb_evac"], 1)

                    def norm(c):
                        own = 4 * (c % 2)
                        dve.wait_ge(s["pv_done"], ONE + CG * G + c + 1)
                        dve.wait_ge(s["o_hi_done"], ONE + CG * G + c)
                        recs = pT[:, c % 2, own:own + 4, :].rearrange("p k (i n) -> p (k i) n", i=4)[:, 0:16:5, :]
                        dve.tensor_tensor(o_f[:].rearrange("p (i n) -> p i n", i=4),
                                          psum[:, O, :].rearrange("p (i n) -> p i n", i=4), recs, ALU.mult)\
                            .then_inc(s["o_norm"], 1)

                    def o_lo(c):
                        j, half = c // 2, c % 2
                        dve.wait_ge(s["o_hi_done"], ONE + CG * G + c + 1)
                        sl = (slice(None), j % 2, slice(512 * half, 512 * half + 512))
                        dve.tensor_tensor(oT_lo[sl], o_f[:], oT_hi[sl].bitcast(F), ALU.subtract).then_inc(s["o_lo_done"], 1)

                    def add_out(pair, tt):
                        dve.wait_ge(s["acc_zero"], b + 1)
                        dve.wait_ge(s["oproj_psum"], ONE + 2 * NT * G + NT * pair + tt + 1)
                        bk = M if pair == 0 or tt % 2 == 0 else O
                        dve.tensor_tensor(acc[:, tt, :], psum[:, bk, :], acc[:, tt, :], ALU.add)\
                            .then_inc(s["oproj_evac"], 1)

                    for t in range(TG):
                        negmax(t)
                        if t >= 1:
                            recip(t - 1)
                        pp = pv_parts(t)
                        if pp is not None and pp[1] == 3:
                            norm(pp[0])
                        if 22 <= t < 22 + NT:
                            add_out(0, t - 22)
                        if t in ropes:
                            n, kind = ropes[t]
                            rope(5 * G + 1 + n, k_f if kind == "k" else q_f)
                        if t in los:
                            q_lo(GQ * G + los[t], los[t])
                        if t >= 2:
                            tb(t - 2)
                        if pp is not None and pp[1] == 3:
                            o_lo(pp[0])
                    recip(TG - 1)
                    tb(TG - 2)
                    norm(6)
                    tb(TG - 1)
                    o_lo(6)
                    if prefetch:
                        k_lo(G + 1)
                    dve.drain()
                    norm(7)
                    add_out(1, 0)
                    o_lo(7)
                    if prefetch:
                        rope(5 * G + 1 + 5, q_f)
                    for tt in range(1, NT):
                        add_out(1, tt)
                        if tt == 2 and prefetch:
                            q_lo(GQ * (G + 1), 0)

                rope(5 * G0, k_f)
                k_lo(G0)
                rope(5 * G0 + 1, q_f)
                q_lo(GQ * G0, 0)
                with dve.Fori(0, KV0 - 1) as g:
                    group(G0 + g, True)
                group(G0 + KV0 - 1, False)

                dve.drain()
                dve.wait_ge(s["gx_loaded"], 16 * (b + 1))
                dve.scalar_tensor_tensor(flat(acc), flat(acc), 0.5, flat(gx), ALU.mult, ALU.mult)
                dve.drain()
                dve.wait_ge(s["xx_loaded"], 16 * (b + 1))
                dve.tensor_tensor(acc[:], acc[:], q1[:], ALU.add)
                dve.drain()
                for t in range(NT):
                    dve.bn_stats(st1[:, t, :], acc[:, t, :])
                dve.drain()
                for t in range(NT):
                    dve.bn_aggr(mv1[:, t, :], st1[:, t, :])
                dve.drain()
                dve.tensor_scalar(rs1[:], mv1[:, :, 1], LN_EPS, None, ALU.add).then_inc(s["x1_stats"], 1)
                dve.wait_ge(s["w1_hi_done"], b + 1)
                dve.tensor_tensor(w1_lo[:], w1_f[:], w1_hi[:].bitcast(F), ALU.subtract).then_inc(s["w1_lo_done"], 1)
                dve.wait_ge(s["x1_rstd"], b + 1)

                def qkv_out(u):
                    dve.wait_ge(s["qkv_psum"], NT * b + u + 1)
                    dve.wait_ge(s["qkv_evac"], ONE + NT * b + u)
                    both = psum[:, 2 + 2 * (u % 2):4 + 2 * (u % 2), :].rearrange("p a n -> p (a n)")
                    nh = QK1 // D1
                    qk = both[:, 0:QK1].rearrange("p (h k d) -> p h k d", k=2, d=D1 // 2)
                    tab = lambda lo, n: cs1[:, u, lo:lo + n].unsqueeze(1).broadcast_to([P, nh, n])
                    rbv = rb[:].rearrange("p (h k d) -> p h k d", k=2, d=D1 // 2)
                    dve.tensor_tensor(ra[:].rearrange("p (h d) -> p h d", d=D1),
                                      both[:, 0:QK1].rearrange("p (h d) -> p h d", d=D1), tab(0, D1), ALU.mult)
                    dve.tensor_tensor(rbv[:, :, 0, :], qk[:, :, 1, :], tab(D1, D1 // 2), ALU.mult)
                    dve.tensor_tensor(rbv[:, :, 1, :], qk[:, :, 0, :], tab(D1 + D1 // 2, D1 // 2), ALU.mult)
                    dve.tensor_copy(v1[:, u, :], both[:, QK1:W1N])
                    dve.drain()
                    dve.tensor_tensor(q1[:, u, :], ra[:, 0:E], rb[:, 0:E], ALU.add)
                    dve.tensor_tensor(k1[:, u, :], ra[:, E:QK1], rb[:, E:QK1], ALU.add).then_inc(s["qkv_evac"], 1)
                    dve.wait_ge(s["ffn_psum"], NT * b + u + 1)
                    dve.tensor_tensor(g_lin[:, u % 2, :], psum[:, 6 + u % 2, :], bias_b[:], ALU.add).then_inc(s["ffn_lin"], 1)

                def silu(u):
                    dve.wait_ge(s["ffn_exp"], NT * b + u + 1)
                    dve.scalar_tensor_tensor(g1[:, u, :], g_exp[:, u % 2, :], 1.0, g_lin[:, u % 2, :],
                                             ALU.add, ALU.mult).then_inc(s["ffn_done"], 1)

                for t in range(NT + 2):
                    if t < NT:
                        dve.tensor_scalar(gx[:, t, :], acc[:, t, :], mv1[:, t, 0:1], rs1[:, t:t + 1],
                                          ALU.subtract, ALU.mult).then_inc(s["xn_ready"], 1)
                        lo_of(t, 2 * NT * b + NT)
                    if 1 <= t <= NT:
                        qkv_out(t - 1)
                    if t >= 2:
                        silu(t - 2)
                dve.drain()

                QM, KM, X, Y = 0, 2, 5, 6

                def stack_evac(dst, half, x):
                    dve.wait_ge(s["qt_psum"], ONE + x + 1)
                    dve.tensor_copy(dst[0:ST1, 512 * half:512 * half + 512], psum[0:ST1, X, :]).then_inc(s["qt_evac"], 1)

                def maximum(h, c):
                    i, k0, w = q_chunks()[c]
                    dve.wait_ge(s["qm_psum"], ONE + CH * h + c + 1)
                    dve.tensor_reduce(nm1[:, k0 // 512, i:i + 1], psum[:, QM + c % 2, 0:w], AX.X, ALU.max, negate=True)\
                        .then_inc(s["qm_max"], 1)

                def max_rows(j, h):
                    rows = q_st[:, (j // GQ) % 2, :, j % GQ, 4 * D1:ST1]
                    dve.drain()
                    dve.tensor_tensor(nm1[:, 0, 4:NT], nm1[:, 0, 4:NT], nm1[:, 1, 4:NT], ALU.min)
                    dve.drain()
                    dve.tensor_copy(rows[:, :, 0], nm1[:, 0, :])
                    dve.drain()
                    dve.tensor_tensor(rows[:, :, 1], nm1[:, 0, :], rows[:, :, 0].bitcast(F), ALU.subtract)\
                        .then_inc(s["nm_ready"], 1)

                def divide_half(N, n, half):
                    cols = slice(512 * half, 512 * half + 512)
                    dve.reciprocal(sumT[:, cols], sumT[:, cols])
                    dve.drain()
                    dve.tensor_tensor(ctxT[:, n, cols], ctxT[:, n, cols], sumT[:, cols], ALU.mult).then_inc(s["ctx_ready"], 1)

                def pair(N, n, first, prefetch):
                    for j in range(PH):
                        h = PH * N + j
                        turns = x_turns(j, prefetch)
                        for c in range(CH):
                            if "T2" in turns:
                                maximum(h + 1, c)
                            if "T1" in turns and c in (3, 7):
                                stack_evac(qTa[:, (j + 2) % 2], c // 4, XP * N + x_at(j, "T1", prefetch) + c // 4)
                        if "T2" in turns:
                            max_rows(j + 1, h + 1)
                        if "K" in turns:
                            stack_evac(kT1[:, (j // GQ + 1) % 2], 1, XP * N + x_at(j, "K", prefetch) + 1)
                        if not first and j == 0:
                            for k in range(2):
                                dve.wait_ge(s[f"o_moved{k}"], ONE + 16 * PH * N)
                        if not first and j < 2:
                            divide_half(N - 1, n - 1, j)

                N0 = NPAIR * b
                stack_evac(kT1[:, 0], 1, XP * N0 + 1)
                for j in range(2):
                    for half in range(2):
                        stack_evac(qTa[:, j], half, XP * N0 + 2 + 2 * j + half)
                for c in range(CH):
                    maximum(PH * N0, c)
                max_rows(0, PH * N0)
                pair(N0, 0, True, True)
                with dve.Fori(1, NPAIR - 1) as n:
                    pair(N0 + n, n, False, True)
                pair(N0 + NPAIR - 1, NPAIR - 1, False, False)
                for k in range(2):
                    dve.wait_ge(s[f"o_moved{k}"], ONE + 16 * PH * (N0 + NPAIR))
                for half in range(2):
                    divide_half(N0 + NPAIR - 1, NPAIR - 1, half)
                for t in range(NT):
                    dve.wait_ge(s["y_psum"], NT * b + t + 1)
                    if t >= 2:
                        dve.wait_ge(s[f"y_stored{t % 2}"], ONE + 8 * NT * b + 16 * (t // 2))
                    dve.scalar_tensor_tensor(y_sb[:, t % 2, :], psum[:, t % 4, :], 0.5, g1[:, t, :],
                                             ALU.mult, ALU.mult)
                    dve.drain()
                    dve.tensor_tensor(y_sb[:, t % 2, :], y_sb[:, t % 2, :], acc[:, t, :], ALU.add).then_inc(s["y_ready"], 1)


def tables():
    t = np.arange(S, dtype=np.float32)
    inv0 = (np.float32(1.0) / np.float32(10000.0) ** (np.arange(0, D0, 2, dtype=np.float32) / np.float32(D0))).astype(np.float32)
    f0 = (t[:, None] * inv0[None, :]).astype(np.float32).astype(np.float64)
    r0 = float(D0) ** -0.25
    cosT = np.concatenate([np.cos(f0), np.cos(f0)], 1).T * r0
    sinT = np.concatenate([-np.sin(f0), np.sin(f0)], 1).T * r0
    inv1 = (np.float32(1.0) / np.float32(500000.0) ** (np.arange(0, D1, 2, dtype=np.float32) / np.float32(D1))).astype(np.float32)
    f1 = (t[:, None] * inv1[None, :]).astype(np.float32).astype(np.float64)
    r1 = float(D1) ** -0.25
    cs1 = np.concatenate([np.cos(f1), np.cos(f1), -np.sin(f1), np.sin(f1)], 1) * r1
    cs1 = cs1.reshape(NT, P, 2 * D1).transpose(1, 0, 2)
    return {k: np.ascontiguousarray(v, dtype=np.float32) for k, v in (("cosT", cosT), ("sinT", sinT), ("cs1", cs1))}


def padded(w, rows, cols):
    o = np.zeros((rows, cols), np.float32)
    o[:w.shape[0], :w.shape[1]] = w
    return o


def chunked(wT):
    return wT.reshape(EC, P, -1).transpose(1, 0, 2)


def layouts(i):
    heads = lambda w, n: w.reshape(n, D0, EC, P).transpose(0, 3, 2, 1).reshape(n, P, EC * D0)
    row = lambda v: np.asarray(v, np.float32).reshape(1, -1)
    er = lambda v: np.repeat(v, 16).reshape(2, P).T
    scal = np.zeros((1, 4), np.float32)
    scal[0, 0], scal[0, 1], scal[0, 2] = i["L0_ffn_bu2"][0], i["L0_ffn_gate_w1"], i["L0_ffn_gate_bias"]
    wa = np.zeros((E, 2 * P), np.float32)
    wa[:, 0:P] = i["L0_ffn_Wu1"].T
    wa[:, P:P + BOT] = i["L0_ffn_Wq"].T
    x = i["L0_attn_hidden_states"]
    d = {
        "x": x.reshape(B * S, E), "x3": x,
        "wq": heads(i["L0_attn_Wq"], H0), "wk": heads(i["L0_attn_Wk"], KV0), "wv": heads(i["L0_attn_Wv"], KV0),
        "wo": i["L0_attn_Wo"].T.reshape(H0, D0, E),
        "wa": chunked(wa),
        "keysT": padded(i["L0_ffn_aux_keys"].T, P, P), "wr": padded(i["L0_ffn_Wr"], P, P),
        "wrT": padded(i["L0_ffn_Wr"].T, P, P),
        "avT": chunked(i["L0_ffn_aux_values"].T), "wvdT": chunked(padded(i["L0_ffn_Wvd"].T, E, P)),
        "wvuT": padded(i["L0_ffn_Wvu"].T, P, E),
        "bu1": row(i["L0_ffn_bu1"]), "wu2": row(i["L0_ffn_Wu2"]), "scal": scal, "log_rel": row(i["L0_ffn_log_rel"]),
        "w_qkv1": chunked(np.concatenate([i["L1_attn_Wq"], i["L1_attn_Wk"], i["L1_attn_Wv"]], 1)),
        "wo1": chunked(i["L1_attn_Wo"]),
        "w_ffn1": chunked(i["L1_ffn_W"].T), "bias1": row(i["L1_ffn_bias"]),
        "lora_a": i["L1_ffn_A"].reshape(2, P, E).transpose(1, 0, 2),
        "lora_b": i["L1_ffn_Bf"].transpose(0, 2, 1).reshape(2, P, E).transpose(1, 0, 2),
        "mix": np.stack([er(i["L1_ffn_coeffs"]), er(i["L1_ffn_scales"])], 2),
    }
    return {k: np.ascontiguousarray(v) for k, v in {**d, **tables()}.items()}


def kernel(**inputs):
    import concourse.bacc as bacc
    from concourse.bass_utils import run_bass_kernel_spmd

    nc = bacc.Bacc("TRN2", target_bir_lowering=False, num_devices=1)
    arrays, aps = {}, {}
    for name, v in layouts({k: np.asarray(v) for k, v in inputs.items()}).items():
        arrays[f"in_{name}"] = v
        aps[name] = nc.dram_tensor(f"in_{name}", v.shape, mybir.dt.from_np(v.dtype), kind="ExternalInput").ap()
    out = nc.dram_tensor("out_0", [B, S, E], F, kind="ExternalOutput").ap()
    aps["out3"] = out
    build(nc, aps, out)
    r = run_bass_kernel_spmd(nc, [arrays], core_ids=[0])
    return r.results[0]["out_0"]
```

```python
from contextlib import ExitStack

import numpy as np
import concourse.bass as bass
from concourse import mybir

F = mybir.dt.float32
R = mybir.dt.float32r
BF = mybir.dt.bfloat16
ALU = mybir.AluOpType
ACT = mybir.ActivationFunctionType
AX = mybir.AxisListType

P = 128
B, S, E = 2, 1024, 512
NT = S // P
EC = E // P
H0, KV0, D0 = 32, 8, 128
GQ = H0 // KV0
KV1, D1 = 8, 16
NSLOT, BOT, RDIM, VB, TOPK = 128, 64, 48, 32, 8
LN_EPS = 1e-5
NEG = -1e30
KEYS = S - P
TG = GQ * NT
CG = TG // 2
CQ = 2 * P
GELU_C, GELU_A = 0.7978845608028654, 0.044715
W1N = E + 2 * KV1 * D1
QK1 = W1N - KV1 * D1
ST1 = 4 * D1 + 2
ONE = 1
VS = 48
SUM_AT = 32


def build(nc, a, out):
    ctx = ExitStack()
    with ctx:
        def sbuf(stack, name, shape, dt=F):
            return stack.enter_context(nc.sbuf_tensor(name, shape, dt))

        def sem(name):
            return ctx.enter_context(nc.semaphore(name))

        ident = sbuf(ctx, "ident", [P, P])
        ident_r = sbuf(ctx, "ident_r", [P, P], R)
        ident_b = sbuf(ctx, "ident_b", [P, P], BF)
        mask_ge = sbuf(ctx, "mask_ge", [P, P], BF)
        mask_le = sbuf(ctx, "mask_le", [P, P], BF)
        bu1_b = sbuf(ctx, "bu1_b", [P, P])
        wu2_b = sbuf(ctx, "wu2_b", [P, P])
        scal_b = sbuf(ctx, "scal_b", [P, 4])
        row64 = sbuf(ctx, "row64", [P, 1])
        minus_half = sbuf(ctx, "minus_half", [P, NT])
        ones = sbuf(ctx, "ones", [P, NT])
        router = sbuf(ctx, "router", [P, 2 * P])
        auxvu = sbuf(ctx, "auxvu", [P, E])
        mv0 = sbuf(ctx, "mv0", [P, B * NT, 2])
        rstd0 = sbuf(ctx, "rstd0", [P, B * NT])
        half_norm = sbuf(ctx, "half_norm", [P, B * NT])
        cs1 = sbuf(ctx, "cs1", [P, NT, 2 * D1])
        xT_hi = sbuf(ctx, "xT_hi", [P, EC, S], R)
        xT_lo = sbuf(ctx, "xT_lo", [P, EC, S], R)
        acc = sbuf(ctx, "acc", [P, NT, E])
        psum = ctx.enter_context(nc.psum_tensor("psum", [P, 8, 512], F))
        g0_dram = nc.dram_tensor("g0_scratch", [B * S, E], F, kind="Internal").ap()
        weff_dram = nc.dram_tensor("weff_scratch", [P, EC * E], F, kind="Internal").ap()

        pre = ExitStack()
        with pre:
            pr_keysT = sbuf(pre, "pr_keysT", [P, P])
            pr_wr = sbuf(pre, "pr_wr", [P, P])
            pr_wrT = sbuf(pre, "pr_wrT", [P, P])
            pr_rkT = sbuf(pre, "pr_rkT", [P, P])
            pr_avT = sbuf(pre, "pr_avT", [P, EC, P])
            pr_wvdT = sbuf(pre, "pr_wvdT", [P, EC, P])
            pr_wvuT = sbuf(pre, "pr_wvuT", [P, E])
            pr_avd = sbuf(pre, "pr_avd", [P, P])
            pr_a = sbuf(pre, "pr_a", [P, 2, E])
            pr_b = sbuf(pre, "pr_b", [P, 2, E])
            pr_w = sbuf(pre, "pr_w", [P, EC, E])
            pr_cs = sbuf(pre, "pr_cs", [P, 2, 2])
            pr_mix = sbuf(pre, "pr_mix", [P, 2])
            pr_x = sbuf(pre, "pr_x", [P, B * NT, E])
            pr_st = sbuf(pre, "pr_st", [P, B * NT, 6])
            pr_sm = sbuf(pre, "pr_sm", [P, 8 * B * NT])
            pr_mh = sbuf(pre, "pr_mh", [P, B * NT])
            pr_ones = sbuf(pre, "pr_ones", [P, P])

        phx = ExitStack()
        with phx:
            cosT = sbuf(phx, "cosT", [P, S])
            sinT = sbuf(phx, "sinT", [P, S])
            raw = sbuf(phx, "raw", [P, S])
            swp = sbuf(phx, "swp", [P, S])
            q_f = sbuf(phx, "q_f", [P, S])
            k_f = sbuf(phx, "k_f", [P, S])
            wq_hi = sbuf(phx, "wq_hi", [P, 2, 512], R)
            wq_lo = sbuf(phx, "wq_lo", [P, 2, 512], R)
            wk_hi = sbuf(phx, "wk_hi", [P, 512], R)
            wk_lo = sbuf(phx, "wk_lo", [P, 512], R)
            wv_hi = sbuf(phx, "wv_hi", [P, 512], R)
            wv_lo = sbuf(phx, "wv_lo", [P, 512], R)
            w_st = sbuf(phx, "w_st", [P, 2, 512])
            kT_hi = sbuf(phx, "kT_hi", [P, 2, KEYS], R)
            kT_lo = sbuf(phx, "kT_lo", [P, 2, KEYS], R)
            qT_hi = sbuf(phx, "qT_hi", [P, 2, S], R)
            qT_lo = sbuf(phx, "qT_lo", [P, 2, S], R)

            pha = ExitStack()
            with pha:
                wa_f = sbuf(pha, "wa_f", [P, EC, 2 * P])
                wa_hi = sbuf(pha, "wa_hi", [P, EC, 2 * P], R)
                wa_lo = sbuf(pha, "wa_lo", [P, EC, 2 * P], R)
                queryT = sbuf(pha, "queryT", [P, S])
                zb = sbuf(pha, "zb", [P, NT, P])
                zt = sbuf(pha, "zt", [P, NT, P])
                sc = sbuf(pha, "sc", [P, NT, P])
                rep = sbuf(pha, "rep", [P, NT, P])
                eT = sbuf(pha, "eT", [P, NT, P])
                top8 = sbuf(pha, "top8", [P, NT, TOPK])
                sma = sbuf(pha, "sma", [P, 12, NT])
                ex_a = sbuf(pha, "ex_a", [P, NT + 2, E])
                xn = sbuf(pha, "xn", [P, NT, E])

            phb = ExitStack()
            with phb:
                probs = sbuf(phb, "probs", [P, 3, KEYS])
                pT_hi = sbuf(phb, "pT_hi", [P, 2, NT, CQ], R)
                pT_lo = sbuf(phb, "pT_lo", [P, 2, NT, CQ], R)
                recs = sbuf(phb, "recs", [P, 2, CQ])
                v_hi = sbuf(phb, "v_hi", [P, NT, D0], R)
                v_lo = sbuf(phb, "v_lo", [P, NT, D0], R)
                o_f = sbuf(phb, "o_f", [P, CQ])
                stat = sbuf(phb, "stat", [P, 3, 4])
                oT_hi = sbuf(phb, "oT_hi", [P, 2, S], R)
                oT_lo = sbuf(phb, "oT_lo", [P, 2, S], R)
                wo_hi = sbuf(phb, "wo_hi", [P, 2, 512], R)
                wo_lo = sbuf(phb, "wo_lo", [P, 2, 512], R)

        phd = ExitStack()
        with phd:
            q1 = sbuf(phd, "q1", [P, NT, E])
            gx = sbuf(phd, "gx", [P, NT, E])
            k1 = sbuf(phd, "k1", [P, NT, KV1 * D1])
            v1 = sbuf(phd, "v1", [P, NT, KV1 * D1])
            bias_b = sbuf(phd, "bias_b", [P, E])
            q_st = sbuf(phd, "q_st", [P, 2, NT, GQ, ST1], R)
            k_st = sbuf(phd, "k_st", [P, 2, NT, ST1], R)
            v_st = sbuf(phd, "v_st", [P, 2, NT, VS])
            phc = ExitStack()
            with phc:
                w1_f = sbuf(phc, "w1_f", [P, EC, W1N + E])
                w1_hi = sbuf(phc, "w1_hi", [P, EC, W1N + E], R)
                w1_lo = sbuf(phc, "w1_lo", [P, EC, W1N + E], R)
                st1 = sbuf(phc, "st1", [P, NT, 6])
                mv1 = sbuf(phc, "mv1", [P, NT, 2])
                rs1 = sbuf(phc, "rs1", [P, NT])
                ra = sbuf(phc, "ra", [P, QK1])
                rb = sbuf(phc, "rb", [P, QK1])
                g_lin = sbuf(phc, "g_lin", [P, 2, E])
                g_exp = sbuf(phc, "g_exp", [P, 2, E])
            kT1 = sbuf(phd, "kT1", [P, 2, S], R)
            qTa = sbuf(phd, "qTa", [P, 2, S], R)
            qTb = sbuf(phd, "qTb", [P, 2, S], R)
            nm1 = sbuf(phd, "nm1", [P, 2, NT])
            o_st = sbuf(phd, "o_st", [VS, 2, S])
            ctxT = sbuf(phd, "ctxT", [P, EC, S])
            sumT = sbuf(phd, "sumT", [P, S])
            wo1 = sbuf(phd, "wo1", [P, EC, E])
            y_sb = sbuf(phd, "y_sb", [P, 2, E])
            pT1 = sbuf(phd, "pT1", [P, NT * (NT + 1) // 2 * P])

        s = {n: sem(n) for n in (
            "consts", "pro_loaded", "pro_x", "pro_mm", "pro_evac", "pro_act", "pro_stats", "pro_pow", "pro_weff",
            "x_loaded", "wa_loaded", "wa_hi_done", "wa_lo_done", "xn_ready", "xT_psum", "xT_hi_done", "xT_lo_done",
            "z_psum", "gelu_in", "gelu_exp", "query_psum", "query_done", "router_psum", "sc_done", "gate_in",
            "gate_exp", "att_in", "att_exp", "att_ready", "eT_psum", "eT_done", "aux_psum", "g0_lin", "g0_exp",
            "g0_ready", "g0_stored",
            "tabs_loaded", "w_loaded0", "w_loaded1", "w_hi_done", "w_ready", "prep_psum", "raw_ready", "swapped", "roped",
            "q_hi_done", "q_ready", "k_hi_done", "k_ready", "v_psum", "v_hi_done", "v_evac", "scores_ready", "negmax_ready", "exp_done", "recip_ready",
            "t_full", "t_hi_done", "t_evac", "pv_done", "o_norm", "o_hi_done", "o_lo_done",
            "oproj_psum", "oproj_evac", "acc_zero", "rope_mul",
            "gx_loaded", "x1_stats", "x1_rstd", "w1_loaded0", "w1_loaded1", "w1_hi_done", "w1_lo_done", "qkv_psum",
            "qkv_evac", "ffn_psum", "ffn_lin", "ffn_exp", "ffn_done", "xx_loaded",
            "wo1_loaded", "st_ready", "qt_psum", "qt_evac", "qm_psum", "qm_max", "nm_ready",
            "km_psum", "km_exp", "v1_ready", "pv1_psum", "pv1_evac", "o_moved0", "o_moved1", "ctx_ready", "y_psum", "y_ready", "y_stored0", "y_stored1",
        )}

        credited = {
            "sync": ("y_stored0", "y_stored1", "o_moved0", "o_moved1",),
            "vector": ("y_ready", "xT_lo_done", "t_evac", "v_evac", "o_norm", "oproj_evac", "qm_max", "ctx_ready", "qkv_evac", "ffn_lin", "g0_lin",),
            "scalar": ("raw_ready", "exp_done", "qt_evac", "km_exp", "pv1_evac", "o_hi_done",),
            "gpsimd": ("w_ready", "roped",),
            "tensor": ("pv_done", "scores_ready", "t_full", "oproj_psum", "qt_psum", "km_psum", "qm_psum", "pv1_psum",),
        }

        def give_credit(eng, name):
            for n in credited[name]:
                eng.sem_inc(s[n], ONE)

        def hilo(pe, dst, lhs, rhs, start=True, stop=True):
            (lh, ll), (rh, rl) = lhs, rhs
            pe.matmul(dst, ll, rh, start=start, stop=False)
            pe.matmul(dst, lh, rl, start=False, stop=False)
            return pe.matmul(dst, lh, rh, start=False, stop=stop)

        W_STEP = {1: ("q", 2), 5: ("o", 0), 7: ("k", 0), 9: ("o", 1), 11: ("q", 3), 13: ("q", 0), 15: ("v", 0),
                  22: ("q", 1), 30: ("o", 2), 31: ("o", 3)}
        V_STEPS = (1, 3)
        W_PRE = [("k", 0), ("q", 0), ("v", 0), ("q", 1)]

        def w_items(prefetch):
            return [(t, *W_STEP[t]) for t in sorted(W_STEP)
                    if prefetch or W_STEP[t][0] == "o" or W_STEP[t][1] > 1]

        def w_index(prefetch, kind, j):
            return [x[1:] for x in w_items(prefetch)].index((kind, j)) + 1

        def preps(prefetch):
            steps = [("q", 1, 0, 2), ("q", 2, 8, 10), ("k", 0, 13, 14), ("q", 3, 17, 19), ("q", 0, TG - 1, TG)]
            return [(n + 1, *x) for n, x in enumerate(x for x in steps if prefetch or x[1] > 0)]

        w_dst = {"q": (wq_hi, wq_lo), "k": (wk_hi, wk_lo), "v": (wv_hi, wv_lo), "o": (wo_hi, wo_lo)}

        def w_slot(kind, j):
            hi, lo = w_dst[kind]
            return (hi[:, j % 2, :], lo[:, j % 2, :]) if kind in "qo" else (hi[:], lo[:])

        O_STEP = 20

        def pv_parts(t):
            return ((t - 5) // 2, (t - 5) % 2) if t >= 5 else None

        def pv_keys(c):
            own = 2 * (c % (NT // 2))
            return [k for k in range(NT) if k not in (own, own + 1)] + [own, own + 1]

        PH, XL, XP = 2 * GQ, 8, 4 * 2 * GQ + 4
        NPAIR = KV1 // 2
        CH = NT + NT // 2

        def x_turns(j, prefetch):
            return [w for w, there in (("T1", prefetch or j + 2 < PH), ("K", j % GQ == 1 and (prefetch or j < GQ)),
                                       ("T2", prefetch or j + 1 < PH)) if there]

        def x_at(j, what, prefetch):
            return XL + 2 * (sum(len(x_turns(i, prefetch)) for i in range(j)) + x_turns(j, prefetch).index(what))

        def q_chunks():
            return [(i, k0, min(512, (i + 1) * P - k0)) for i in reversed(range(NT)) for k0 in range(0, (i + 1) * P, 512)]

        def k_chunks():
            return [(i, q0, min(512, S - q0)) for i in range(NT) for q0 in range(i * P, S, 512)]

        def pT1_cols(i, q0, w):
            at = (i * NT - i * (i - 1) // 2) * P + q0 - i * P
            return pT1[:, at:at + w]

        block = ctx.enter_context(nc.Block())

        @block.sync
        def _(sp):
            give_credit(sp, "sync")
            x_view = a["x"].rearrange("(t p) e -> p t e", p=P)
            sp.dma_start(pr_x[:], x_view).then_inc(s["pro_x"], 16)
            pro = [(pr_keysT[:], a["keysT"]), (pr_wr[:], a["wr"]), (pr_wrT[:], a["wrT"]),
                   (pr_avT[:], a["avT"]), (pr_wvdT[:], a["wvdT"]), (pr_wvuT[:], a["wvuT"]),
                   (pr_a[:], a["lora_a"]), (pr_b[:], a["lora_b"]), (pr_w[:], a["w_ffn1"]), (pr_cs[:], a["mix"]),
                   (cs1[:], a["cs1"]),
                   (bu1_b[:], a["bu1"].partition_broadcast(P)[:, 0, :]),
                   (wu2_b[:], a["wu2"].partition_broadcast(P)[:, 0, :]),
                   (scal_b[:], a["scal"].partition_broadcast(P)[:, 0, :])]
            for dst, src in pro:
                sp.dma_start(dst, src).then_inc(s["pro_loaded"], 16)
            sp.wait_ge(s["consts"], 1)
            sp.dma_start(router[BOT:BOT + 1, 0:P], a["log_rel"]).then_inc(s["pro_loaded"], 16)
            sp.dma_start(router[BOT:BOT + 1, P:2 * P], a["log_rel"]).then_inc(s["pro_loaded"], 16)
            sp.wait_ge(s["pro_evac"], 4 + EC)
            sp.dma_start(weff_dram, pr_w[:].rearrange("p c e -> p (c e)")).then_inc(s["pro_weff"], 16)
            sp.wait_ge(s["pro_weff"], 16)
            sp.wait_ge(s["pro_stats"], 5)
            with sp.Fori(0, B) as b:
                G0 = b * KV0
                for k in range(2):
                    sp.wait_ge(s[f"y_stored{k}"], ONE + 8 * NT * b)
                xb = a["x3"][b, :, :].rearrange("(t p) e -> p t e", p=P)
                w_src = {"q": a["wq"], "k": a["wk"], "v": a["wv"], "o": a["wo"]}

                def load_unit(kind, j, g, slot, busy_until):
                    src = w_src[kind]
                    n = GQ * g + j if kind in "qo" else g + j
                    if busy_until is not None:
                        sp.wait_ge(s["w_ready"], ONE + busy_until)
                    sp.dma_start(w_st[:, slot, :], src[n, :, :]).then_inc(s[f"w_loaded{slot}"], 16)

                def swap(p):
                    sp.wait_ge(s["raw_ready"], ONE + 2 * (p + 1))
                    sp.dma_start(swp[0:64, :], raw[64:128, :]).then_inc(s["swapped"], 16)
                    sp.dma_start(swp[64:128, :], raw[0:64, :]).then_inc(s["swapped"], 16)

                for i, (kind, j) in enumerate(W_PRE):
                    if i == 2:
                        sp.dma_start(cosT[:], a["cosT"]).then_inc(s["tabs_loaded"], 16)
                        sp.dma_start(sinT[:], a["sinT"]).then_inc(s["tabs_loaded"], 16)
                    load_unit(kind, j, 0, i % 2, 10 * G0 + max(i - 1, 0))
                swap(5 * G0)
                swap(5 * G0 + 1)
                sp.wait_ge(s["g0_ready"], b + 1)
                g0b = g0_dram.rearrange("(b t p) e -> b p t e", b=B, p=P)[b, :, :, :]
                sp.dma_start(g0b, xn[:]).then_inc(s["g0_stored"], 16)


                def group(G, g, prefetch):
                    at = [0] + [t for t, _, _ in w_items(prefetch)]
                    items = {at[i]: (i, k, j) for i, (_, k, j) in enumerate(w_items(prefetch))}
                    swaps = {t2: n for n, _, _, _, t2 in preps(prefetch)}
                    for t in range(TG):
                        if t in items:
                            i, kind, j = items[t]
                            nxt = kind in "kv" or (kind == "q" and j < 2)
                            u = 10 * G + 4 + i
                            load_unit(kind, j, g + 1 if nxt else g, i % 2, u - 1)
                        if t in swaps:
                            swap(5 * G + 1 + swaps[t])
                    if TG in swaps:
                        swap(5 * G + 1 + swaps[TG])
                with sp.Fori(0, KV0 - 1) as g:
                    group(G0 + g, g, True)
                group(G0 + KV0 - 1, KV0 - 1, False)

                sp.wait_ge(s["q_ready"], GQ * KV0 * (b + 1))
                sp.dma_start(q1[:], xb).then_inc(s["xx_loaded"], 16)
                sp.wait_ge(s["g0_stored"], 16 * (b + 1))
                sp.dma_start(gx[:], g0b).then_inc(s["gx_loaded"], 16)
                sp.wait_ge(s["oproj_evac"], ONE + 2 * NT * KV0 * (b + 1))
                for h in range(2):
                    cs = slice(2 * h, 2 * h + 2)
                    sp.dma_start(w1_f[:, cs, 0:W1N], a["w_qkv1"][:, cs, :]).then_inc(s[f"w1_loaded{h}"], 16)
                    sp.dma_start(w1_f[:, cs, W1N:], weff_dram.rearrange("p (c e) -> p c e", c=EC)[:, cs, :])\
                        .then_inc(s[f"w1_loaded{h}"], 16)
                sp.dma_start(bias_b[:], a["bias1"].partition_broadcast(P)[:, 0, :]).then_inc(s["w1_loaded1"], 16)
                sp.wait_ge(s["ffn_done"], NT * (b + 1))
                sp.dma_start(wo1[:], a["wo1"]).then_inc(s["wo1_loaded"], 16)
                with sp.Fori(0, NPAIR) as n:
                    N = NPAIR * b + n
                    for j in range(PH):
                        sp.wait_ge(s["pv1_evac"], ONE + 2 * (PH * N + j + 1))
                        rows = slice(j * D1, (j + 1) * D1)
                        sp.dma_start(ctxT[rows, n, :], o_st[0:D1, j % 2, :]).then_inc(s[f"o_moved{j % 2}"], 16)
                        if j == 0:
                            sp.wait_ge(s["ctx_ready"], ONE + 2 * N)
                        sp.dma_start(sumT[rows, :], o_st[SUM_AT:SUM_AT + D1, j % 2, :]).then_inc(s[f"o_moved{j % 2}"], 16)
                for t in range(NT):
                    sp.wait_ge(s["y_ready"], ONE + NT * b + t + 1)
                    sp.dma_start(a["out3"][b, :, :].rearrange("(t p) e -> t p e", p=P)[t, :, :],
                                 y_sb[:, t % 2, :]).then_inc(s[f"y_stored{t % 2}"], 16)
            for k in range(2):
                sp.wait_ge(s[f"y_stored{k}"], ONE + 8 * NT * B)
            sp.wait_ge(s["g0_stored"], 16 * B)

        @block.gpsimd
        def _(pool):
            give_credit(pool, "gpsimd")
            pool.memset(router[:], 0.0).then_inc(s["consts"], 1)
            for m in (ident, mask_ge, mask_le, row64, ident_b):
                pool.memset(m[:], 0.0)
            pool.memset(minus_half[:], -0.5)
            pool.memset(pr_ones[:], 1.0)
            pool.memset(ones[:], 1.0)
            pool.drain()
            for m in (ident, ident_b):
                pool.affine_select(out=m[:], in_=m[:], compare_op=ALU.not_equal, fill=1.0, base=0,
                                   pattern=[[-1, P]], channel_multiplier=1)
            pool.affine_select(out=mask_ge[:], in_=mask_ge[:], compare_op=ALU.is_ge, fill=NEG, base=0,
                               pattern=[[1, P]], channel_multiplier=-1)
            pool.affine_select(out=mask_le[:], in_=mask_le[:], compare_op=ALU.is_ge, fill=NEG, base=0,
                               pattern=[[-1, P]], channel_multiplier=1)
            pool.affine_select(out=row64[:], in_=row64[:], compare_op=ALU.not_equal, fill=1.0, base=-BOT,
                               pattern=[[0, 1]], channel_multiplier=1)
            pool.drain()
            pool.memset(pr_mh[:], -0.5).then_inc(s["consts"], 1)
            pool.wait_ge(s["consts"], 2)
            pool.wait_ge(s["pro_stats"], 1)
            pool.tensor_tensor(rstd0[:], pr_sm[:, 0:B * NT], pr_mh[:], ALU.pow).then_inc(s["pro_pow"], 1)

            with pool.Fori(0, B) as b:
                G0 = b * KV0

                def split_lo(u, kind, j):
                    hi, lo = w_slot(kind, j)
                    slot = u[1] % 2
                    pool.wait_ge(s["w_hi_done"], u[0] + 1)
                    pool.tensor_tensor(lo, w_st[:, slot, :], hi.bitcast(F), ALU.subtract).then_inc(s["w_ready"], 1)

                def rope(p, dst, dst_free):
                    pool.wait_ge(s["raw_ready"], ONE + 2 * (p + 1))
                    if dst_free is not None:
                        pool.wait_ge(*dst_free)
                    pool.tensor_tensor(dst[:], raw[:], cosT[:], ALU.mult)
                    pool.wait_ge(s["swapped"], 32 * (p + 1))
                    pool.tensor_tensor(swp[:], swp[:], sinT[:], ALU.mult).then_inc(s["rope_mul"], 1)
                    pool.wait_ge(s["rope_mul"], p + 1)
                    pool.tensor_tensor(dst[:], dst[:], swp[:], ALU.add).then_inc(s["roped"], 1)

                def q_rest(n, j):
                    pool.wait_ge(s["q_hi_done"], n + 1)
                    pool.tensor_tensor(qT_lo[:, j % 2, :], q_f[:], qT_hi[:, j % 2, :].bitcast(F), ALU.subtract)\
                        .then_inc(s["q_ready"], 1)

                for i, (kind, j) in enumerate(W_PRE):
                    split_lo((10 * G0 + i, i), kind, j)
                pool.wait_ge(s["tabs_loaded"], 32 * (b + 1))
                rope(5 * G0, k_f, None)
                rope(5 * G0 + 1, q_f, None)
                q_rest(GQ * G0, 0)

                def group(G, prefetch):
                    items = {t: (i, k, j) for i, (t, k, j) in enumerate(w_items(prefetch))}
                    ropes = {t2: (n, kind, j) for n, kind, j, _, t2 in preps(prefetch)}
                    for t in range(TG + 3):
                        for n, kind, j, _, t2 in preps(prefetch):
                            if kind == "q" and t == t2 + 2:
                                q_rest(GQ * G + (j if j > 0 else GQ), j)
                        if t in items:
                            i, kind, j = items[t]
                            split_lo((10 * G + 4 + i, i), kind, j)
                        if t in ropes:
                            n, kind, j = ropes[t]
                            if kind == "k":
                                rope(5 * G + 1 + n, k_f, (s["k_ready"], G + 1))
                            else:
                                rope(5 * G + 1 + n, q_f, (s["q_ready"], GQ * G + (j if j > 0 else GQ)))
                with pool.Fori(0, KV0 - 1) as g:
                    group(G0 + g, True)
                group(G0 + KV0 - 1, False)

                for h in range(2):
                    pool.wait_ge(s["x1_stats"], 2 * b + h + 1)
                    pool.tensor_tensor(rs1[:, 4 * h:4 * h + 4], rs1[:, 4 * h:4 * h + 4], minus_half[:, 0:4], ALU.pow)\
                        .then_inc(s["x1_rstd"], 1)
                    if h == 0:
                        pool.wait_ge(s["w1_hi_done"], 2 * b + 1)
                        pool.tensor_tensor(w1_lo[:, 0:2, :], w1_f[:, 0:2, :], w1_hi[:, 0:2, :].bitcast(F), ALU.subtract)\
                            .then_inc(s["w1_lo_done"], 1)

                def stacks(g, par, ts, last_tiles):
                    n = ts.stop - ts.start
                    k_src = k1[:].rearrange("p t (g d) -> p t g d", d=D1)[:, ts, g, :]
                    q_src = q1[:].rearrange("p t (g j d) -> p t g j d", j=GQ, d=D1)[:, ts, g, :, :]
                    kd, qd = k_st[:, par, ts, :], q_st[:, par, ts, :, :]
                    one_b = ones[:, 0:n].unsqueeze(2).broadcast_to([P, n, D1])
                    for o in (0, 1):
                        pool.tensor_tensor(kd[:, :, o * D1:(o + 1) * D1], k_src, one_b, ALU.mult)
                    for o in (0, 2):
                        pool.tensor_copy(qd[:, :, :, o * D1:(o + 1) * D1], q_src)
                    pool.memset(kd[:, :, 4 * D1:ST1].bitcast(F), 1.0)
                    pool.memset(qd[:, :, :, 4 * D1:ST1].bitcast(F), 0.0)
                    pool.drain()
                    for o in (2, 3):
                        last = pool.tensor_tensor(kd[:, :, o * D1:(o + 1) * D1], k_src, kd[:, :, 0:D1].bitcast(F),
                                                  ALU.subtract)
                    if last_tiles:
                        last.then_inc(s["st_ready"], 1)
                    for o in (1, 3):
                        last = pool.tensor_tensor(qd[:, :, :, o * D1:(o + 1) * D1], q_src,
                                                  qd[:, :, :, 0:D1].bitcast(F), ALU.subtract)
                    if last_tiles:
                        last.then_inc(s["st_ready"], 1)

                def values(g, par):
                    pool.tensor_tensor(v_st[:, par, :, 0:D1], v1[:].rearrange("p t (g d) -> p t g d", d=D1)[:, :, g, :],
                                       ones[:].unsqueeze(2).broadcast_to([P, NT, D1]), ALU.mult).then_inc(s["v1_ready"], 1)

                for t in range(NT):
                    pool.wait_ge(s["qkv_evac"], ONE + NT * b + t + 1)
                    for par in range(2):
                        stacks(par, par, slice(t, t + 1), t == NT - 1)
                    if t == 0:
                        pool.memset(v_st[:, :, :, D1:SUM_AT], 0.0)
                        pool.memset(v_st[:, :, :, SUM_AT:SUM_AT + D1], 1.0)
                for par in range(2):
                    values(par, par)

                with pool.Fori(0, NPAIR - 1) as n:
                    for par in range(2):
                        pool.wait_ge(s["qt_psum"], ONE + XP * (NPAIR * b + n) + x_at(GQ * par + 2, "T2", True) + 2)
                        stacks(2 * n + 2 + par, par, slice(0, NT), True)
                    values(2 * n + 2, 0)
                    pool.wait_ge(s["pv1_psum"], ONE + 2 * PH * (NPAIR * b + n + 1))
                    values(2 * n + 3, 1)

        @block.tensor
        def _(pe):
            give_credit(pe, "tensor")
            bank = lambda i: psum[:, i, :]
            pe.wait_ge(s["consts"], 2)
            pe.wait_ge(s["pro_loaded"], 16 * 16)
            pe.matmul(bank(0)[:, 0:P], pr_wrT[:], pr_keysT[:], start=True, stop=True).then_inc(s["pro_mm"], 1)
            for c in range(EC):
                last = pe.matmul(bank(1)[:, 0:P], pr_wvdT[:, c, :], pr_avT[:, c, :], start=(c == 0), stop=(c == EC - 1))
            last.then_inc(s["pro_mm"], 1)
            pe.wait_ge(s["pro_evac"], 2)
            pe.matmul(bank(2)[:, 0:P], pr_wr[:], pr_rkT[:], start=True, stop=True).then_inc(s["pro_mm"], 1)
            pe.matmul(bank(3), pr_avd[:], pr_wvuT[:], start=True, stop=True).then_inc(s["pro_mm"], 1)
            pe.wait_ge(s["pro_act"], 1)
            for c in range(EC):
                for k in range(2):
                    last = pe.matmul(bank(4 + c), pr_a[:, k, c * P:(c + 1) * P], pr_b[:, k, :],
                                     start=(k == 0), stop=(k == 1))
                last.then_inc(s["pro_mm"], 1)
            pe.wait_ge(s["pro_act"], 3)
            pe.wait_ge(s["pro_evac"], 4)
            pe.matmul(bank(2)[:, 0:2], pr_ones[:], pr_sm[:, 6 * B * NT:6 * B * NT + 2], start=True, stop=True)\
                .then_inc(s["pro_mm"], 1)

            with pe.Fori(0, B) as b:
                G0 = b * KV0
                pe.wait_ge(s["y_ready"], ONE + NT * b)

                def transposed(t, src, base):
                    pe.wait_ge(s["xn_ready"], base + t + 1)
                    pe.wait_ge(s["xT_lo_done"], ONE + base + max(t - 1, 0))
                    for c in range(EC):
                        last = pe.matmul(bank(t % 2)[:, c * P:(c + 1) * P], src[:, t, c * P:(c + 1) * P], ident[:],
                                         start=True, stop=True, is_transpose=True)
                    last.then_inc(s["xT_psum"], 1)

                def xT(c, lo, hi):
                    return (xT_hi[:, c, lo:hi], xT_lo[:, c, lo:hi])

                def prep_lump(bk, half, w):
                    for c in range(EC):
                        last = hilo(pe, bank(bk), (w[0][:, c * P:(c + 1) * P], w[1][:, c * P:(c + 1) * P]),
                                    xT(c, 512 * half, 512 * half + 512), c == 0, c == EC - 1)
                    last.then_inc(s["prep_psum"], 1)

                pe.wait_ge(s["wa_lo_done"], b + 1)
                for t in range(NT + 1):
                    if t < NT:
                        transposed(t, xn, 2 * NT * b)
                    if t >= 1:
                        u = t - 1
                        pe.wait_ge(s["xT_lo_done"], ONE + 2 * NT * b + u + 1)
                        for c in range(EC):
                            last = hilo(pe, psum[:, 2 + u // 4, (u % 4) * P:(u % 4 + 1) * P], xT(c, u * P, (u + 1) * P),
                                        (wa_hi[:, c, 0:P], wa_lo[:, c, 0:P]), c == 0, c == EC - 1)
                        last.then_inc(s["z_psum"], 1)
                for h in range(2):
                    for c in range(EC):
                        last = hilo(pe, bank(4 + h), (wa_hi[:, c, P:2 * P], wa_lo[:, c, P:2 * P]),
                                    xT(c, 512 * h, 512 * h + 512), c == 0, c == EC - 1)
                    last.then_inc(s["query_psum"], 1)
                rbank = (0, 1, 6, 7)
                pe.wait_ge(s["query_done"], 2 * (b + 1))
                for t in range(NT):
                    last = pe.matmul(psum[:, rbank[t // 2], (t % 2) * 256:(t % 2) * 256 + 256], queryT[:, t * P:(t + 1) * P],
                                     router[:], start=True, stop=True)
                last.then_inc(s["router_psum"], 1)
                pe.wait_ge(s["gelu_in"], b + 1)
                for i, kind in enumerate(("k", "q")):
                    pe.wait_ge(s["w_ready"], ONE + 10 * G0 + i + 1)
                    for half in range(2):
                        if i == 1:
                            pe.wait_ge(s["raw_ready"], ONE + 10 * G0 + half + 1)
                        prep_lump(2 + half, half, w_slot(kind, 0))
                pe.wait_ge(s["att_ready"], b + 1)
                pe.wait_ge(s["raw_ready"], ONE + 10 * G0 + 4)
                for t in range(NT):
                    last = pe.matmul(psum[:, 2 + t // 4, (t % 4) * P:(t % 4 + 1) * P], sc[:, t, :], ident[:],
                                     start=True, stop=True, is_transpose=True)
                last.then_inc(s["eT_psum"], 1)
                pe.wait_ge(s["eT_done"], b + 1)
                for t in range(NT):
                    if t >= 2:
                        pe.wait_ge(s["g0_lin"], ONE + NT * b + t - 1)
                    pe.matmul(bank(4 + t % 2), eT[:, t, :], auxvu[:], start=True, stop=True).then_inc(s["aux_psum"], 1)

                M, O, TA, TB = 7, 6, 4, 5

                def group(G, prefetch):
                    wbase = 10 * G + 4
                    lumps = {}
                    for n, kind, j, t1, t2 in preps(prefetch):
                        lumps[t1] = (n, kind, j, 0)
                        lumps[t2] = (n, kind, j, 1)
                    m_user = [(s["oproj_evac"], ONE + 2 * NT * G)]

                    def m_free():
                        pe.wait_ge(*m_user[0])

                    def scores(t):
                        j, qi = t // NT, t % NT
                        if qi == 0:
                            if j == 0:
                                pe.wait_ge(s["k_ready"], G + 1)
                            pe.wait_ge(s["q_ready"], GQ * G + j + 1)
                        pe.wait_ge(s["exp_done"], ONE + TG * G + (t - 1 if t >= 2 else 0))
                        sl = 2 * (t % 2)
                        lhs = (qT_hi[:, j % 2, qi * P:(qi + 1) * P], qT_lo[:, j % 2, qi * P:(qi + 1) * P])
                        kh, kl = kT_hi[:].rearrange("p a n -> p (a n)"), kT_lo[:].rearrange("p a n -> p (a n)")
                        k0 = qi * P
                        for bi, (lo, n) in enumerate(((0, 512), (512, KEYS - 512))):
                            dst = psum[:, sl + bi, 0:n]
                            rhs = (kh[:, k0 + lo:k0 + lo + n], kl[:, k0 + lo:k0 + lo + n])
                            masked = (qi < NT - 1) if bi == 0 else (qi > 0)
                            last = hilo(pe, dst, lhs, rhs, True, not masked)
                            if masked:
                                m, at = (mask_ge, 0) if bi == 0 else (mask_le, n - P)
                                last = pe.matmul(psum[:, sl + bi, at:at + P], ident_b[:], m[:], start=False, stop=True)
                        last.then_inc(s["scores_ready"], 1)

                    def transposes(t):
                        qi = t % NT
                        sl = t % 3
                        pe.wait_ge(s["recip_ready"], TG * G + t + 1)
                        pe.wait_ge(s["t_evac"], ONE + 2 * (TG * G + t))
                        if t == 0:
                            pe.wait_ge(s["g0_lin"], ONE + NT * (b + 1))
                        for kb in range(NT):
                            if kb == qi:
                                src = stat[:, 2, t % 4:t % 4 + 1].broadcast_to([P, P])
                            else:
                                c = (kb - qi - 1) % NT
                                src = probs[:, sl, c * P:(c + 1) * P]
                            last = pe.matmul(psum[:, TA + kb // 4, (kb % 4) * P:(kb % 4 + 1) * P], src, ident[:],
                                             start=True, stop=True, is_transpose=True)
                            if kb % 4 == 3:
                                last.then_inc(s["t_full"], 1)

                    def pv(c, part):
                        own = 2 * (c % (NT // 2))
                        if part == 0:
                            pe.wait_ge(s["t_evac"], ONE + 2 * (TG * G + 2 * c + 2))
                            pe.wait_ge(s["o_norm"], ONE + CG * G + c)
                            if c == 0:
                                pe.wait_ge(s["v_evac"], ONE + 2 * (G + 1))
                        for i in range(4 * part, 4 * part + 4):
                            kb = pv_keys(c)[i]
                            lo, hi = {0: (P, CQ), 1: (0, P)}.get(kb - own, (0, CQ))
                            last = hilo(pe, psum[:, O, CQ * (c % 2) + lo:CQ * (c % 2) + hi], (v_hi[:, kb, :], v_lo[:, kb, :]),
                                        (pT_hi[:, c % 2, kb, lo:hi], pT_lo[:, c % 2, kb, lo:hi]), i == 0, i == NT - 1)
                        if part == 1:
                            last.then_inc(s["pv_done"], 1)

                    def oproj(pair, tt, dst):
                        if tt % 2 == 0:
                            pe.wait_ge(s["o_lo_done"], CG * G + NT * pair + NT // 2 + tt // 2 + 1)
                            if tt == 0:
                                for i in (0, 1):
                                    pe.wait_ge(s["w_ready"], ONE + wbase + w_index(prefetch, "o", 2 * pair + i))
                        for i in range(2):
                            lhs = (oT_hi[:, i, tt * P:(tt + 1) * P], oT_lo[:, i, tt * P:(tt + 1) * P])
                            last = hilo(pe, bank(dst), lhs, (wo_hi[:, i, :], wo_lo[:, i, :]), i == 0, i == 1)
                        last.then_inc(s["oproj_psum"], 1)

                    def lump(t):
                        if t in lumps:
                            n, kind, j, half = lumps[t]
                            m_free()
                            if half == 0:
                                need = 10 * G + 4 if (kind, j) == ("q", 1) else wbase + w_index(prefetch, kind, j)
                                pe.wait_ge(s["w_ready"], ONE + need)
                            prep_lump(M, half, w_slot(kind, j))
                            m_user[0] = (s["raw_ready"], ONE + 10 * G + 2 * (n + 1) + half + 1)

                    for t in range(TG):
                        scores(t)
                        if t in V_STEPS:
                            half = V_STEPS.index(t)
                            if half == 0:
                                pe.wait_ge(s["w_ready"], ONE + 10 * G + 3)
                            else:
                                pe.wait_ge(s["v_evac"], ONE + 2 * G + 1)
                            for u in range(4):
                                tt = 4 * half + u
                                for c in range(EC):
                                    last = hilo(pe, psum[:, O, u * P:(u + 1) * P], xT(c, tt * P, (tt + 1) * P),
                                                (wv_hi[:, c * P:(c + 1) * P], wv_lo[:, c * P:(c + 1) * P]),
                                                c == 0, c == EC - 1)
                            last.then_inc(s["v_psum"], 1)
                        if pv_parts(t) is not None:
                            pv(*pv_parts(t))
                        if O_STEP <= t < O_STEP + NT:
                            m_free()
                            oproj(0, t - O_STEP, M)
                            m_user[0] = (s["oproj_evac"], ONE + 2 * NT * G + t - O_STEP + 1)
                        lump(t)
                        if t >= 2:
                            transposes(t - 2)
                    pv(CG - 3, 1)
                    transposes(TG - 2)
                    for part in range(2):
                        pv(CG - 2, part)
                    transposes(TG - 1)
                    lump(TG)
                    for part in range(2):
                        pv(CG - 1, part)
                    for tt in range(NT):
                        if tt == 0:
                            m_free()
                        elif tt == 1:
                            pe.wait_ge(s["o_norm"], ONE + CG * G + CG)
                        else:
                            pe.wait_ge(s["oproj_evac"], ONE + 2 * NT * G + NT + tt - 1)
                        oproj(1, tt, M if tt % 2 == 0 else O)

                with pe.Fori(0, KV0 - 1) as g:
                    group(G0 + g, True)
                group(G0 + KV0 - 1, False)

                pe.wait_ge(s["oproj_evac"], ONE + 2 * NT * KV0 * (b + 1))
                for t in range(NT + 1):
                    if t < NT:
                        transposed(t, gx, 2 * NT * b + NT)
                    if t >= 1:
                        u = t - 1
                        if u == 0:
                            pe.wait_ge(s["w1_lo_done"], 2 * (b + 1))
                        pe.wait_ge(s["xT_lo_done"], ONE + 2 * NT * b + NT + u + 1)
                        if u >= 2:
                            pe.wait_ge(s["qkv_evac"], ONE + NT * b + u - 1)
                            pe.wait_ge(s["ffn_lin"], ONE + NT * b + u - 1)
                        for lo, n in ((0, 512), (512, W1N - 512)):
                            for c in range(EC):
                                last = hilo(pe, psum[:, 2 + 2 * (u % 2) + lo // 512, 0:n], xT(c, u * P, (u + 1) * P),
                                            (w1_hi[:, c, lo:lo + n], w1_lo[:, c, lo:lo + n]), c == 0, c == EC - 1)
                        last.then_inc(s["qkv_psum"], 1)
                        for c in range(EC):
                            last = hilo(pe, bank(6 + u % 2), xT(c, u * P, (u + 1) * P),
                                        (w1_hi[:, c, W1N:], w1_lo[:, c, W1N:]), c == 0, c == EC - 1)
                        last.then_inc(s["ffn_psum"], 1)

                QM, KM, X, Y = 0, 2, 5, 6

                def stack_T(src, half, x):
                    pe.wait_ge(s["qt_evac"], ONE + x)
                    for i in range(4):
                        last = pe.matmul(psum[0:ST1, X, i * P:(i + 1) * P].bitcast(R), src[:, 4 * half + i, :],
                                         ident_r[:], start=True, stop=True, is_transpose=True)
                    last.then_inc(s["qt_psum"], 1)

                def q_scores(j, h, c):
                    i, k0, w = q_chunks()[c]
                    pe.wait_ge(s["qm_max"], ONE + CH * h + (c - 1 if c >= 2 else 0))
                    diag = k0 + w == (i + 1) * P
                    last = pe.matmul(psum[:, QM + c % 2, 0:w], qTa[0:ST1, j % 2, i * P:(i + 1) * P],
                                     kT1[0:ST1, (j // GQ) % 2, k0:k0 + w], start=True, stop=not diag)
                    if diag:
                        last = pe.matmul(psum[:, QM + c % 2, w - P:w], ident_b[:], mask_le[:], start=False, stop=True)
                    last.then_inc(s["qm_psum"], 1)

                def k_scores(j, h, c):
                    i, q0, w = k_chunks()[c]
                    pe.wait_ge(s["km_exp"], ONE + CH * h + (c - 2 if c >= 3 else 0))
                    diag = q0 == i * P
                    last = pe.matmul(psum[:, KM + c % 3, 0:w], kT1[0:ST1, (j // GQ) % 2, i * P:(i + 1) * P],
                                     qTb[0:ST1, j % 2, q0:q0 + w], start=True, stop=not diag)
                    if diag:
                        last = pe.matmul(psum[:, KM + c % 3, 0:P], ident_b[:], mask_ge[:], start=False, stop=True)
                    last.then_inc(s["km_psum"], 1)

                def pv1(j, h, c):
                    i, q0, w = k_chunks()[c]
                    pe.wait_ge(s["km_exp"], ONE + CH * h + c + 1)
                    if c == 0:
                        pe.wait_ge(s["pv1_evac"], ONE + 2 * h)
                    for lo, hi in ((q0, min(q0 + w, 512)), (max(q0, 512), q0 + w)):
                        if lo < hi:
                            half = lo // 512
                            last = pe.matmul(psum[0:VS, Y + half, lo % 512:lo % 512 + hi - lo],
                                             v_st[:, (j // GQ) % 2, i, :], pT1_cols(i, lo, hi - lo),
                                             start=(i == 0), stop=(i == 4 * half + 3))
                    if c in (7, CH - 1):
                        last.then_inc(s["pv1_psum"], 1)

                def pair(N, prefetch):
                    for j in range(PH):
                        h = PH * N + j
                        turns = x_turns(j, prefetch)
                        for c in range(CH):
                            if c + 2 < CH:
                                k_scores(j, h, c + 2)
                            elif "T2" in turns:
                                if c + 2 == CH:
                                    pe.wait_ge(s["qt_evac"], ONE + XP * N + x_at(j, "T2", prefetch) + 2)
                                k_scores(j + 1, h + 1, c + 2 - CH)
                            if "T2" in turns and c < CH // 2:
                                q_scores(j + 1, h + 1, 2 * c)
                                q_scores(j + 1, h + 1, 2 * c + 1)
                            if "T1" in turns and c in (1, 3):
                                if c == 1:
                                    pe.wait_ge(s["st_ready"], 2 * (2 * N + (j + 2) // GQ + 1))
                                stack_T(q_st[:, ((j + 2) // GQ) % 2, :, (j + 2) % GQ, :], c // 2,
                                        XP * N + x_at(j, "T1", prefetch) + c // 2)
                            if "K" in turns and c in (5, 6):
                                if c == 5:
                                    pe.wait_ge(s["st_ready"], 2 * (2 * N + j // GQ + 1) + 1)
                                stack_T(k_st[:, (j // GQ + 1) % 2], c - 5, XP * N + x_at(j, "K", prefetch) + c - 5)
                            if "T2" in turns and c in (7, 8):
                                if c == 7:
                                    pe.wait_ge(s["nm_ready"], h + 2)
                                stack_T(q_st[:, ((j + 1) // GQ) % 2, :, (j + 1) % GQ, :], c - 7,
                                        XP * N + x_at(j, "T2", prefetch) + c - 7)
                            if c == 0 and j % GQ == 0:
                                pe.wait_ge(s["v1_ready"], 2 * N + j // GQ + 1)
                            pv1(j, h, c)

                N0 = NPAIR * b
                pe.wait_ge(s["qkv_evac"], ONE + NT * (b + 1))
                pe.wait_ge(s["ffn_lin"], ONE + NT * (b + 1))
                pe.wait_ge(s["st_ready"], 4 * N0 + 1)
                for half in range(2):
                    stack_T(k_st[:, 0], half, XP * N0 + half)
                pe.wait_ge(s["st_ready"], 4 * N0 + 2)
                for j in range(2):
                    for half in range(2):
                        stack_T(q_st[:, 0, :, j, :], half, XP * N0 + 2 + 2 * j + half)
                for c in range(CH):
                    q_scores(0, PH * N0, c)
                pe.wait_ge(s["nm_ready"], PH * N0 + 1)
                for half in range(2):
                    stack_T(q_st[:, 0, :, 0, :], half, XP * N0 + 6 + half)
                pe.wait_ge(s["qt_evac"], ONE + XP * N0 + XL)
                for c in range(2):
                    k_scores(0, PH * N0, c)
                with pe.Fori(0, NPAIR - 1) as n:
                    pair(N0 + n, True)
                pair(N0 + NPAIR - 1, False)

                pe.wait_ge(s["wo1_loaded"], 16 * (b + 1))
                for t in range(NT):
                    if t in (0, NT // 2):
                        pe.wait_ge(s["ctx_ready"], ONE + 2 * NPAIR * (b + 1) - 1 + (t > 0))
                    pe.wait_ge(s["y_ready"], ONE + NT * b + max(t - 3, 0))
                    for c in range(EC):
                        last = pe.matmul(bank(t % 4), ctxT[:, c, t * P:(t + 1) * P], wo1[:, c, :],
                                         start=(c == 0), stop=(c == EC - 1))
                    last.then_inc(s["y_psum"], 1)

        @block.scalar
        def _(act):
            give_credit(act, "scalar")
            act.wait_ge(s["consts"], 2)
            act.activation(ident_r[:], ident[:], ACT.Copy)
            act.wait_ge(s["pro_stats"], 3)
            act.activation(pr_sm[:, 7 * B * NT:7 * B * NT + 1], pr_sm[:, 0:1], ACT.Copy).then_inc(s["pro_act"], 1)
            act.activation(pr_sm[:, 7 * B * NT + 1:7 * B * NT + 2], pr_sm[:, 0:1], ACT.Copy).then_inc(s["pro_act"], 1)
            act.wait_ge(s["pro_stats"], 4)
            act.activation(half_norm[:], pr_sm[:, B * NT:2 * B * NT], ACT.Ln, bias=1.0,
                           accum_out=pr_sm[:, 6 * B * NT:6 * B * NT + 1]).then_inc(s["pro_act"], 1)

            with act.Fori(0, B) as b:
                G0 = b * KV0

                def hi_of(t, base):
                    act.wait_ge(s["xT_psum"], base + t + 1)
                    act.activation(xT_hi[:, :, t * P:(t + 1) * P], psum[:, t % 2, :].rearrange("p (c n) -> p c n", c=EC),
                                   ACT.Copy).then_inc(s["xT_hi_done"], 1)

                def w_hi(idx, i, kind, j):
                    act.wait_ge(s[f"w_loaded{i % 2}"], 16 * (idx + 1))
                    act.activation(w_slot(kind, j)[0], w_st[:, i % 2, :], ACT.Copy).then_inc(s["w_hi_done"], 1)

                def raw_copy(p, half, bk=7):
                    act.wait_ge(s["prep_psum"], 2 * p + half + 1)
                    if half == 0:
                        act.wait_ge(s["roped"], ONE + p)
                    act.activation(raw[:, 512 * half:512 * half + 512], psum[:, bk, :], ACT.Copy)\
                        .then_inc(s["raw_ready"], 1)

                def q_hi(p, j, free):
                    act.wait_ge(s["roped"], ONE + p + 1)
                    act.wait_ge(s["scores_ready"], ONE + free)
                    act.activation(qT_hi[:, j % 2, :], q_f[:], ACT.Copy).then_inc(s["q_hi_done"], 1)

                def k_hi(G, p):
                    act.wait_ge(s["roped"], ONE + p + 1)
                    act.wait_ge(s["scores_ready"], ONE + TG * G)
                    for half in range(2):
                        last = act.activation(kT_hi[:, half, :], k_f[:, P:S] if half == 0 else k_f[:, 0:KEYS], ACT.Copy)
                    last.then_inc(s["k_hi_done"], 1)

                act.wait_ge(s["ctx_ready"], ONE + 2 * NPAIR * b)
                act.dma_start(xn[:], a["x3"][b, :, :].rearrange("(t p) e -> p t e", p=P)).then_inc(s["x_loaded"], 16)
                act.dma_start(wa_f[:], a["wa"]).then_inc(s["wa_loaded"], 16)
                act.wait_ge(s["y_ready"], ONE + NT * b)
                act.wait_ge(s["wa_loaded"], 16 * (b + 1))
                act.activation(wa_hi[:], wa_f[:], ACT.Copy).then_inc(s["wa_hi_done"], 1)
                for t in range(NT):
                    hi_of(t, 2 * NT * b)
                    if t in (3, 5, 6, 7):
                        i = (3, 5, 6, 7).index(t)
                        w_hi(5 * G0 + i // 2, i, *W_PRE[i])
                act.wait_ge(s["gelu_in"], b + 1)
                act.activation(zt[:], zt[:], ACT.Tanh, scale=GELU_C).then_inc(s["gelu_exp"], 1)
                act.wait_ge(s["router_psum"], b + 1)
                for i, bk in enumerate((0, 1, 6, 7)):
                    last = act.activation(sc[:, 2 * i:2 * i + 2, :],
                                          psum[:, bk, :].rearrange("p (t k n) -> p t k n", t=2, k=2)[:, :, 0, :], ACT.Copy)
                last.then_inc(s["sc_done"], 1)
                for half in range(2):
                    raw_copy(5 * G0, half, 2 + half)
                for k in range(2):
                    act.wait_ge(s["gate_in"], 2 * b + k + 1)
                    act.activation(sma[:, 1 + k, :], sma[:, 1 + k, :], ACT.Tanh, scale=0.5).then_inc(s["gate_exp"], 1)
                for half in range(2):
                    raw_copy(5 * G0 + 1, half, 2 + half)
                k_hi(G0, 5 * G0)
                act.wait_ge(s["att_in"], b + 1)
                act.activation(sc[:], rep[:], ACT.Exp).then_inc(s["att_exp"], 1)
                act.wait_ge(s["eT_psum"], b + 1)
                act.activation(eT[:].rearrange("p t n -> p (t n)"),
                               psum[:, 2:4, :].rearrange("p a n -> p (a n)"), ACT.Copy).then_inc(s["eT_done"], 1)
                for t in range(NT):
                    act.wait_ge(s["g0_lin"], ONE + NT * b + t + 1)
                    act.activation(ex_a[:, t, :], xn[:, t, :], ACT.Tanh, scale=0.5).then_inc(s["g0_exp"], 1)
                q_hi(5 * G0 + 1, 0, TG * G0)

                M, O, TA, TB = 7, 6, 4, 5

                def group(G, prefetch):
                    w_at = {t: (i, k, j) for i, (t, k, j) in enumerate(w_items(prefetch))}
                    raws, his = {}, {}
                    for n, kind, j, t1, t2 in preps(prefetch):
                        raws[t1] = (n, 0)
                        raws[t2] = (n, 1)
                        if kind == "q" and j > 0:
                            his[t2 + 2] = (n, j)

                    def exp(t):
                        act.wait_ge(s["negmax_ready"], TG * G + t + 1)
                        act.wait_ge(s["t_full"], ONE + 2 * (TG * G + (t - 2 if t >= 3 else 0)))
                        act.activation(probs[:, t % 3, :], psum[:, 2 * (t % 2):2 * (t % 2) + 2, :]
                                       .rearrange("p a n -> p (a n)")[:, 0:KEYS], ACT.Exp, bias=stat[:, 0, t % 4:t % 4 + 1],
                                       accum_out=stat[:, 1, t % 4:t % 4 + 1]).then_inc(s["exp_done"], 1)

                    def t_hi(t):
                        for k in range(2):
                            act.wait_ge(s["t_full"], ONE + 2 * (TG * G + t) + k + 1)
                            act.activation(pT_hi[:, (t // 2) % 2, 4 * k:4 * k + 4, (t % 2) * P:(t % 2 + 1) * P],
                                           psum[:, TA + k, :].rearrange("p (k n) -> p k n", k=4), ACT.Copy)\
                                .then_inc(s["t_hi_done"], 1)

                    def o_hi(c):
                        j, at = c // 4, CQ * (c % 4)
                        act.wait_ge(s["o_norm"], ONE + CG * G + c + 1)
                        act.wait_ge(s["oproj_psum"], ONE + 2 * NT * G + (0 if j < 2 else 2 * (c % 4) + 2))
                        act.activation(oT_hi[:, j % 2, at:at + CQ], o_f[:], ACT.Copy).then_inc(s["o_hi_done"], 1)

                    for t in range(TG):
                        early = t < 2 or t in raws or t in V_STEPS or O_STEP <= t < O_STEP + NT
                        if early:
                            exp(t)
                        if t in V_STEPS:
                            half = V_STEPS.index(t)
                            act.wait_ge(s["v_psum"], 2 * G + half + 1)
                            act.activation(v_hi[:, 4 * half:4 * half + 4, :],
                                           psum[:, O, :].rearrange("p (k n) -> p k n", k=4), ACT.Copy)\
                                .then_inc(s["v_hi_done"], 1)
                        if pv_parts(t) is not None and pv_parts(t)[1] == 1:
                            o_hi(pv_parts(t)[0])
                        if t in raws:
                            pr, half = raws[t]
                            raw_copy(5 * G + 1 + pr, half)
                        if t >= 2:
                            t_hi(t - 2)
                        if not early:
                            exp(t)
                        if t in his:
                            n, j = his[t]
                            q_hi(5 * G + 1 + n, j, TG * G + NT * (j - 1))
                        if t in w_at:
                            i, kind, j = w_at[t]
                            if kind == "o" and j == 0:
                                act.wait_ge(s["oproj_psum"], ONE + 2 * NT * G)
                                act.wait_ge(s["g0_stored"], 16 * (b + 1))
                            if kind == "o" and j == 2:
                                act.wait_ge(s["oproj_psum"], ONE + 2 * NT * G + NT)
                            if kind == "q":
                                act.wait_ge(s["prep_psum"], 10 * G + {2: 4, 3: 6, 0: 8, 1: 12}[j])
                            if kind == "v":
                                act.wait_ge(s["v_psum"], 2 * G + 2)
                            w_hi(5 * G + 2 + i // 2, i, kind, j)
                    o_hi(CG - 3)
                    t_hi(TG - 2)
                    o_hi(CG - 2)
                    t_hi(TG - 1)
                    if prefetch:
                        raw_copy(5 * G + 1 + 5, 1)
                        k_hi(G + 1, 5 * G + 1 + 3)
                    o_hi(CG - 1)
                    if prefetch:
                        q_hi(5 * G + 1 + 5, 0, TG * G + 3 * NT)

                with act.Fori(0, KV0 - 1) as g:
                    group(G0 + g, True)
                group(G0 + KV0 - 1, False)

                for h in range(2):
                    act.wait_ge(s[f"w1_loaded{h}"], (32 + 16 * h) * (b + 1))
                    act.activation(w1_hi[:, 2 * h:2 * h + 2, :], w1_f[:, 2 * h:2 * h + 2, :], ACT.Copy)\
                        .then_inc(s["w1_hi_done"], 1)
                for t in range(NT + 1):
                    if t < NT:
                        hi_of(t, 2 * NT * b + NT)
                    if t >= 1:
                        u = t - 1
                        act.wait_ge(s["ffn_lin"], ONE + NT * b + u + 1)
                        act.activation(g_exp[:, u % 2, :], g_lin[:, u % 2, :], ACT.Tanh, scale=0.5).then_inc(s["ffn_exp"], 1)

                QM, KM, X, Y = 0, 2, 5, 6
                act.wait_ge(s["qkv_evac"], ONE + NT * (b + 1))
                act.wait_ge(s["ffn_done"], NT * (b + 1))

                def stack_evac(dst, half, x):
                    act.wait_ge(s["qt_psum"], ONE + x + 1)
                    act.activation(dst[0:ST1, 512 * half:512 * half + 512], psum[0:ST1, X, :], ACT.Copy)\
                        .then_inc(s["qt_evac"], 1)

                def out_evac(j, h):
                    act.wait_ge(s["pv1_psum"], ONE + 2 * h + 1)
                    act.wait_ge(s[f"o_moved{j % 2}"], ONE + 16 * (h - j) + 32 * (j // 2))
                    act.activation(o_st[:, j % 2, 0:512], psum[0:VS, Y, :], ACT.Copy).then_inc(s["pv1_evac"], 1)

                def pair(N, prefetch):
                    for j in range(PH):
                        h = PH * N + j
                        turns = x_turns(j, prefetch)
                        for c in range(CH):
                            i, q0, w = k_chunks()[c]
                            act.wait_ge(s["km_psum"], ONE + CH * h + c + 1)
                            act.activation(pT1_cols(i, q0, w), psum[:, KM + c % 3, 0:w], ACT.Exp).then_inc(s["km_exp"], 1)
                            if c == 5 and "K" in turns:
                                stack_evac(kT1[:, (j // GQ + 1) % 2], 0, XP * N + x_at(j, "K", prefetch))
                            if c in (7, 8) and "T2" in turns:
                                stack_evac(qTb[:, (j + 1) % 2], c - 7, XP * N + x_at(j, "T2", prefetch) + c - 7)
                            if c == 9:
                                out_evac(j, h)

                N0 = NPAIR * b
                stack_evac(kT1[:, 0], 0, XP * N0)
                for half in range(2):
                    stack_evac(qTb[:, 0], half, XP * N0 + 6 + half)
                with act.Fori(0, NPAIR - 1) as n:
                    pair(N0 + n, True)
                pair(N0 + NPAIR - 1, False)

        @block.vector
        def _(dve):
            give_credit(dve, "vector")
            N2 = B * NT

            def sm(i, n=N2):
                return pr_sm[:, i * N2:i * N2 + n]

            dve.wait_ge(s["pro_x"], 16)
            for t in range(N2):
                dve.bn_stats(pr_st[:, t, :], pr_x[:, t, :])
            dve.drain()
            for t in range(N2):
                dve.bn_aggr(mv0[:, t, :], pr_st[:, t, :])
            dve.drain()
            dve.tensor_scalar(sm(0), mv0[:, :, 1], LN_EPS, None, ALU.add).then_inc(s["pro_stats"], 1)
            dve.memset(sm(6, 2), 0.0)
            dve.wait_ge(s["pro_loaded"], 16 * 16)
            dve.tensor_tensor(pr_mix[:], pr_cs[:, :, 0], pr_cs[:, :, 1], ALU.mult)
            dve.drain()
            for k in range(2):
                last = dve.tensor_scalar(pr_b[:, k, :], pr_b[:, k, :], pr_mix[:, k:k + 1], None, ALU.mult)
                last.then_inc(s["pro_stats"], 1)
            dve.wait_ge(s["pro_pow"], 1)
            dve.tensor_tensor(sm(2), rstd0[:], rstd0[:], ALU.mult)
            dve.drain()
            dve.tensor_tensor(sm(1), sm(2), mv0[:, :, 1], ALU.mult).then_inc(s["pro_stats"], 1)
            dve.wait_ge(s["pro_mm"], 1)
            dve.tensor_copy(pr_rkT[:], psum[:, 0, 0:P]).then_inc(s["pro_evac"], 1)
            dve.wait_ge(s["pro_mm"], 2)
            dve.tensor_copy(pr_avd[:], psum[:, 1, 0:P]).then_inc(s["pro_evac"], 1)
            dve.wait_ge(s["pro_mm"], 3)
            dve.tensor_scalar(router[0:BOT, 0:P], psum[0:BOT, 2, 0:P], float(RDIM) ** -0.5, None, ALU.mult)
            dve.tensor_scalar(router[0:BOT, P:2 * P], pr_keysT[0:BOT, :], float(BOT) ** -0.5, None, ALU.mult)\
                .then_inc(s["pro_evac"], 1)
            dve.wait_ge(s["pro_mm"], 4)
            dve.tensor_copy(auxvu[:], psum[:, 3, :]).then_inc(s["pro_evac"], 1)
            for c in range(EC):
                dve.wait_ge(s["pro_mm"], 5 + c)
                dve.tensor_tensor(pr_w[:, c, :], psum[:, 4 + c, :], pr_w[:, c, :], ALU.add).then_inc(s["pro_evac"], 1)
            dve.wait_ge(s["pro_mm"], 5 + EC)
            dve.tensor_scalar(sm(3, 1), psum[:, 2, 0:1], 1.0 / (B * S), 1e-6, ALU.mult, ALU.add)
            dve.drain()
            dve.reciprocal(sm(4, 1), sm(3, 1))
            dve.drain()
            dve.tensor_scalar(half_norm[:], half_norm[:], sm(4, 1), 0.5, ALU.mult, ALU.mult).then_inc(s["pro_stats"], 1)
            dve.drain()

            with dve.Fori(0, B) as b:
                G0 = b * KV0

                def lo_of(t, base):
                    dve.wait_ge(s["xT_hi_done"], base + t + 1)
                    dve.tensor_tensor(xT_lo[:, :, t * P:(t + 1) * P], psum[:, t % 2, :].rearrange("p (c n) -> p c n", c=EC),
                                      xT_hi[:, :, t * P:(t + 1) * P].bitcast(F), ALU.subtract).then_inc(s["xT_lo_done"], 1)

                def k_lo(G):
                    dve.wait_ge(s["k_hi_done"], G + 1)
                    for half in range(2):
                        last = dve.tensor_tensor(kT_lo[:, half, :], k_f[:, P:S] if half == 0 else k_f[:, 0:KEYS],
                                                 kT_hi[:, half, :].bitcast(F), ALU.subtract)
                    last.then_inc(s["k_ready"], 1)

                dve.wait_ge(s["x_loaded"], 16 * (b + 1))
                dve.wait_ge(s["wa_hi_done"], b + 1)
                dve.tensor_tensor(wa_lo[:], wa_f[:], wa_hi[:].bitcast(F), ALU.subtract).then_inc(s["wa_lo_done"], 1)
                mean, rstd, hn = sma[:, 8, :], sma[:, 9, :], sma[:, 10, :]
                dve.tensor_copy(mean, mv0[:, :, 0].rearrange("p (b t) -> p b t", b=B)[:, b, :])
                dve.tensor_copy(rstd, rstd0[:].rearrange("p (b t) -> p b t", b=B)[:, b, :])
                dve.tensor_copy(hn, half_norm[:].rearrange("p (b t) -> p b t", b=B)[:, b, :])
                dve.drain()
                for t in range(NT):
                    dve.tensor_scalar(xn[:, t, :], xn[:, t, :], mean[:, t:t + 1], rstd[:, t:t + 1],
                                      ALU.subtract, ALU.mult).then_inc(s["xn_ready"], 1)
                    if t >= 1:
                        lo_of(t - 1, 2 * NT * b)
                lo_of(NT - 1, 2 * NT * b)
                dve.memset(acc[:], 0.0).then_inc(s["acc_zero"], 1)
                dve.wait_ge(s["z_psum"], NT * (b + 1))
                zps = psum[:, 2:4, :].rearrange("p a (t n) -> p (a t) n", t=4)
                bc = lambda v: v[:, :].unsqueeze(1).broadcast_to([P, NT, P])
                dve.tensor_tensor(zb[:], zps, bc(bu1_b), ALU.add)
                dve.drain()
                dve.tensor_tensor(zt[:], zb[:], zb[:], ALU.mult)
                dve.drain()
                dve.tensor_scalar(zt[:], zt[:], GELU_A, 1.0, ALU.mult, ALU.add)
                dve.drain()
                dve.tensor_tensor(zt[:], zt[:], zb[:], ALU.mult).then_inc(s["gelu_in"], 1)
                for h in range(2):
                    dve.wait_ge(s["query_psum"], 2 * b + h + 1)
                    dve.tensor_scalar(queryT[:, 512 * h:512 * h + 512], psum[:, 4 + h, :], row64[:], None, ALU.add)\
                        .then_inc(s["query_done"], 1)
                dve.wait_ge(s["gelu_exp"], b + 1)
                dve.scalar_tensor_tensor(zt[:].rearrange("p t n -> p (t n)"), zt[:].rearrange("p t n -> p (t n)"), 1.0,
                                         zb[:].rearrange("p t n -> p (t n)"), ALU.add, ALU.mult)
                dve.drain()
                dve.tensor_tensor(zt[:], zt[:], bc(wu2_b), ALU.mult)
                dve.drain()
                sig, u, gate, ssum, coef, mx = sma[:, 1, :], sma[:, 2, :], sma[:, 3, :], sma[:, 4, :], sma[:, 5, :], sma[:, 6, :]
                tmp = sma[:, 7, :]
                dve.tensor_reduce(sig, zt[:], AX.X, ALU.add)
                dve.drain()
                dve.tensor_scalar(sig, sig, 0.5, scal_b[:, 0:1], ALU.mult, ALU.add).then_inc(s["gate_in"], 1)
                dve.wait_ge(s["gate_exp"], 2 * b + 1)
                dve.tensor_scalar(u, sig, 1.25, 1.25, ALU.mult, ALU.add)
                dve.drain()
                dve.tensor_tensor(u, u, hn, ALU.add)
                dve.drain()
                dve.tensor_scalar(u, u, 0.0, 5.0, ALU.max, ALU.min)
                dve.drain()
                dve.tensor_scalar(u, u, 0.5, 1.0 / 1.5, ALU.subtract, ALU.mult)
                dve.drain()
                dve.tensor_scalar(u, u, 0.0, 1.0, ALU.max, ALU.min)
                dve.drain()
                dve.tensor_scalar(u, u, scal_b[:, 1:2], scal_b[:, 2:3], ALU.mult, ALU.add).then_inc(s["gate_in"], 1)
                dve.wait_ge(s["gate_exp"], 2 * b + 2)
                dve.tensor_scalar(gate, u, 0.5, 0.5, ALU.mult, ALU.add)
                dve.drain()
                dve.tensor_scalar(tmp, gate, 0.05, None, ALU.is_ge)
                dve.drain()
                dve.wait_ge(s["sc_done"], b + 1)
                dve.tensor_tensor(gate, gate, tmp, ALU.mult)
                for t in range(NT):
                    dve.max(top8[:, t, :], sc[:, t, :])
                dve.drain()
                for t in range(NT):
                    dve.match_replace(rep[:, t, :], top8[:, t, :], sc[:, t, :], -3.0e38)
                dve.drain()
                dve.tensor_tensor(rep[:], rep[:], sc[:], ALU.not_equal)
                dve.drain()
                dve.tensor_scalar(rep[:], rep[:], -NEG, NEG, ALU.mult, ALU.add)
                dve.drain()
                for i, bk in enumerate((0, 1, 6, 7)):
                    dve.tensor_tensor(rep[:, 2 * i:2 * i + 2, :],
                                      psum[:, bk, :].rearrange("p (t k n) -> p t k n", t=2, k=2)[:, :, 1, :],
                                      rep[:, 2 * i:2 * i + 2, :], ALU.add)
                dve.drain()
                dve.tensor_reduce(mx, rep[:], AX.X, ALU.max)
                dve.drain()
                dve.tensor_tensor(rep[:], rep[:], mx.unsqueeze(2).broadcast_to([P, NT, P]), ALU.subtract)\
                    .then_inc(s["att_in"], 1)
                dve.wait_ge(s["att_exp"], b + 1)
                dve.tensor_reduce(ssum, sc[:], AX.X, ALU.add).then_inc(s["att_ready"], 1)
                dve.drain()
                dve.reciprocal(coef, ssum)
                dve.drain()
                dve.tensor_tensor(coef, coef, gate, ALU.mult)
                k_lo(G0)
                dve.drain()
                for t in range(NT):
                    dve.wait_ge(s["aux_psum"], NT * b + t + 1)
                    dve.scalar_tensor_tensor(xn[:, t, :], psum[:, 4 + t % 2, :], coef[:, t:t + 1], xn[:, t, :],
                                             ALU.mult, ALU.add).then_inc(s["g0_lin"], 1)
                dve.wait_ge(s["g0_exp"], NT * (b + 1))
                flat = lambda v: v[:].rearrange("p t n -> p (t n)")
                dve.scalar_tensor_tensor(flat(xn), ex_a[:, 0:NT, :].rearrange("p t n -> p (t n)"), 1.0, flat(xn), ALU.add, ALU.mult)\
                    .then_inc(s["g0_ready"], 1)

                M, O, TA, TB = 7, 6, 4, 5
                def group(G, prefetch):

                    def negmax(t):
                        dve.wait_ge(s["scores_ready"], ONE + TG * G + t + 1)
                        dve.tensor_reduce(stat[:, 0, t % 4:t % 4 + 1], psum[:, 2 * (t % 2):2 * (t % 2) + 2, :]
                                          .rearrange("p a n -> p (a n)")[:, 0:KEYS], AX.X, ALU.max, negate=True)\
                            .then_inc(s["negmax_ready"], 1)

                    def recip(t):
                        dve.wait_ge(s["exp_done"], ONE + TG * G + t + 1)
                        dve.reciprocal(stat[:, 2, t % 4:t % 4 + 1], stat[:, 1, t % 4:t % 4 + 1]).then_inc(s["recip_ready"], 1)

                    def t_lo(t):
                        c, qi, at = t // 2, t % NT, (t % 2) * P
                        for k in range(2):
                            dve.wait_ge(s["t_hi_done"], 2 * (TG * G + t) + k + 1)
                            if qi // 4 == k:
                                dve.tensor_copy(recs[:, c % 2, at:at + P], psum[:, TA + k, (qi % 4) * P:(qi % 4 + 1) * P])
                            dst = (slice(None), c % 2, slice(4 * k, 4 * k + 4), slice(at, at + P))
                            dve.tensor_tensor(pT_lo[dst], psum[:, TA + k, :].rearrange("p (k n) -> p k n", k=4),
                                              pT_hi[dst].bitcast(F), ALU.subtract).then_inc(s["t_evac"], 1)

                    def norm(c):
                        dve.wait_ge(s["pv_done"], ONE + CG * G + c + 1)
                        dve.wait_ge(s["o_hi_done"], ONE + CG * G + c)
                        dve.tensor_tensor(o_f[:], psum[:, O, CQ * (c % 2):CQ * (c % 2) + CQ], recs[:, c % 2, :], ALU.mult)\
                            .then_inc(s["o_norm"], 1)

                    def o_lo(c):
                        dve.wait_ge(s["o_hi_done"], ONE + CG * G + c + 1)
                        sl = (slice(None), (c // 4) % 2, slice(CQ * (c % 4), CQ * (c % 4) + CQ))
                        dve.tensor_tensor(oT_lo[sl], o_f[:], oT_hi[sl].bitcast(F), ALU.subtract).then_inc(s["o_lo_done"], 1)

                    def v_rest(half):
                        dve.wait_ge(s["v_hi_done"], 2 * G + half + 1)
                        sl = (slice(None), slice(4 * half, 4 * half + 4), slice(None))
                        dve.tensor_tensor(v_lo[sl], psum[:, O, :].rearrange("p (k n) -> p k n", k=4), v_hi[sl].bitcast(F),
                                          ALU.subtract).then_inc(s["v_evac"], 1)

                    def add_out(pair, tt):
                        dve.wait_ge(s["acc_zero"], b + 1)
                        dve.wait_ge(s["oproj_psum"], ONE + 2 * NT * G + NT * pair + tt + 1)
                        bk = M if pair == 0 or tt % 2 == 0 else O
                        dve.tensor_tensor(acc[:, tt, :], psum[:, bk, :], acc[:, tt, :], ALU.add)\
                            .then_inc(s["oproj_evac"], 1)

                    for t in range(TG):
                        negmax(t)
                        if t >= 1:
                            recip(t - 1)
                        pp = pv_parts(t)
                        if pp is not None and pp[1] == 1:
                            norm(pp[0])
                        if t in V_STEPS:
                            v_rest(V_STEPS.index(t))
                        if O_STEP <= t < O_STEP + NT:
                            add_out(0, t - O_STEP)
                        if t >= 2:
                            t_lo(t - 2)
                        if pp is not None and pp[1] == 1:
                            o_lo(pp[0])
                    recip(TG - 1)
                    norm(CG - 3)
                    t_lo(TG - 2)
                    o_lo(CG - 3)
                    dve.drain()
                    norm(CG - 2)
                    t_lo(TG - 1)
                    o_lo(CG - 2)
                    if prefetch:
                        k_lo(G + 1)
                    dve.drain()
                    norm(CG - 1)
                    add_out(1, 0)
                    o_lo(CG - 1)
                    for tt in range(1, NT):
                        add_out(1, tt)

                with dve.Fori(0, KV0 - 1) as g:
                    group(G0 + g, True)
                group(G0 + KV0 - 1, False)

                dve.drain()
                dve.wait_ge(s["gx_loaded"], 16 * (b + 1))
                for h in range(2):
                    ts = slice(4 * h, 4 * h + 4)
                    four = lambda v: v[:, ts, :].rearrange("p t n -> p (t n)")
                    dve.scalar_tensor_tensor(four(acc), four(acc), 0.5, four(gx), ALU.mult, ALU.mult)
                    dve.drain()
                    if h == 0:
                        dve.wait_ge(s["xx_loaded"], 16 * (b + 1))
                    dve.tensor_tensor(acc[:, ts, :], acc[:, ts, :], q1[:, ts, :], ALU.add)
                    dve.drain()
                    for t in range(4 * h, 4 * h + 4):
                        dve.bn_stats(st1[:, t, :], acc[:, t, :])
                    dve.drain()
                    for t in range(4 * h, 4 * h + 4):
                        dve.bn_aggr(mv1[:, t, :], st1[:, t, :])
                    dve.drain()
                    dve.tensor_scalar(rs1[:, ts], mv1[:, ts, 1], LN_EPS, None, ALU.add).then_inc(s["x1_stats"], 1)
                dve.wait_ge(s["w1_hi_done"], 2 * (b + 1))
                dve.tensor_tensor(w1_lo[:, 2:4, :], w1_f[:, 2:4, :], w1_hi[:, 2:4, :].bitcast(F), ALU.subtract)\
                    .then_inc(s["w1_lo_done"], 1)

                def qkv_out(u):
                    dve.wait_ge(s["qkv_psum"], NT * b + u + 1)
                    dve.wait_ge(s["qkv_evac"], ONE + NT * b + u)
                    both = psum[:, 2 + 2 * (u % 2):4 + 2 * (u % 2), :].rearrange("p a n -> p (a n)")
                    nh = QK1 // D1
                    qk = both[:, 0:QK1].rearrange("p (h k d) -> p h k d", k=2, d=D1 // 2)
                    tab = lambda lo, n: cs1[:, u, lo:lo + n].unsqueeze(1).broadcast_to([P, nh, n])
                    rbv = rb[:].rearrange("p (h k d) -> p h k d", k=2, d=D1 // 2)
                    dve.tensor_tensor(ra[:].rearrange("p (h d) -> p h d", d=D1),
                                      both[:, 0:QK1].rearrange("p (h d) -> p h d", d=D1), tab(0, D1), ALU.mult)
                    dve.tensor_tensor(rbv[:, :, 0, :], qk[:, :, 1, :], tab(D1, D1 // 2), ALU.mult)
                    dve.tensor_tensor(rbv[:, :, 1, :], qk[:, :, 0, :], tab(D1 + D1 // 2, D1 // 2), ALU.mult)
                    dve.tensor_copy(v1[:, u, :], both[:, QK1:W1N])
                    dve.drain()
                    dve.tensor_tensor(q1[:, u, :], ra[:, 0:E], rb[:, 0:E], ALU.add)
                    dve.tensor_tensor(k1[:, u, :], ra[:, E:QK1], rb[:, E:QK1], ALU.add).then_inc(s["qkv_evac"], 1)
                    dve.wait_ge(s["ffn_psum"], NT * b + u + 1)
                    dve.tensor_tensor(g_lin[:, u % 2, :], psum[:, 6 + u % 2, :], bias_b[:], ALU.add).then_inc(s["ffn_lin"], 1)

                def silu(u):
                    dve.wait_ge(s["ffn_exp"], NT * b + u + 1)
                    dve.scalar_tensor_tensor(gx[:, u, :], g_exp[:, u % 2, :], 1.0, g_lin[:, u % 2, :],
                                             ALU.add, ALU.mult).then_inc(s["ffn_done"], 1)

                def xn1(t):
                    if t % 4 == 0:
                        dve.wait_ge(s["x1_rstd"], 2 * b + t // 4 + 1)
                    dve.tensor_scalar(gx[:, t, :], acc[:, t, :], mv1[:, t, 0:1], rs1[:, t:t + 1],
                                      ALU.subtract, ALU.mult).then_inc(s["xn_ready"], 1)

                xn1(0)
                for t in range(NT + 2):
                    if t < NT:
                        if t + 1 < NT:
                            xn1(t + 1)
                        lo_of(t, 2 * NT * b + NT)
                    if 1 <= t <= NT:
                        qkv_out(t - 1)
                    if t >= 2:
                        silu(t - 2)
                dve.drain()

                QM, KM, X, Y = 0, 2, 5, 6

                def stack_evac(dst, half, x):
                    dve.wait_ge(s["qt_psum"], ONE + x + 1)
                    dve.tensor_copy(dst[0:ST1, 512 * half:512 * half + 512], psum[0:ST1, X, :]).then_inc(s["qt_evac"], 1)

                def maximum(h, c):
                    i, k0, w = q_chunks()[c]
                    dve.wait_ge(s["qm_psum"], ONE + CH * h + c + 1)
                    dve.tensor_reduce(nm1[:, k0 // 512, i:i + 1], psum[:, QM + c % 2, 0:w], AX.X, ALU.max, negate=True)\
                        .then_inc(s["qm_max"], 1)

                def max_rows(j, h):
                    rows = q_st[:, (j // GQ) % 2, :, j % GQ, 4 * D1:ST1]
                    dve.drain()
                    dve.tensor_tensor(nm1[:, 0, 4:NT], nm1[:, 0, 4:NT], nm1[:, 1, 4:NT], ALU.min)
                    dve.drain()
                    dve.tensor_copy(rows[:, :, 0], nm1[:, 0, :])
                    dve.drain()
                    dve.tensor_tensor(rows[:, :, 1], nm1[:, 0, :], rows[:, :, 0].bitcast(F), ALU.subtract)\
                        .then_inc(s["nm_ready"], 1)

                def divide_half(N, n, half):
                    cols = slice(512 * half, 512 * half + 512)
                    dve.reciprocal(sumT[:, cols], sumT[:, cols])
                    dve.drain()
                    dve.tensor_tensor(ctxT[:, n, cols], ctxT[:, n, cols], sumT[:, cols], ALU.mult).then_inc(s["ctx_ready"], 1)

                def pair(N, n, first, prefetch):
                    for j in range(PH):
                        h = PH * N + j
                        turns = x_turns(j, prefetch)
                        for c in range(CH):
                            if "T2" in turns:
                                maximum(h + 1, c)
                            if "T1" in turns and c in (3, 7):
                                stack_evac(qTa[:, (j + 2) % 2], c // 4, XP * N + x_at(j, "T1", prefetch) + c // 4)
                        if "T2" in turns:
                            max_rows(j + 1, h + 1)
                        if "K" in turns:
                            stack_evac(kT1[:, (j // GQ + 1) % 2], 1, XP * N + x_at(j, "K", prefetch) + 1)
                        if not first and j == 0:
                            for k in range(2):
                                dve.wait_ge(s[f"o_moved{k}"], ONE + 16 * PH * N)
                        if not first and j < 2:
                            divide_half(N - 1, n - 1, j)
                        dve.wait_ge(s["pv1_psum"], ONE + 2 * h + 2)
                        dve.tensor_copy(o_st[:, j % 2, 512:S], psum[0:VS, Y + 1, :]).then_inc(s["pv1_evac"], 1)

                N0 = NPAIR * b
                stack_evac(kT1[:, 0], 1, XP * N0 + 1)
                for j in range(2):
                    for half in range(2):
                        stack_evac(qTa[:, j], half, XP * N0 + 2 + 2 * j + half)
                for c in range(CH):
                    maximum(PH * N0, c)
                max_rows(0, PH * N0)
                pair(N0, 0, True, True)
                with dve.Fori(1, NPAIR - 1) as n:
                    pair(N0 + n, n, False, True)
                pair(N0 + NPAIR - 1, NPAIR - 1, False, False)
                for k in range(2):
                    dve.wait_ge(s[f"o_moved{k}"], ONE + 16 * PH * (N0 + NPAIR))
                for half in range(2):
                    divide_half(N0 + NPAIR - 1, NPAIR - 1, half)
                for t in range(NT):
                    dve.wait_ge(s["y_psum"], NT * b + t + 1)
                    if t >= 2:
                        dve.wait_ge(s[f"y_stored{t % 2}"], ONE + 8 * NT * b + 16 * (t // 2))
                    dve.scalar_tensor_tensor(y_sb[:, t % 2, :], psum[:, t % 4, :], 0.5, gx[:, t, :],
                                             ALU.mult, ALU.mult)
                    dve.drain()
                    dve.tensor_tensor(y_sb[:, t % 2, :], y_sb[:, t % 2, :], acc[:, t, :], ALU.add).then_inc(s["y_ready"], 1)


def tables():
    t = np.arange(S, dtype=np.float32)
    inv0 = (np.float32(1.0) / np.float32(10000.0) ** (np.arange(0, D0, 2, dtype=np.float32) / np.float32(D0))).astype(np.float32)
    f0 = (t[:, None] * inv0[None, :]).astype(np.float32).astype(np.float64)
    r0 = float(D0) ** -0.25
    cosT = np.concatenate([np.cos(f0), np.cos(f0)], 1).T * r0
    sinT = np.concatenate([-np.sin(f0), np.sin(f0)], 1).T * r0
    inv1 = (np.float32(1.0) / np.float32(500000.0) ** (np.arange(0, D1, 2, dtype=np.float32) / np.float32(D1))).astype(np.float32)
    f1 = (t[:, None] * inv1[None, :]).astype(np.float32).astype(np.float64)
    r1 = float(D1) ** -0.25
    cs1 = np.concatenate([np.cos(f1), np.cos(f1), -np.sin(f1), np.sin(f1)], 1) * r1
    cs1 = cs1.reshape(NT, P, 2 * D1).transpose(1, 0, 2)
    return {k: np.ascontiguousarray(v, dtype=np.float32) for k, v in (("cosT", cosT), ("sinT", sinT), ("cs1", cs1))}


def padded(w, rows, cols):
    o = np.zeros((rows, cols), np.float32)
    o[:w.shape[0], :w.shape[1]] = w
    return o


def chunked(wT):
    return wT.reshape(EC, P, -1).transpose(1, 0, 2)


def layouts(i):
    heads = lambda w, n: w.reshape(n, D0, EC, P).transpose(0, 3, 2, 1).reshape(n, P, EC * D0)
    row = lambda v: np.asarray(v, np.float32).reshape(1, -1)
    er = lambda v: np.repeat(v, 16).reshape(2, P).T
    scal = np.zeros((1, 4), np.float32)
    scal[0, 0], scal[0, 1], scal[0, 2] = i["L0_ffn_bu2"][0], i["L0_ffn_gate_w1"], i["L0_ffn_gate_bias"]
    wa = np.zeros((E, 2 * P), np.float32)
    wa[:, 0:P] = i["L0_ffn_Wu1"].T
    wa[:, P:P + BOT] = i["L0_ffn_Wq"].T
    x = i["L0_attn_hidden_states"]
    d = {
        "x": x.reshape(B * S, E), "x3": x,
        "wq": heads(i["L0_attn_Wq"], H0), "wk": heads(i["L0_attn_Wk"], KV0), "wv": heads(i["L0_attn_Wv"], KV0),
        "wo": i["L0_attn_Wo"].T.reshape(H0, D0, E),
        "wa": chunked(wa),
        "keysT": padded(i["L0_ffn_aux_keys"].T, P, P), "wr": padded(i["L0_ffn_Wr"], P, P),
        "wrT": padded(i["L0_ffn_Wr"].T, P, P),
        "avT": chunked(i["L0_ffn_aux_values"].T), "wvdT": chunked(padded(i["L0_ffn_Wvd"].T, E, P)),
        "wvuT": padded(i["L0_ffn_Wvu"].T, P, E),
        "bu1": row(i["L0_ffn_bu1"]), "wu2": row(i["L0_ffn_Wu2"]), "scal": scal, "log_rel": row(i["L0_ffn_log_rel"]),
        "w_qkv1": chunked(np.concatenate([i["L1_attn_Wq"], i["L1_attn_Wk"], i["L1_attn_Wv"]], 1)),
        "wo1": chunked(i["L1_attn_Wo"]),
        "w_ffn1": chunked(i["L1_ffn_W"].T), "bias1": row(i["L1_ffn_bias"]),
        "lora_a": i["L1_ffn_A"].reshape(2, P, E).transpose(1, 0, 2),
        "lora_b": i["L1_ffn_Bf"].transpose(0, 2, 1).reshape(2, P, E).transpose(1, 0, 2),
        "mix": np.stack([er(i["L1_ffn_coeffs"]), er(i["L1_ffn_scales"])], 2),
    }
    return {k: np.ascontiguousarray(v) for k, v in {**d, **tables()}.items()}


def kernel(**inputs):
    import concourse.bacc as bacc
    from concourse.bass_utils import run_bass_kernel_spmd

    nc = bacc.Bacc("TRN2", target_bir_lowering=False, num_devices=1)
    arrays, aps = {}, {}
    for name, v in layouts({k: np.asarray(v) for k, v in inputs.items()}).items():
        arrays[f"in_{name}"] = v
        aps[name] = nc.dram_tensor(f"in_{name}", v.shape, mybir.dt.from_np(v.dtype), kind="ExternalInput").ap()
    out = nc.dram_tensor("out_0", [B, S, E], F, kind="ExternalOutput").ap()
    aps["out3"] = out
    build(nc, aps, out)
    r = run_bass_kernel_spmd(nc, [arrays], core_ids=[0])
    return r.results[0]["out_0"]
```
